# Optimizing a Trainium2 kernel written in Bass

```python
import numpy as np
import jax
import jax.numpy as jnp

def _softmax(x, axis=-1):
    return jax.nn.softmax(x, axis=axis)

def _gelu(x):
    return jax.nn.gelu(x, approximate=True)

def _silu(x):
    return jax.nn.silu(x)

def _sigmoid(x):
    return jax.nn.sigmoid(x)

def _layernorm(x, axis=-1, eps=1e-05):
    m = jnp.mean(x, axis=axis, keepdims=True)
    v = jnp.var(x, axis=axis, keepdims=True)
    return (x - m) / jnp.sqrt(v + eps)

def _scatter_add(tgt, idx, src, axis=0):
    return tgt.at[idx].add(src)

def _segment_sum(src, seg, n):
    return jax.ops.segment_sum(src, seg, n)
kernel_name = 'mk_adaln_d2_jaxref_r8_ba7602'

def setup_inputs(seed: int=0):
    np.random.seed(seed)
    _w = jnp.asarray

    def _L0_attn_setup():
        import jax, jax.numpy as jnp
        import numpy as np
        N_HEAD = 16
        N_LANDMARKS = 64
        N_ITER = 6

        def _landmarks(t, nL):
            B, nh, T, hs = t.shape
            return t.reshape(B, nh, nL, T // nL, hs).mean(axis=3)

        def _iterative_inv(K, n_iter=N_ITER):
            I = jnp.eye(K.shape[-1], dtype=K.dtype)
            denom = jnp.max(jnp.sum(K, axis=-2), axis=-1)[..., None, None]
            V = K.swapaxes(-1, -2) / denom
            for _ in range(n_iter):
                KV = K @ V
                V = 0.25 * V @ (13.0 * I - KV @ (15.0 * I - KV @ (7.0 * I - KV)))
            return V
        key = jax.random.key(seed)
        k1, k2, k3 = jax.random.split(key, 3)
        B, T, C = (4, 512, 128)
        x = jax.random.normal(k1, (B, T, C), dtype=jnp.float32)
        W_attn = jax.random.normal(k2, (C, 3 * C), dtype=jnp.float32) * (1.0 / np.sqrt(C))
        W_proj = jax.random.normal(k3, (C, C), dtype=jnp.float32) * (1.0 / np.sqrt(C))
        return {'x': x, 'W_attn': W_attn, 'W_proj': W_proj}
    _L0_attn_in = _L0_attn_setup()

    def _L0_ffn_setup():
        import jax, jax.numpy as jnp
        import numpy as np
        NUM_EXPERTS = 8
        CAPACITY_FACTOR = 1.0
        key = jax.random.key(seed)
        k1, k2, k3, k4 = jax.random.split(key, 4)
        B, S, D, E, F = (8, 256, 128, NUM_EXPERTS, 512)
        x = jax.random.normal(k1, (B, S, D), dtype=jnp.float32)
        router_w = jax.random.normal(k2, (D, E), dtype=jnp.float32) * D ** (-0.5)
        w1 = jax.random.normal(k3, (E, D, F), dtype=jnp.float32) * D ** (-0.5)
        w2 = jax.random.normal(k4, (E, F, D), dtype=jnp.float32) * F ** (-0.5)
        return {'x': x, 'router_w': router_w, 'w1': w1, 'w2': w2}
    _L0_ffn_in = _L0_ffn_setup()
    _L0_c = _w((lambda *s: np.random.randn(*s).astype(np.float32) * 0.05)(8, 128))
    _L0_wmod = _w((lambda *s: np.random.randn(*s).astype(np.float32) * 0.05)(128, 6 * 128) * 128 ** (-0.5))

    def _L1_attn_setup():
        import jax, jax.numpy as jnp
        import numpy as np
        B, S, D = (2, 256, 128)
        H = 16
        K = 21
        HD = D // H

        def _tisa_bias(amplitudes, sharpness, offsets, seq_len):
            rel = jnp.arange(-(seq_len - 1), seq_len, dtype=jnp.float32)
            d = rel[None, None, :] - offsets[:, :, None]
            scores = amplitudes[:, :, None] * jnp.exp(-jnp.abs(sharpness)[:, :, None] * d * d)
            scores = scores.sum(axis=1)
            idx = jnp.arange(seq_len)
            rel_idx = idx[None, :] - idx[:, None] + (seq_len - 1)
            return scores[:, rel_idx]
        key = jax.random.key(seed)
        ks = jax.random.split(key, 7)
        x = jax.random.normal(ks[0], (B, S, D), dtype=jnp.float32)
        w_in = jax.random.normal(ks[1], (D, 3 * D), dtype=jnp.float32) * (1.0 / np.sqrt(D))
        w_gate = jax.random.normal(ks[2], (D, 2 * D), dtype=jnp.float32) * (1.0 / np.sqrt(D))
        b_gate = jnp.zeros((2 * D,), dtype=jnp.float32)
        amplitudes = jax.random.normal(ks[3], (H, K), dtype=jnp.float32) * 0.1
        sharpness = jax.random.uniform(ks[4], (H, K), dtype=jnp.float32, minval=0.05, maxval=0.3)
        max_fv, min_fv = (S // 2, 5)
        offsets = jax.random.uniform(ks[5], (H, K), dtype=jnp.float32, minval=-float(max_fv), maxval=float(max_fv))
        return {'x': x, 'w_in': w_in, 'w_gate': w_gate, 'b_gate': b_gate, 'amplitudes': amplitudes, 'sharpness': sharpness, 'offsets': offsets}
    _L1_attn_in = _L1_attn_setup()

    def _L1_ffn_setup():
        import jax, jax.numpy as jnp
        import numpy as np
        EMB = 128
        HEADS = 16
        SEQ = 256
        LATENT = 64
        N_EXP = 8
        TOP_K = 2
        EXP_DIM = 256
        BATCH = 2
        EPS = 1e-06

        def _rmsnorm(x, g):
            return x * jax.lax.rsqrt(jnp.mean(x * x, axis=-1, keepdims=True) + EPS) * g

        def _mla(h, Wq, Wdkv, Wuk, Wuv, Wo):
            B, S, D = h.shape
            hd = D // HEADS
            q = (h @ Wq).reshape(B, S, HEADS, hd)
            c = h @ Wdkv
            k = (c @ Wuk).reshape(B, S, HEADS, hd)
            v = (c @ Wuv).reshape(B, S, HEADS, hd)
            scores = jnp.einsum('bqhd,bkhd->bhqk', q, k) / jnp.sqrt(jnp.asarray(hd, h.dtype))
            causal = jnp.tril(jnp.ones((S, S), bool))
            scores = jnp.where(causal, scores, jnp.asarray(-1000000000.0, h.dtype))
            a = jax.nn.softmax(scores, axis=-1)
            out = jnp.einsum('bhqk,bkhd->bqhd', a, v).reshape(B, S, D)
            return out @ Wo

        def _moe(h, gate_w, w1, w2):
            B, S, D = h.shape
            t = h.reshape(B * S, D)
            logits = t @ gate_w
            top_v, top_i = jax.lax.top_k(logits, TOP_K)
            gates = jax.nn.softmax(top_v, axis=-1)
            T = t.shape[0]
            combine = jnp.zeros((T, N_EXP), t.dtype).at[jnp.arange(T)[:, None], top_i].add(gates)
            hid = jax.nn.silu(jnp.einsum('td,edh->teh', t, w1))
            ye = jnp.einsum('teh,ehd->ted', hid, w2)
            out = jnp.einsum('te,ted->td', combine, ye)
            return out.reshape(B, S, D)
        key = jax.random.key(seed)
        ks = jax.random.split(key, 12)
        s = 0.02
        return {'x': jax.random.normal(ks[0], (BATCH, SEQ, EMB), jnp.float32), 'g1': jnp.ones((EMB,), jnp.float32), 'Wq': jax.random.normal(ks[1], (EMB, EMB), jnp.float32) * s, 'Wdkv': jax.random.normal(ks[2], (EMB, LATENT), jnp.float32) * s, 'Wuk': jax.random.normal(ks[3], (LATENT, EMB), jnp.float32) * s, 'Wuv': jax.random.normal(ks[4], (LATENT, EMB), jnp.float32) * s, 'Wo': jax.random.normal(ks[5], (EMB, EMB), jnp.float32) * s, 'g2': jnp.ones((EMB,), jnp.float32), 'gate_w': jax.random.normal(ks[6], (EMB, N_EXP), jnp.float32) * s, 'w1': jax.random.normal(ks[7], (N_EXP, EMB, EXP_DIM), jnp.float32) * s, 'w2': jax.random.normal(ks[8], (N_EXP, EXP_DIM, EMB), jnp.float32) * s}
    _L1_ffn_in = _L1_ffn_setup()
    _L1_c = _w((lambda *s: np.random.randn(*s).astype(np.float32) * 0.05)(8, 128))
    _L1_wmod = _w((lambda *s: np.random.randn(*s).astype(np.float32) * 0.05)(128, 6 * 128) * 128 ** (-0.5))
    _d = {'L0_attn_x': _L0_attn_in['x'], 'L0_attn_W_attn': _L0_attn_in['W_attn'], 'L0_attn_W_proj': _L0_attn_in['W_proj'], 'L0_ffn_router_w': _L0_ffn_in['router_w'], 'L0_ffn_w1': _L0_ffn_in['w1'], 'L0_ffn_w2': _L0_ffn_in['w2'], 'L0_c': _L0_c, 'L0_wmod': _L0_wmod, 'L1_attn_w_in': _L1_attn_in['w_in'], 'L1_attn_w_gate': _L1_attn_in['w_gate'], 'L1_attn_b_gate': _L1_attn_in['b_gate'], 'L1_attn_amplitudes': _L1_attn_in['amplitudes'], 'L1_attn_sharpness': _L1_attn_in['sharpness'], 'L1_attn_offsets': _L1_attn_in['offsets'], 'L1_ffn_g1': _L1_ffn_in['g1'], 'L1_ffn_Wq': _L1_ffn_in['Wq'], 'L1_ffn_Wdkv': _L1_ffn_in['Wdkv'], 'L1_ffn_Wuk': _L1_ffn_in['Wuk'], 'L1_ffn_Wuv': _L1_ffn_in['Wuv'], 'L1_ffn_Wo': _L1_ffn_in['Wo'], 'L1_ffn_g2': _L1_ffn_in['g2'], 'L1_ffn_gate_w': _L1_ffn_in['gate_w'], 'L1_ffn_w1': _L1_ffn_in['w1'], 'L1_ffn_w2': _L1_ffn_in['w2'], 'L1_c': _L1_c, 'L1_wmod': _L1_wmod}
    _x0 = _d['L0_attn_x']
    _d['L0_attn_x'] = jax.random.normal(jax.random.fold_in(jax.random.key(seed), 1), (8, 512, 128), dtype=_x0.dtype)
    del _x0
    return _d

def reference(L0_attn_x, L0_attn_W_attn, L0_attn_W_proj, L0_ffn_router_w, L0_ffn_w1, L0_ffn_w2, L0_c, L0_wmod, L1_attn_w_in, L1_attn_w_gate, L1_attn_b_gate, L1_attn_amplitudes, L1_attn_sharpness, L1_attn_offsets, L1_ffn_g1, L1_ffn_Wq, L1_ffn_Wdkv, L1_ffn_Wuk, L1_ffn_Wuv, L1_ffn_Wo, L1_ffn_g2, L1_ffn_gate_w, L1_ffn_w1, L1_ffn_w2, L1_c, L1_wmod):

    def _L0_attn_ref(x, W_attn, W_proj):
        import jax, jax.numpy as jnp
        import numpy as np
        N_HEAD = 16
        N_LANDMARKS = 64
        N_ITER = 6

        def _landmarks(t, nL):
            B, nh, T, hs = t.shape
            return t.reshape(B, nh, nL, T // nL, hs).mean(axis=3)

        def _iterative_inv(K, n_iter=N_ITER):
            I = jnp.eye(K.shape[-1], dtype=K.dtype)
            denom = jnp.max(jnp.sum(K, axis=-2), axis=-1)[..., None, None]
            V = K.swapaxes(-1, -2) / denom
            for _ in range(n_iter):
                KV = K @ V
                V = 0.25 * V @ (13.0 * I - KV @ (15.0 * I - KV @ (7.0 * I - KV)))
            return V
        B, T, C = x.shape
        nh, nL = (N_HEAD, N_LANDMARKS)
        hs = C // nh
        qkv = x @ W_attn
        q, k, v = jnp.split(qkv, 3, axis=-1)

        def heads(t):
            return t.reshape(B, T, nh, hs).transpose(0, 2, 1, 3)
        q, k, v = (heads(q), heads(k), heads(v))
        q_l = _landmarks(q, nL)
        k_l = _landmarks(k, nL)
        L = jax.nn.softmax(jnp.einsum('bhtd,bhld->bhtl', q, k_l), axis=-1)
        P = _iterative_inv(jax.nn.softmax(jnp.einsum('bhld,bhmd->bhlm', q_l, k_l), axis=-1))
        N = jax.nn.softmax(jnp.einsum('bhld,bhtd->bhlt', q_l, k), axis=-1)
        y = L @ (P @ (N @ v))
        y = y.transpose(0, 2, 1, 3).reshape(B, T, C)
        return y @ W_proj

    def _L0_ffn_ref(x, router_w, w1, w2):
        import jax, jax.numpy as jnp
        import numpy as np
        NUM_EXPERTS = 8
        CAPACITY_FACTOR = 1.0
        B, S, D = x.shape
        E = router_w.shape[1]
        T = B * S
        C = int(CAPACITY_FACTOR * T / E)
        x_flat = x.reshape(T, D)
        logits = x_flat @ router_w
        probs = jax.nn.softmax(logits, axis=-1)
        expert_idx = jnp.argmax(probs, axis=-1)
        gate = jnp.take_along_axis(probs, expert_idx[:, None], axis=1)[:, 0]
        onehot = jax.nn.one_hot(expert_idx, E, dtype=jnp.float32)
        pos_all = jnp.cumsum(onehot, axis=0) - 1.0
        pos = jnp.take_along_axis(pos_all, expert_idx[:, None], axis=1)[:, 0]
        pos = pos.astype(jnp.int32)
        keep = (pos < C).astype(x_flat.dtype)
        pos_c = jnp.clip(pos, 0, C - 1)
        expert_in = jnp.zeros((E, C, D), dtype=x_flat.dtype)
        expert_in = expert_in.at[expert_idx, pos_c].add(x_flat * keep[:, None])
        hidden = jax.nn.gelu(jnp.einsum('ecd,edf->ecf', expert_in, w1))
        expert_out = jnp.einsum('ecf,efd->ecd', hidden, w2)
        y = expert_out[expert_idx, pos_c] * (gate * keep)[:, None]
        return y.reshape(B, S, D)

    def _L1_attn_ref(x, w_in, w_gate, b_gate, amplitudes, sharpness, offsets):
        import jax, jax.numpy as jnp
        import numpy as np
        B, S, D = (2, 256, 128)
        H = 16
        K = 21
        HD = D // H

        def _tisa_bias(amplitudes, sharpness, offsets, seq_len):
            rel = jnp.arange(-(seq_len - 1), seq_len, dtype=jnp.float32)
            d = rel[None, None, :] - offsets[:, :, None]
            scores = amplitudes[:, :, None] * jnp.exp(-jnp.abs(sharpness)[:, :, None] * d * d)
            scores = scores.sum(axis=1)
            idx = jnp.arange(seq_len)
            rel_idx = idx[None, :] - idx[:, None] + (seq_len - 1)
            return scores[:, rel_idx]
        b, s, d = x.shape
        proj = x @ w_in
        k, v, q = jnp.split(proj, 3, axis=-1)

        def heads(t):
            return t.reshape(b, s, H, HD).transpose(0, 2, 1, 3)
        q, k, v = (heads(q), heads(k), heads(v))
        scale = 1.0 / jnp.sqrt(jnp.float32(HD))
        scores = jnp.einsum('bhqd,bhkd->bhqk', q, k) * scale
        scores = scores + _tisa_bias(amplitudes, sharpness, offsets, s)[None]
        weights = jax.nn.softmax(scores, axis=-1)
        attn = jnp.einsum('bhqk,bhkd->bhqd', weights, v)
        out = attn.transpose(0, 2, 1, 3).reshape(b, s, d)
        gated = out @ w_gate + b_gate
        a, g = jnp.split(gated, 2, axis=-1)
        return a * jax.nn.sigmoid(g)

    def _L1_ffn_ref(x, g1, Wq, Wdkv, Wuk, Wuv, Wo, g2, gate_w, w1, w2):
        import jax, jax.numpy as jnp
        import numpy as np
        EMB = 128
        HEADS = 16
        SEQ = 256
        LATENT = 64
        N_EXP = 8
        TOP_K = 2
        EXP_DIM = 256
        BATCH = 2
        EPS = 1e-06

        def _rmsnorm(x, g):
            return x * jax.lax.rsqrt(jnp.mean(x * x, axis=-1, keepdims=True) + EPS) * g

        def _mla(h, Wq, Wdkv, Wuk, Wuv, Wo):
            B, S, D = h.shape
            hd = D // HEADS
            q = (h @ Wq).reshape(B, S, HEADS, hd)
            c = h @ Wdkv
            k = (c @ Wuk).reshape(B, S, HEADS, hd)
            v = (c @ Wuv).reshape(B, S, HEADS, hd)
            scores = jnp.einsum('bqhd,bkhd->bhqk', q, k) / jnp.sqrt(jnp.asarray(hd, h.dtype))
            causal = jnp.tril(jnp.ones((S, S), bool))
            scores = jnp.where(causal, scores, jnp.asarray(-1000000000.0, h.dtype))
            a = jax.nn.softmax(scores, axis=-1)
            out = jnp.einsum('bhqk,bkhd->bqhd', a, v).reshape(B, S, D)
            return out @ Wo

        def _moe(h, gate_w, w1, w2):
            B, S, D = h.shape
            t = h.reshape(B * S, D)
            logits = t @ gate_w
            top_v, top_i = jax.lax.top_k(logits, TOP_K)
            gates = jax.nn.softmax(top_v, axis=-1)
            T = t.shape[0]
            combine = jnp.zeros((T, N_EXP), t.dtype).at[jnp.arange(T)[:, None], top_i].add(gates)
            hid = jax.nn.silu(jnp.einsum('td,edh->teh', t, w1))
            ye = jnp.einsum('teh,ehd->ted', hid, w2)
            out = jnp.einsum('te,ted->td', combine, ye)
            return out.reshape(B, S, D)
        x = x + _mla(_rmsnorm(x, g1), Wq, Wdkv, Wuk, Wuv, Wo)
        x = x + _moe(_rmsnorm(x, g2), gate_w, w1, w2)
        return x
    x = L0_attn_x
    mod = (_silu(L0_c) @ L0_wmod).reshape(L0_c.shape[0], 6, 1, -1)
    sa, ca, ga, sb, cb, gb = (mod[:, 0], mod[:, 1], mod[:, 2], mod[:, 3], mod[:, 4], mod[:, 5])
    ga = (2 * (ga >= 0) - 1) * jnp.maximum(jnp.abs(ga), 0.25)
    gb = (2 * (gb >= 0) - 1) * jnp.maximum(jnp.abs(gb), 0.25)
    h = _layernorm(x, axis=-1) * (1 + ca) + sa
    x = x + ga * _L0_attn_ref(h, L0_attn_W_attn, L0_attn_W_proj)
    h = _layernorm(x, axis=-1) * (1 + cb) + sb
    x = x + gb * _L0_ffn_ref(h, L0_ffn_router_w, L0_ffn_w1, L0_ffn_w2)
    mod = (_silu(L1_c) @ L1_wmod).reshape(L1_c.shape[0], 6, 1, -1)
    sa, ca, ga, sb, cb, gb = (mod[:, 0], mod[:, 1], mod[:, 2], mod[:, 3], mod[:, 4], mod[:, 5])
    ga = (2 * (ga >= 0) - 1) * jnp.maximum(jnp.abs(ga), 0.25)
    gb = (2 * (gb >= 0) - 1) * jnp.maximum(jnp.abs(gb), 0.25)
    h = _layernorm(x, axis=-1) * (1 + ca) + sa
    x = x + ga * _L1_attn_ref(h, L1_attn_w_in, L1_attn_w_gate, L1_attn_b_gate, L1_attn_amplitudes, L1_attn_sharpness, L1_attn_offsets)
    h = _layernorm(x, axis=-1) * (1 + cb) + sb
    x = x + gb * _L1_ffn_ref(h, L1_ffn_g1, L1_ffn_Wq, L1_ffn_Wdkv, L1_ffn_Wuk, L1_ffn_Wuv, L1_ffn_Wo, L1_ffn_g2, L1_ffn_gate_w, L1_ffn_w1, L1_ffn_w2)
    return x

_drawn_inputs = setup_inputs


def setup_inputs(seed=0):
    import zlib

    import numpy as np

    out = dict(_drawn_inputs(seed))
    spreads = {'L1_attn_b_gate': (0.0, 0.675), 'L1_ffn_g1': (1.0, 0.6), 'L1_ffn_g2': (1.0, 0.6)}
    factors = {'L1_attn_w_in': 3.936,
     'L1_attn_w_gate': 3.929,
     'L1_attn_amplitudes': 8.0,
     'L1_attn_sharpness': 8.0,
     'L1_attn_offsets': 8.0,
     'L1_ffn_Wq': 8.0,
     'L1_ffn_Wdkv': 8.0,
     'L1_ffn_Wuk': 8.0,
     'L1_ffn_Wuv': 8.0,
     'L1_ffn_Wo': 8.0,
     'L1_ffn_gate_w': 8.0,
     'L1_ffn_w1': 8.0,
     'L1_ffn_w2': 8.0}
    for name, (base, spread) in spreads.items():
        noise = np.random.default_rng([zlib.crc32(name.encode()), seed]).standard_normal(out[name].shape)
        drawn = base * np.exp(spread * noise) if base else spread * noise
        out[name] = jnp.asarray(drawn.astype(out[name].dtype))
    for name, factor in factors.items():
        out[name] = (out[name] * factor).astype(out[name].dtype)
    return out
```

```python
import concourse.bass as bass
from concourse import mybir
from contextlib import ExitStack

FP32 = mybir.dt.float32
BF16 = mybir.dt.bfloat16
INT32 = mybir.dt.int32
ALU = mybir.AluOpType
ACT = mybir.ActivationFunctionType
AX = mybir.AxisListType

P = 128
B = 8
T = 512
TT = T // P
C = 128
H = 16
HD = C // H
G = H // 4
NL = 64
SEG = T // NL
PAIRS = H // 2
N_ITER = 6
E = 8
CAP = B * T // E
F0 = 512
F1 = 256
LAT = 64
KG = 21
STRIP = T + (TT - 1) * P
QL = T + NL
STACK = 96
BIG = 1.0e9
LN_EPS = 1e-05
RMS_EPS = 1e-06


class Chain:

    def __init__(self, eng, sem, base=0, links=0, turn=None):
        self.eng, self.sem, self.base, self.links, self.turn, self.n = eng, sem, base, links, turn, 0

    def link(self, ins, passed=None):
        self.n += 1
        ins.then_inc(self.sem, 1)
        if self.turn is None:
            self.eng.wait_ge(self.sem, self.base + self.n)
        elif passed is None:
            self.eng.wait_ge(self.sem, self.turn * self.links + (self.base + self.n))
        else:
            wait_apart(self.eng, self.sem, self.turn * self.links + (self.base + self.n), passed)

    def done(self):
        assert self.n == self.links, ("links", self.n, self.links)


def bc(ap, shape):
    return ap.to_broadcast(shape)


def wait_apart(eng, sem, value, passed):
    eng.wait_ge(sem, value)
    eng.sem_inc(passed, 1)


def adaln_kernel(nc, L0_attn_x, L0_attn_W_attn, L0_attn_W_proj, L0_ffn_router_w, L0_ffn_w1, L0_ffn_w2,
                 L0_c, L0_wmod, L1_attn_w_in, L1_attn_w_gate, L1_attn_b_gate, L1_attn_amplitudes,
                 L1_attn_sharpness, L1_attn_offsets, L1_ffn_g1, L1_ffn_Wq, L1_ffn_Wdkv, L1_ffn_Wuk,
                 L1_ffn_Wuv, L1_ffn_Wo, L1_ffn_g2, L1_ffn_gate_w, L1_ffn_w1, L1_ffn_w2, L1_c, L1_wmod,
                 out):
    bias_dram = nc.dram_tensor("bias_dram", (H, 2 * T), FP32, kind="Internal").ap()
    slots_in = nc.dram_tensor("slots_in", (E * CAP, C), FP32, kind="Internal").ap()
    slots_out = nc.dram_tensor("slots_out", (E * CAP, C), FP32, kind="Internal").ap()

    parts_dram = nc.dram_tensor("parts_dram", (2, 3, C, QL), BF16, kind="Internal").ap()

    ctx = ExitStack()
    with ctx:
        def sb(name, shape, dt=FP32, where=ctx):
            return where.enter_context(nc.sbuf_tensor(name, shape, dt))

        def sem(name):
            return ctx.enter_context(nc.semaphore(name))

        ps = ctx.enter_context(nc.psum_tensor("ps", [P, 8, 512], FP32))

        x_sb = sb("x_sb", [P, B * TT, C])
        ident = sb("ident", [P, P])
        half = sb("half", [P, 1])
        mod_col = sb("mod_col", [P, 2, 2, B])
        gb0 = sb("gb0", [P, B, C])
        mod_row1 = sb("mod_row1", [P, 4, B, C])
        gate_keep = sb("gate_keep", [P, B * TT])
        slot_all = sb("slot_all", [P, B * TT], INT32)

        with ExitStack() as early:
            mod_row0 = sb("mod_row0", [P, 3, B, C], FP32, early)
            setup_phase(nc, sb, sem, ps, x_sb, ident, half, mod_col, mod_row0, gb0, mod_row1, bias_dram,
                        L0_attn_x, L0_c, L0_wmod, L1_c, L1_wmod, L1_attn_amplitudes, L1_attn_sharpness,
                        L1_attn_offsets, slots_in, slots_out)
            nystrom_phase(nc, sb, sem, ps, x_sb, ident, half, mod_col, mod_row0, gate_keep, slot_all,
                          slots_in, parts_dram, L0_attn_W_attn, L0_attn_W_proj, L0_ffn_router_w)
        strips = sb("strips", [P, H, STRIP])
        expert_phase(nc, sb, sem, ps, ident, strips, bias_dram, slots_in, slots_out, L0_ffn_w1, L0_ffn_w2)
        layer1_phase(nc, sb, sem, ps, x_sb, ident, half, mod_col, gb0, mod_row1, strips, parts_dram, gate_keep, slot_all,
                     slots_out, L1_attn_w_in, L1_attn_w_gate, L1_attn_b_gate, L1_ffn_g1, L1_ffn_Wq,
                     L1_ffn_Wdkv, L1_ffn_Wuk, L1_ffn_Wuv, L1_ffn_Wo, L1_ffn_g2, L1_ffn_gate_w,
                     L1_ffn_w1, L1_ffn_w2, out)


def setup_phase(nc, sb_, sem, ps, x_sb, ident, half, mod_col, mod_row0, gb0, mod_row1, bias_dram, x, c0, wmod0,
                c1, wmod1, amplitudes, sharpness, offsets, slots_in, slots_out):
    local = ExitStack()
    with local:
        def sb(name, shape, dt=FP32):
            return sb_(name, shape, dt, local)

        cT = sb("cT", [P, 2, B])
        silu_c = sb("silu_c", [P, 2, B])
        silu_rep = sb("silu_rep", [P, 2, B, P])
        wmod = sb("wmod", [P, 2, 6 * C])
        amp = sb("amp", [P, H * KG])
        shp = sb("shp", [P, H * KG])
        off = sb("off", [P, H * KG])
        rel_i = sb("rel_i", [P, 8], INT32)
        rel = sb("rel", [P, 8])
        dist = sb("dist", [P, 8, H * KG])
        gauss = sb("gauss", [P, 8, H * KG])
        bias_rel = sb("bias_rel", [P, 8, H])
        bias_hr = sb("bias_hr", [H, 2 * T])
        guard = sb("guard", [P, 2, B * C])
        zeros = sb("zeros", [P, 2048])

        mods_loaded = sem("mods_loaded")
        gauss_loaded = sem("gauss_loaded")
        x_loaded = sem("x_loaded")
        bias_stored = sem("bias_stored")
        slots_zeroed = sem("slots_zeroed")
        ident_zeroed = sem("ident_zeroed")
        ident_ready = sem("ident_ready")
        zeros_ready = sem("zeros_ready")
        rel_ready = sem("rel_ready")
        silu_ready = sem("silu_ready")
        silu_rep_ready = sem("silu_rep_ready")
        cols_ready = sem("cols_ready")
        row_ready = sem("row_ready")
        row_evac = sem("row_evac")
        exponent_ready = sem("exponent_ready")
        gauss_ready = sem("gauss_ready")
        bias_ready = sem("bias_ready")
        bias_T_ready = sem("bias_T_ready")
        bias_hr_ready = sem("bias_hr_ready")
        setup_dve = sem("setup_dve")

        with nc.Block() as block:
            @block.sync
            def _(sp):
                for l, (c, w) in enumerate(((c0, wmod0), (c1, wmod1))):
                    sp.dma_start(cT[:, l, :], c).then_inc(mods_loaded, 16)
                    sp.dma_start(wmod[:, l, :], w).then_inc(mods_loaded, 16)
                for dst, src in ((amp, amplitudes), (shp, sharpness), (off, offsets)):
                    row = src.rearrange("(a h) k -> a (h k)", a=1)
                    sp.dma_start(dst[:], row.to_broadcast([P, H * KG])).then_inc(gauss_loaded, 16)
                sp.dma_start(x_sb[:], x.rearrange("b (t p) c -> p (b t) c", p=P)).then_inc(x_loaded, 16)
                sp.wait_ge(zeros_ready, 1)
                for half_, dst in enumerate((slots_in, slots_out)):
                    for r in range(2):
                        sp.dma_start(dst[r * 2048:(r + 1) * 2048, :].rearrange("(p a) c -> p (a c)", p=P),
                                     zeros[:]).then_inc(slots_zeroed, 16)
                sp.wait_ge(bias_hr_ready, 1)
                sp.dma_start(bias_dram, bias_hr[:]).then_inc(bias_stored, 16)
                sp.wait_ge(bias_stored, 16)
                sp.wait_ge(x_loaded, 16)
                sp.wait_ge(slots_zeroed, 64)

            @block.gpsimd
            def _(pool):
                nc.gpsimd.memset(half[:], -0.5)
                nc.gpsimd.memset(zeros[:], 0.0).then_inc(zeros_ready, 1)
                nc.gpsimd.memset(ident[:], 0.0).then_inc(ident_zeroed, 1)
                nc.gpsimd.iota(rel_i[:], [[-P, 8]], base=T - 1, channel_multiplier=-1).then_inc(rel_ready, 1)
                pool.wait_ge(ident_zeroed, 1)
                nc.gpsimd.affine_select(out=ident[:], in_=ident[:], compare_op=ALU.not_equal, fill=1.0, base=0,
                                        pattern=[[-1, P]], channel_multiplier=1).then_inc(ident_ready, 1)

            @block.scalar
            def _(act):
                act.wait_ge(mods_loaded, 64)
                nc.scalar.activation(silu_c[:], cT[:], ACT.Silu).then_inc(silu_ready, 1)
                act.wait_ge(exponent_ready, 1)
                nc.scalar.activation(gauss[:], dist[:], ACT.Exp).then_inc(gauss_ready, 1)
                for i in range(2 * B):
                    act.wait_ge(row_ready, i + 1)
                    row = ps[:, 1 + i % 2, :].rearrange("p (k c) -> p k c", k=4)
                    if i < B:
                        nc.scalar.copy(mod_row0[:, :, i, :], row[:, 0:3, :])
                        nc.scalar.copy(gb0[:, i, :], row[:, 3, :]).then_inc(row_evac, 1)
                    else:
                        nc.scalar.copy(mod_row1[:, :, i - B, :], row).then_inc(row_evac, 1)
                act.wait_ge(bias_T_ready, 1)
                nc.scalar.copy(bias_hr[:], ps[0:H, 3:5, :].rearrange("h a r -> h (a r)")).then_inc(bias_hr_ready, 1)

            @block.tensor
            def _(pe):
                pe.wait_ge(silu_ready, 1)
                for l in range(2):
                    for k in range(2):
                        last = nc.tensor.matmul(ps[:, 0, (2 * l + k) * B:(2 * l + k + 1) * B],
                                                wmod[:, l, k * C:(k + 1) * C], silu_c[:, l, :], start=True, stop=True)
                last.then_inc(cols_ready, 1)
                pe.wait_ge(silu_rep_ready, 1)
                for i in range(2 * B):
                    if i >= 2:
                        pe.wait_ge(row_evac, i - 1)
                    nc.tensor.matmul(ps[:, 1 + i % 2, :], silu_rep[:, i // B, i % B, :],
                                     wmod[:, i // B, 2 * C:6 * C], start=True, stop=True).then_inc(row_ready, 1)
                pe.wait_ge(bias_ready, 1)
                pe.wait_ge(ident_ready, 1)
                for n in range(8):
                    last = nc.tensor.transpose(ps[0:H, 3 + n // 4, (n % 4) * P:(n % 4 + 1) * P],
                                               bias_rel[:, n, :], ident[:])
                last.then_inc(bias_T_ready, 1)

            @block.vector
            def _(dve):
                link = Chain(dve, setup_dve).link
                dve.wait_ge(silu_ready, 1)
                nc.vector.tensor_copy(silu_rep[:], bc(silu_c[:].unsqueeze(3), [P, 2, B, P])).then_inc(silu_rep_ready, 1)
                dve.wait_ge(cols_ready, 1)
                cols = ps[:, 0, 0:4 * B].rearrange("p (l k b) -> p l k b", l=2, k=2)
                nc.vector.tensor_copy(mod_col[:, :, 0, :], cols[:, :, 0, :])
                nc.vector.tensor_scalar_add(mod_col[:, :, 1, :], cols[:, :, 1, :], 1.0)
                dve.wait_ge(gauss_loaded, 48)
                dve.wait_ge(rel_ready, 1)
                link(nc.vector.tensor_copy(rel[:], rel_i[:]))
                link(nc.vector.scalar_tensor_tensor(out=shp[:], in0=shp[:], scalar=-1.0, in1=shp[:], op0=ALU.mult, op1=ALU.min))
                wide = [P, 8, H * KG]
                link(nc.vector.tensor_tensor(dist[:], bc(rel[:].unsqueeze(2), wide), bc(off[:].unsqueeze(1), wide), ALU.subtract))
                link(nc.vector.tensor_tensor(gauss[:], dist[:], bc(shp[:].unsqueeze(1), wide), ALU.mult))
                link(nc.vector.tensor_tensor(dist[:], gauss[:], dist[:], ALU.mult))
                nc.vector.tensor_copy(rel[:], rel_i[:]).then_inc(exponent_ready, 1)
                dve.wait_ge(gauss_ready, 1)
                link(nc.vector.tensor_tensor(dist[:], gauss[:], bc(amp[:].unsqueeze(1), wide), ALU.mult))
                nc.vector.tensor_reduce(bias_rel[:], dist[:].rearrange("p n (h k) -> p n h k", k=KG), AX.X,
                                        ALU.add).then_inc(bias_ready, 1)
                dve.wait_ge(row_evac, 2 * B)
                for cb, gates in ((mod_row0[:, 2], (mod_row0[:, 0], gb0[:])), (mod_row1[:, 2], (mod_row1[:, 0], mod_row1[:, 3]))):
                    nc.vector.tensor_scalar_add(cb, cb, 1.0)
                    for g in gates:
                        g = g.rearrange("p b c -> p (b c)")
                        link(nc.vector.tensor_scalar(guard[:, 0], g, 0.0, 2.0, ALU.is_ge, ALU.mult))
                        link(nc.vector.scalar_tensor_tensor(out=guard[:, 1], in0=g, scalar=-1.0, in1=g, op0=ALU.mult, op1=ALU.max))
                        link(nc.vector.tensor_scalar_max(guard[:, 1], guard[:, 1], 0.25))
                        link(nc.vector.tensor_scalar_sub(guard[:, 0], guard[:, 0], 1.0))
                        link(nc.vector.tensor_tensor(g, guard[:, 0], guard[:, 1], ALU.mult))


NY_LINKS = 52


def nystrom_phase(nc, sb_, sem, ps, x_sb, ident, half, mod_col, mod_row0, gate_keep, slot_all, slots_in,
                  parts_dram, W_attn, W_proj, router_w):
    local = ExitStack()
    with local:
        def sb(name, shape, dt=FP32):
            return sb_(name, shape, dt, local)

        w_attn = sb("w_attn", [P, 3 * C])
        w_proj = sb("w_proj", [P, C])
        w_router = sb("w_router", [P, E])
        w_gated = sb("w_gated", [P, C])
        ones = sb("ones", [P, P])
        upto = sb("upto", [P, P])
        blocks = sb("blocks", [P, P])
        eye = sb("eye", [P, NL])
        eye7 = sb("eye7", [P, NL])
        eye15 = sb("eye15", [P, NL])
        eye325 = sb("eye325", [P, NL])
        rank_i = sb("rank_i", [P, E], INT32)
        rank = sb("rank", [P, E])
        stats = sb("stats", [P, TT, 6])
        mean_var = sb("mean_var", [P, TT, 2])
        var_eps = sb("var_eps", [P, TT])
        rstd = sb("rstd", [P, TT])
        xn = sb("xn", [P, TT, C])
        hT = sb("hT", [P, T])
        lm = sb("lm", [P, 2, NL])
        qk = sb("qk", [P, 2, QL])
        rest = sb("rest", [P, 2, QL])
        parts = sb("parts", [P, 2, 3, QL], BF16)
        stack = sb("stack", [STACK, 2, H, QL], BF16)
        v_tok = sb("v_tok", [P, TT, C])
        kmax = sb("kmax", [P, PAIRS])
        ksum = sb("ksum", [P, PAIRS])
        krec = sb("krec", [P, PAIRS])
        den = sb("den", [P, PAIRS])
        rden = sb("rden", [P, PAIRS])
        K_sb = sb("K_sb", [P, PAIRS, NL])
        KT = sb("KT", [P, PAIRS, NL])
        AV = sb("AV", [P, 2, PAIRS, 2, NL])
        X = sb("X", [P, PAIRS, NL])
        Q = sb("Q", [P, PAIRS, NL])
        L_tok = sb("L_tok", [P, 2, H * NL])
        lmax = sb("lmax", [P, H])
        LT = sb("LT", [P, PAIRS, T])
        N_lm = sb("N_lm", [P, 2, T])
        NT = sb("NT", [P, 2, TT, P])
        nmax = sb("nmax", [P, PAIRS])
        nsum = sb("nsum", [P, PAIRS])
        nrec = sb("nrec", [P, PAIRS])
        Nv = sb("Nv", [P, PAIRS, HD])
        Z = sb("Z", [P, PAIRS, NL])
        O_sb = sb("O_sb", [P, 2, T])
        orec = sb("orec", [P, TT, 4])
        o_tok = sb("o_tok", [P, TT, C])
        oT = sb("oT", [P, T])
        h2 = sb("h2", [P, TT, C])
        logit = sb("logit", [P, TT, E])
        lgmax = sb("lgmax", [P, TT])
        prob = sb("prob", [P, TT, E])
        psum_ = sb("psum_", [P, TT])
        gate = sb("gate", [P, TT])
        first = sb("first", [P, TT, E])
        top = sb("top", [P, TT])
        onehot = sb("onehot", [P, TT, E])
        before = sb("before", [P, TT + 1, E])
        count = sb("count", [P, TT, E])
        pos1 = sb("pos1", [P, TT])
        keep = sb("keep", [P, TT])
        slot = sb("slot", [P, TT])
        beyond = sb("beyond", [P, TT])
        slot_now = sb("slot_now", [P, TT], INT32)

        ny_loaded = sem("ny_loaded")
        consts_pool = sem("consts_pool")
        pool_order = sem("pool_order")
        eyes_ready = sem("eyes_ready")
        var_ready = sem("var_ready")
        rstd_ready = sem("rstd_ready")
        xn_ready = sem("xn_ready")
        xT_ready = sem("xT_ready")
        hT_ready = sem("hT_ready")
        qkv_ready = sem("qkv_ready")
        qk_evac = sem("qk_evac")
        parts_ready = sem("parts_ready")
        parts_stored = [sem("q_parts_stored"), sem("k_parts_stored")]
        stacked = sem("stacked")
        kscore_ready = sem("kscore_ready")
        kshift_ready = sem("kshift_ready")
        kexp_ready = sem("kexp_ready")
        k_ready = sem("k_ready")
        colsum_ready = sem("colsum_ready")
        kT_ready = sem("kT_ready")
        kT_evac = sem("kT_evac")
        a0_ready = sem("a0_ready")
        a0_evac = sem("a0_evac")
        x_ready = sem("x_ready")
        b_ready = sem("b_ready")
        q_ready = sem("q_ready")
        step_ready = sem("step_ready")
        step_evac = sem("step_evac")
        side_scores = sem("side_scores")
        side_max = sem("side_max")
        side_exp = sem("side_exp")
        side_T = sem("side_T")
        side_evac = sem("side_evac")
        nv_sums = sem("nv_sums")
        nv_ready = sem("nv_ready")
        z_ready = sem("z_ready")
        z_evac = sem("z_evac")
        o_ready = sem("o_ready")
        o_evac = sem("o_evac")
        otok_T = sem("otok_T")
        otok_ready = sem("otok_ready")
        oT_ready = sem("oT_ready")
        oT_evac = sem("oT_evac")
        w_gated_ready = sem("w_gated_ready")
        y_ready = sem("y_ready")
        h2_ready = sem("h2_ready")
        h2T_ready = sem("h2T_ready")
        h2T_evac = sem("h2T_evac")
        logits_ready = sem("logits_ready")
        lshift_ready = sem("lshift_ready")
        prob_ready = sem("prob_ready")
        onehot_ready = sem("onehot_ready")
        count_ready = sem("count_ready")
        slot_ready = sem("slot_ready")
        scattered = sem("scattered")
        h2_free = sem("h2_free")
        ny_dve = sem("ny_dve")
        consts_dve = sem("consts_dve")

        SIDES = TT + PAIRS

        def rows(h):
            return slice(NL * (h % 2), NL * (h % 2) + NL)

        passed = sem("passed")

        with nc.Block() as block:
            @block.sync
            def _(sp):
                for dst, src in ((w_attn, W_attn), (w_proj, W_proj), (w_router, router_w)):
                    sp.dma_start(dst[:], src).then_inc(ny_loaded, 16)
                with sp.Fori(0, B) as b:
                    for s in range(2):
                        sp.wait_ge(parts_ready, b * 2 + (s + 1))
                        sp.dma_start(parts_dram[s].rearrange("n p t -> p n t"), parts[:, s]).then_inc(parts_stored[s], 16)
                    for s in range(2):
                        sp.wait_ge(parts_stored[s], b * 16 + 16)
                        flat = parts_dram[s].rearrange("n (d h) t -> (n d) (h t)", d=HD)
                        for i in range(3):
                            rows_i = stack[3 * HD * i:3 * HD * (i + 1), s].rearrange("r h t -> r (h t)")
                            if s == 0:
                                sp.dma_start(rows_i, flat).then_inc(stacked, 16)
                            else:
                                for j in range(3):
                                    sp.dma_start(stack[HD * (3 * i + j):HD * (3 * i + j + 1), s].rearrange("r h t -> r (h t)"),
                                                 flat[HD * i:HD * (i + 1), :]).then_inc(stacked, 16)

            @block.gpsimd
            def _(pool):
                link = Chain(pool, consts_pool).link
                link(nc.gpsimd.memset(stack[64:STACK, :, :, :], 0.0))
                link(nc.gpsimd.memset(before[:], 0.0))
                link(nc.gpsimd.memset(ones[:], 1.0))
                link(nc.gpsimd.memset(blocks[:], 0.0))
                link(nc.gpsimd.memset(Z[:], 0.0))
                link(nc.gpsimd.iota(rank_i[:], [[-1, E]], base=E, channel_multiplier=0))
                link(nc.gpsimd.affine_select(out=upto[:], in_=ones[:], compare_op=ALU.is_ge, fill=0.0, base=0,
                                             pattern=[[1, P]], channel_multiplier=-1))
                for r in range(2):
                    link(nc.gpsimd.memset(blocks[r * NL:(r + 1) * NL, r * NL:(r + 1) * NL], 1.0))
                    link(nc.gpsimd.memset(Z[r * NL:(r + 1) * NL, :, 32 * r + HD:32 * r + 32], 1.0))
                pool.sem_inc(h2_free, 1)
                with pool.Fori(0, B) as b:
                    for n in range(2):
                        pool.wait_ge(var_ready, b * 2 + (n + 1))
                        nc.gpsimd.tensor_tensor(rstd[:], var_eps[:], bc(half[:], [P, TT]), ALU.pow).then_inc(rstd_ready, 1)
                    wait_apart(pool, slot_ready, b + 1, passed)
                    for t in range(TT):
                        nc.gpsimd.indirect_dma_start(slots_in, bass.IndirectOffsetOnAxis(ap=slot_now[:, t:t + 1], axis=0),
                                                     h2[:, t, :], None, bounds_check=E * CAP - 1,
                                                     oob_is_err=False).then_inc(scattered, 16)
                    pool.wait_ge(scattered, b * (16 * TT) + 16 * TT)
                    pool.sem_inc(h2_free, 1)

            @block.scalar
            def _(act):
                with act.Fori(0, B) as b:
                    act.wait_ge(xT_ready, b + 1)
                    nc.scalar.activation(hT[:], ps[:, 0, :], ACT.Identity, bias=mod_col[:, 0, 0, bass.ds(b, 1)],
                                         scale=mod_col[:, 0, 1, bass.ds(b, 1)]).then_inc(hT_ready, 1)
                    for s in range(2):
                        act.wait_ge(qkv_ready, b * 3 + (s + 1))
                        nc.scalar.copy(qk[:, s, 0:T], ps[:, 1 + s, :]).then_inc(qk_evac, 1)
                    act.wait_ge(qkv_ready, b * 3 + 3)
                    nc.scalar.copy(v_tok[:], ps[:, 3, :].rearrange("p (t c) -> p t c", t=TT)).then_inc(qk_evac, 1)
                    act.wait_ge(kshift_ready, b + 1)
                    nc.scalar.activation(K_sb[:], K_sb[:], ACT.Exp).then_inc(kexp_ready, 1)
                    act.wait_ge(kT_ready, b + 1)
                    nc.scalar.copy(KT[:], ps[:, 6, :].rearrange("p (j m) -> p j m", j=PAIRS)).then_inc(kT_evac, 1)

                    def side_exps(k):
                        act.wait_ge(side_max, b * SIDES + (k + 1))
                        if k < TT:
                            nc.scalar.activation(L_tok[:, k % 2, :], L_tok[:, k % 2, :], ACT.Exp).then_inc(side_exp, 1)
                        else:
                            j = k - TT
                            if k >= TT + 2:
                                act.wait_ge(side_T, b * SIDES + (k - 1))
                            nc.scalar.activation(N_lm[:, k % 2, :], ps[:, 2 + k % 2, :], ACT.Exp,
                                                 bias=nmax[:, j:j + 1], accum_out=nsum[:, j:j + 1]).then_inc(side_exp, 1)

                    def side_evacs(k):
                        act.wait_ge(side_T, b * SIDES + (k + 1))
                        if k < TT:
                            nc.scalar.copy(LT[:, :, k * P:(k + 1) * P],
                                           ps[:, 4:6, :].rearrange("p a (j t) -> p (a j) t", t=P)).then_inc(side_evac, 1)
                        else:
                            if k >= TT + 2:
                                act.wait_ge(nv_sums, b * PAIRS + (k - TT - 1))
                            nc.scalar.copy(NT[:, k % 2],
                                           ps[:, 4 + k % 2, :].rearrange("p (t m) -> p t m", t=TT)).then_inc(side_evac, 1)

                    for n in range(N_ITER):
                        for u in range(2):
                            k = 2 * n + u
                            side_exps(k)
                            if k:
                                side_evacs(k - 1)
                        for f in range(2):
                            act.wait_ge(step_ready, b * (2 * N_ITER) + (2 * n + f + 1))
                            pairs = slice(4 * f, 4 * f + 4)
                            if n < N_ITER - 1:
                                nc.scalar.copy(AV[:, (n + 1) % 2, pairs],
                                               ps[:, f, :].rearrange("p (j a m) -> p j a m", j=4, a=2)).then_inc(step_evac, 1)
                            else:
                                nc.scalar.copy(AV[:, (n + 1) % 2, pairs, 1],
                                               ps[:, f, 0:256].rearrange("p (j m) -> p j m", j=4)).then_inc(step_evac, 1)
                    side_evacs(SIDES - 1)
                    for g in range(G):
                        act.wait_ge(o_ready, b * G + (g + 1))
                        if g >= 2:
                            act.wait_ge(otok_T, b * G + (g - 1))
                        nc.scalar.copy(O_sb[:, g % 2, :], ps[:, 2 + g % 2, :]).then_inc(o_evac, 1)
                    act.wait_ge(oT_ready, b + 1)
                    nc.scalar.copy(oT[:], ps[:, 6, :]).then_inc(oT_evac, 1)
                    act.wait_ge(h2T_ready, b + 1)
                    nc.scalar.copy(hT[:], ps[:, 0, :]).then_inc(h2T_evac, 1)
                    act.wait_ge(lshift_ready, b + 1)
                    nc.scalar.activation(prob[:], logit[:], ACT.Exp).then_inc(prob_ready, 1)

            @block.tensor
            def _(pe):
                pe.wait_ge(ny_loaded, 48)
                pe.wait_ge(consts_pool, 11)
                with pe.Fori(0, B) as b:
                    pe.wait_ge(xn_ready, b + 1)
                    for t in range(TT):
                        last = nc.tensor.transpose(ps[:, 0, t * P:(t + 1) * P], xn[:, t, :], ident[:])
                    last.then_inc(xT_ready, 1)
                    pe.wait_ge(hT_ready, b + 1)
                    for s in range(2):
                        nc.tensor.matmul(ps[:, 1 + s, :], w_attn[:, s * C:(s + 1) * C], hT[:],
                                         start=True, stop=True).then_inc(qkv_ready, 1)
                    for t in range(TT):
                        last = nc.tensor.matmul(ps[:, 3, t * C:(t + 1) * C], hT[:, t * P:(t + 1) * P],
                                                w_attn[:, 2 * C:3 * C], start=True, stop=True)
                    last.then_inc(qkv_ready, 1)

                    def side_A(k):
                        if k == 0:
                            pe.wait_ge(qk_evac, b * 3 + 3)
                        if 1 <= k <= TT:
                            pe.wait_ge(side_max, b * SIDES + k)
                        if k > TT + 1:
                            pe.wait_ge(side_exp, b * SIDES + (k - 1))
                        if k < TT:
                            for h in range(H):
                                last = nc.tensor.matmul(ps[:, 2 + h // 8, (h % 8) * NL:(h % 8 + 1) * NL],
                                                        stack[:, 0, h, k * P:(k + 1) * P], stack[:, 1, h, T:QL],
                                                        start=True, stop=True)
                        else:
                            for h in (2 * (k - TT), 2 * (k - TT) + 1):
                                last = nc.tensor.matmul(ps[rows(h), 2 + k % 2, :], stack[:, 0, h, T:QL],
                                                        stack[:, 1, h, 0:T], start=True, stop=True,
                                                        tile_position=(0, NL * (h % 2)))
                        last.then_inc(side_scores, 1)

                    def side_B(k):
                        pe.wait_ge(side_exp, b * SIDES + (k + 1))
                        if k:
                            pe.wait_ge(side_evac, b * SIDES + k)
                        for m in range(PAIRS if k < TT else TT):
                            if k < TT:
                                last = nc.tensor.transpose(ps[:, 4 + m // 4, (m % 4) * P:(m % 4 + 1) * P],
                                                           L_tok[:, k % 2, m * P:(m + 1) * P], ident[:])
                            else:
                                last = nc.tensor.transpose(ps[:, 4 + k % 2, m * P:(m + 1) * P],
                                                           N_lm[:, k % 2, m * P:(m + 1) * P], ident[:])
                        last.then_inc(side_T, 1)

                    def side_C(k):
                        j = k - TT
                        pe.wait_ge(side_evac, b * SIDES + (k + 1))
                        for t in range(TT):
                            last = nc.tensor.matmul(ps[:, 7, j * 2 * HD:(j + 1) * 2 * HD], NT[:, k % 2, t, :],
                                                    v_tok[:, t, j * 2 * HD:(j + 1) * 2 * HD],
                                                    start=(t == 0), stop=(t == TT - 1))
                        last.then_inc(nv_sums, 1)

                    def each(f, out, lhs, rhs):
                        for h in range(8 * f, 8 * f + 8):
                            last = nc.tensor.matmul(out(h), lhs(h), rhs(h), start=True, stop=True)
                        return last

                    pe.wait_ge(stacked, b * (12 * 16) + 12 * 16)
                    for h in range(H):
                        last = nc.tensor.matmul(ps[rows(h), 4, h // 2 * NL:(h // 2 + 1) * NL], stack[:, 0, h, T:QL],
                                                stack[:, 1, h, T:QL], start=True, stop=True,
                                                tile_position=(0, NL * (h % 2)))
                    last.then_inc(kscore_ready, 1)
                    wait_apart(pe, k_ready, b + 1, passed)
                    nc.tensor.matmul(ps[:, 5, :], blocks[:], K_sb[:].rearrange("p j m -> p (j m)"),
                                     start=True, stop=True).then_inc(colsum_ready, 1)
                    for f in range(2):
                        last = each(f, lambda h: ps[rows(h), 6, h // 2 * NL:(h // 2 + 1) * NL],
                                    lambda h: K_sb[rows(h), h // 2, :], lambda h: ident[rows(h), rows(h)])
                    last.then_inc(kT_ready, 1)
                    wait_apart(pe, kT_evac, b + 1, passed)
                    for f in range(2):
                        each(f, lambda h: ps[rows(h), f, h // 2 % 4 * NL:(h // 2 % 4 + 1) * NL],
                             lambda h: KT[rows(h), h // 2, :], lambda h: KT[rows(h), h // 2, :]).then_inc(a0_ready, 1)
                    for n in range(N_ITER):
                        for s in range(2):
                            for f in range(2):
                                if s == 0:
                                    wait_apart(pe, a0_evac, b * 2 + (f + 1), passed)
                                    if n:
                                        wait_apart(pe, step_evac, b * (2 * N_ITER) + (2 * n + f - 1), passed)
                                wait_apart(pe, x_ready, b * (4 * N_ITER) + (4 * n + 2 * s + f + 1), passed)
                                each(f, lambda h: ps[rows(h), f, h // 2 % 4 * NL:(h // 2 % 4 + 1) * NL],
                                     lambda h: AV[rows(h), n % 2, h // 2, 0, :],
                                     lambda h: X[rows(h), h // 2, :]).then_inc(b_ready, 1)
                            k = 2 * n + s
                            side_A(k)
                            if k:
                                side_B(k - 1)
                            if k - 2 >= TT:
                                side_C(k - 2)
                        for f in range(2):
                            wait_apart(pe, q_ready, b * (2 * N_ITER) + (2 * n + f + 1), passed)
                            w = 2 * NL if n < N_ITER - 1 else NL
                            each(f, lambda h: ps[rows(h), f, h // 2 % 4 * w:(h // 2 % 4 + 1) * w],
                                 lambda h: Q[rows(h), h // 2, :],
                                 lambda h: AV[rows(h), n % 2, h // 2].rearrange("p a m -> p (a m)")[:, 2 * NL - w:]
                                 ).then_inc(step_ready, 1)
                    side_C(SIDES - 2)
                    side_B(SIDES - 1)
                    side_C(SIDES - 1)
                    wait_apart(pe, nv_ready, b + 1, passed)
                    wait_apart(pe, step_evac, b * (2 * N_ITER) + 2 * N_ITER, passed)
                    for f in range(2):
                        last = each(f, lambda h: ps[rows(h), 7, 256 + h // 2 * HD:256 + (h // 2 + 1) * HD],
                                    lambda h: AV[rows(h), N_ITER % 2, h // 2, 1, :], lambda h: Nv[rows(h), h // 2, :])
                    last.then_inc(z_ready, 1)
                    pe.wait_ge(z_evac, b + 1)

                    def tail(g):
                        pe.wait_ge(o_evac, b * G + (g + 1))
                        if g >= 2:
                            pe.wait_ge(otok_ready, b * G + (g - 1))
                        for t in range(TT):
                            last = nc.tensor.transpose(ps[:, 4 + g % 2, t * P:(t + 1) * P],
                                                       O_sb[:, g % 2, t * P:(t + 1) * P], ident[:])
                        last.then_inc(otok_T, 1)

                    for g in range(G):
                        if g >= 2:
                            pe.wait_ge(o_evac, b * G + (g - 1))
                        for m in range(2):
                            last = nc.tensor.matmul(ps[m * NL:(m + 1) * NL, 2 + g % 2, :], Z[:, 2 * g + m, :],
                                                    LT[:, 2 * g + m, :], start=True, stop=True,
                                                    tile_position=(0, NL * m))
                        last.then_inc(o_ready, 1)
                        if g:
                            tail(g - 1)
                    tail(G - 1)
                    pe.wait_ge(otok_ready, b * G + G)
                    for t in range(TT):
                        last = nc.tensor.transpose(ps[:, 6, t * P:(t + 1) * P], o_tok[:, t, :], ident[:])
                    last.then_inc(oT_ready, 1)
                    pe.wait_ge(oT_evac, b + 1)
                    pe.wait_ge(w_gated_ready, b + 1)
                    for t in range(TT):
                        last = nc.tensor.matmul(ps[:, 7, t * C:(t + 1) * C], oT[:, t * P:(t + 1) * P], w_gated[:],
                                                start=True, stop=True)
                    last.then_inc(y_ready, 1)
                    pe.wait_ge(h2_ready, b + 1)
                    for t in range(TT):
                        last = nc.tensor.transpose(ps[:, 0, t * P:(t + 1) * P], h2[:, t, :], ident[:])
                    last.then_inc(h2T_ready, 1)
                    pe.wait_ge(h2T_evac, b + 1)
                    for t in range(TT):
                        last = nc.tensor.matmul(ps[:, 1, t * E:(t + 1) * E], hT[:, t * P:(t + 1) * P], w_router[:],
                                                start=True, stop=True)
                    last.then_inc(logits_ready, 1)
                    pe.wait_ge(onehot_ready, b + 1)
                    for t in range(TT):
                        nc.tensor.matmul(ps[:, 1, (TT + t) * E:(TT + t + 1) * E], upto[:], onehot[:, t, :],
                                         start=True, stop=False)
                        last = nc.tensor.matmul(ps[:, 1, (TT + t) * E:(TT + t + 1) * E], ones[:], before[:, t, :],
                                                start=False, stop=True)
                    last.then_inc(count_ready, 1)

            @block.vector
            def _(dve):
                setup = Chain(dve, consts_dve).link
                dve.wait_ge(consts_pool, 11)
                setup(nc.vector.tensor_copy(rank[:], rank_i[:]))
                setup(nc.vector.tensor_tensor(eye[:], ident[:, 0:NL], ident[:, NL:P], ALU.add))
                for dst, by in ((eye7, 7.0), (eye15, 15.0), (eye325, 3.25)):
                    setup(nc.vector.tensor_scalar_mul(dst[:], eye[:], by))
                dve.wait_ge(ny_loaded, 48)

                with dve.Fori(0, B) as b:
                    chain = Chain(dve, ny_dve, links=NY_LINKS, turn=b)
                    link = chain.link
                    x_b = x_sb[:, bass.ds(b * TT, TT), :]

                    def norm(n):
                        for t in range(TT):
                            last = nc.vector.bn_stats(stats[:, t, :], x_sb[:, bass.ds(b * TT + t, 1), :].rearrange("p a c -> p (a c)"))
                        link(last, passed)
                        for t in range(TT):
                            last = nc.vector.bn_aggr(mean_var[:, t, :], stats[:, t, :])
                        link(last)
                        nc.vector.tensor_scalar_add(var_eps[:], mean_var[:, :, 1], LN_EPS).then_inc(var_ready, 1)
                        dve.wait_ge(rstd_ready, b * 2 + (n + 1))
                        for t in range(TT):
                            last = nc.vector.tensor_scalar(xn[:, t, :], x_sb[:, bass.ds(b * TT + t, 1), :].rearrange("p a c -> p (a c)"),
                                                           mean_var[:, t, 0:1], rstd[:, t:t + 1], ALU.subtract, ALU.mult)
                        return last

                    norm(0).then_inc(xn_ready, 1)
                    nc.vector.tensor_tensor(w_gated[:], w_proj[:], mod_row0[:, 0, bass.ds(b, 1), :].rearrange("p a c -> p (a c)"), ALU.mult).then_inc(w_gated_ready, 1)
                    for s in range(2):
                        dve.wait_ge(qk_evac, b * 3 + (s + 1))
                        link(nc.vector.tensor_reduce(lm[:, s, :], qk[:, s, 0:T].rearrange("p (l n) -> p l n", n=SEG), AX.X, ALU.add))
                        link(nc.vector.tensor_scalar_mul(qk[:, s, T:QL], lm[:, s, :], 1.0 / SEG))
                        link(nc.vector.tensor_copy(parts[:, s, 0, :], qk[:, s, :]))
                        link(nc.vector.tensor_tensor(rest[:, s, :], qk[:, s, :], parts[:, s, 0, :], ALU.subtract))
                        link(nc.vector.tensor_copy(parts[:, s, 1, :], rest[:, s, :]))
                        nc.vector.tensor_tensor(parts[:, s, 2, :], rest[:, s, :], parts[:, s, 1, :], ALU.subtract).then_inc(parts_ready, 1)
                    wide = [P, PAIRS, NL]
                    dve.wait_ge(kscore_ready, b + 1)
                    scores = ps[:, 4, :].rearrange("p (j m) -> p j m", j=PAIRS)
                    link(nc.vector.tensor_reduce(kmax[:], scores, AX.X, ALU.max))
                    nc.vector.tensor_tensor(K_sb[:], scores, bc(kmax[:].unsqueeze(2), wide), ALU.subtract).then_inc(kshift_ready, 1)
                    dve.wait_ge(kexp_ready, b + 1)
                    link(nc.vector.tensor_reduce(ksum[:], K_sb[:], AX.X, ALU.add))
                    link(nc.vector.reciprocal(krec[:], ksum[:]))
                    nc.vector.tensor_tensor(K_sb[:], K_sb[:], bc(krec[:].unsqueeze(2), wide), ALU.mult).then_inc(k_ready, 1)
                    dve.wait_ge(colsum_ready, b + 1)
                    dve.wait_ge(k_ready, b + 1)
                    link(nc.vector.tensor_reduce(den[:], ps[:, 5, :].rearrange("p (j m) -> p j m", j=PAIRS), AX.X, ALU.max))
                    link(nc.vector.reciprocal(rden[:], den[:]))
                    link(nc.vector.tensor_tensor(AV[:, 0, :, 1, :], K_sb[:], bc(rden[:].unsqueeze(2), wide), ALU.mult))
                    for f in range(2):
                        pairs = slice(4 * f, 4 * f + 4)
                        dve.wait_ge(a0_ready, b * 2 + (f + 1))
                        nc.vector.tensor_tensor(AV[:, 0, pairs, 0, :], ps[:, f, 0:256].rearrange("p (j m) -> p j m", j=4),
                                                bc(rden[:, pairs].unsqueeze(2), [P, 4, NL]), ALU.mult).then_inc(a0_evac, 1)

                    def side(k):
                        dve.wait_ge(side_scores, b * SIDES + (k + 1))
                        if k < TT:
                            s = ps[:, 2:4, :].rearrange("p a (h m) -> p (a h) m", m=NL)
                            link(nc.vector.tensor_reduce(lmax[:], s, AX.X, ALU.max))
                            if k >= 2:
                                dve.wait_ge(side_T, b * SIDES + (k - 1))
                            nc.vector.tensor_tensor(L_tok[:, k % 2, :].rearrange("p (h m) -> p h m", m=NL), s,
                                                    bc(lmax[:].unsqueeze(2), [P, H, NL]), ALU.subtract).then_inc(side_max, 1)
                        else:
                            nc.vector.tensor_reduce(nmax[:, k - TT:k - TT + 1], ps[:, 2 + k % 2, :], AX.X, ALU.max,
                                                    negate=True).then_inc(side_max, 1)

                    for n in range(N_ITER):
                        for s in range(2):
                            for f in range(2):
                                pairs = slice(4 * f, 4 * f + 4)
                                if s == 0:
                                    if n == 0:
                                        dve.wait_ge(a0_evac, b * 2 + (f + 1))
                                    else:
                                        dve.wait_ge(step_evac, b * (2 * N_ITER) + (2 * n + f - 1))
                                    a = AV[:, n % 2, pairs, 0, :]
                                    scale, shift = -1.0, eye7
                                else:
                                    dve.wait_ge(b_ready, b * (4 * N_ITER) + (4 * n + f + 1))
                                    a, scale, shift = ps[:, f, 0:256].rearrange("p (j m) -> p j m", j=4), -1.0, eye15
                                nc.vector.scalar_tensor_tensor(out=X[:, pairs, :], in0=a, scalar=scale,
                                                               in1=bc(shift[:].unsqueeze(1), [P, 4, NL]),
                                                               op0=ALU.mult, op1=ALU.add).then_inc(x_ready, 1)
                            side(2 * n + s)
                        for f in range(2):
                            pairs = slice(4 * f, 4 * f + 4)
                            dve.wait_ge(b_ready, b * (4 * N_ITER) + (4 * n + 2 + f + 1))
                            nc.vector.scalar_tensor_tensor(out=Q[:, pairs, :], in0=ps[:, f, 0:256].rearrange("p (j m) -> p j m", j=4),
                                                           scalar=-0.25, in1=bc(eye325[:].unsqueeze(1), [P, 4, NL]),
                                                           op0=ALU.mult, op1=ALU.add).then_inc(q_ready, 1)
                    dve.wait_ge(nv_sums, b * PAIRS + PAIRS)
                    link(nc.vector.reciprocal(nrec[:], nsum[:]))
                    for r in range(2):
                        part = ps[r * NL:(r + 1) * NL, 7, 0:P].rearrange("p (j a d) -> p j a d", a=2, d=HD)[:, :, r, :]
                        last = nc.vector.tensor_tensor(Nv[r * NL:(r + 1) * NL], part,
                                                       bc(nrec[r * NL:(r + 1) * NL].unsqueeze(2), [NL, PAIRS, HD]), ALU.mult)
                    last.then_inc(nv_ready, 1)
                    dve.wait_ge(z_ready, b + 1)
                    for r in range(2):
                        last = nc.vector.tensor_copy(Z[r * NL:(r + 1) * NL, :, 32 * r:32 * r + HD],
                                                     ps[r * NL:(r + 1) * NL, 7, 256:256 + 64].rearrange("p (j d) -> p j d", d=HD))
                    last.then_inc(z_evac, 1)
                    for g in range(G):
                        dve.wait_ge(otok_T, b * G + (g + 1))
                        if g:
                            dve.wait_ge(otok_ready, b * G + g)
                        o = ps[:, 4 + g % 2, :].rearrange("p (t j r) -> p t j r", t=TT, j=4)
                        link(nc.vector.reciprocal(orec[:], o[:, :, :, HD]))
                        nc.vector.tensor_tensor(o_tok[:, :, g * 32:(g + 1) * 32].rearrange("p t (j d) -> p t j d", j=4),
                                                o[:, :, :, 0:HD], bc(orec[:].unsqueeze(3), [P, TT, 4, HD]),
                                                ALU.mult).then_inc(otok_ready, 1)
                    dve.wait_ge(y_ready, b + 1)
                    link(nc.vector.tensor_tensor(x_b, x_b, ps[:, 7, :].rearrange("p (t c) -> p t c", t=TT), ALU.add), passed)
                    link(norm(1))
                    wide = [P, TT, C]
                    dve.wait_ge(h2_free, b + 1)
                    link(nc.vector.tensor_tensor(h2[:], xn[:], bc(mod_row0[:, 2, bass.ds(b, 1), :], wide), ALU.mult))
                    nc.vector.tensor_tensor(h2[:], h2[:], bc(mod_row0[:, 1, bass.ds(b, 1), :], wide), ALU.add).then_inc(h2_ready, 1)
                    wide = [P, TT, E]
                    dve.wait_ge(logits_ready, b + 1)
                    lg = ps[:, 1, 0:TT * E].rearrange("p (t e) -> p t e", t=TT)
                    link(nc.vector.tensor_reduce(lgmax[:], lg, AX.X, ALU.max))
                    nc.vector.tensor_tensor(logit[:], lg, bc(lgmax[:].unsqueeze(2), wide), ALU.subtract).then_inc(lshift_ready, 1)
                    dve.wait_ge(lshift_ready, b + 1)
                    link(nc.vector.tensor_single_scalar(first[:], logit[:], 0.0, ALU.is_equal))
                    link(nc.vector.tensor_tensor(first[:], first[:], bc(rank[:].unsqueeze(1), wide), ALU.mult))
                    link(nc.vector.tensor_reduce(top[:], first[:], AX.X, ALU.max))
                    link(nc.vector.tensor_tensor(onehot[:], first[:], bc(top[:].unsqueeze(2), wide), ALU.is_equal))
                    for t in range(TT):
                        last = nc.vector.tensor_tensor(before[:, t + 1, :], before[:, t, :], onehot[:, t, :], ALU.add)
                        if t < TT - 1:
                            link(last)
                    last.then_inc(onehot_ready, 1)
                    dve.wait_ge(prob_ready, b + 1)
                    link(nc.vector.tensor_reduce(psum_[:], prob[:], AX.X, ALU.add))
                    link(nc.vector.reciprocal(gate[:], psum_[:]))
                    dve.wait_ge(count_ready, b + 1)
                    link(nc.vector.tensor_copy(before[:, 0, :], before[:, TT, :]))
                    link(nc.vector.tensor_tensor(count[:], onehot[:], ps[:, 1, TT * E:2 * TT * E].rearrange("p (t e) -> p t e", t=TT), ALU.mult))
                    link(nc.vector.tensor_reduce(pos1[:], count[:], AX.X, ALU.add))
                    link(nc.vector.tensor_single_scalar(keep[:], pos1[:], float(CAP), ALU.is_le))
                    link(nc.vector.tensor_tensor(gate_keep[:, bass.ds(b * TT, TT)], gate[:], keep[:], ALU.mult))
                    link(nc.vector.tensor_scalar(slot[:], top[:], -float(CAP), float(E * CAP - 1), ALU.mult, ALU.add))
                    link(nc.vector.tensor_tensor(slot[:], slot[:], pos1[:], ALU.add))
                    link(nc.vector.tensor_scalar(beyond[:], keep[:], -2.0 * E * CAP, 2.0 * E * CAP, ALU.mult, ALU.add))
                    link(nc.vector.tensor_tensor(slot[:], slot[:], beyond[:], ALU.add))
                    link(nc.vector.tensor_copy(slot_all[:, bass.ds(b * TT, TT)], slot[:]))
                    nc.vector.tensor_copy(slot_now[:], slot[:]).then_inc(slot_ready, 1)
                    chain.done()


def expert_phase(nc, sb_, sem, ps, ident, strips, bias_dram, slots_in, slots_out, w1, w2):
    local = ExitStack()
    with local:
        def sb(name, shape, dt=FP32):
            return sb_(name, shape, dt, local)

        FT = F0 // P
        CT = CAP // P
        x_e = sb("x_e", [P, 2, CT, C])
        w1_e = sb("w1_e", [P, 2, F0])
        w2_e = sb("w2_e", [P, 2, FT, C])
        xT_e = sb("xT_e", [P, 2, CAP])
        hid = sb("hid", [P, 2, FT, CAP])
        y_e = sb("y_e", [P, 2, CT, C])

        strips_loaded = sem("strips_loaded")
        expert_loaded = [sem("expert_loaded0"), sem("expert_loaded1")]
        expert_stored = [sem("expert_stored0"), sem("expert_stored1")]
        ex_xT_ready = sem("ex_xT_ready")
        ex_xT_evac = sem("ex_xT_evac")
        hidden_ready = sem("hidden_ready")
        hidden_evac = sem("hidden_evac")
        ex_y_ready = sem("ex_y_ready")
        ex_y_evac = sem("ex_y_evac")

        def run(eng, emit):
            with eng.Fori(0, E // 2) as i:
                for u in range(2):
                    emit(i, u)

        with nc.Block() as block:
            @block.sync
            def _(sp):
                def load(i, u):
                    sp.wait_ge(ex_y_ready, i * 2 + 1)
                    e = i * 2 + u
                    sp.dma_start(x_e[:, u], slots_in[bass.ds(e * CAP, CAP), :].rearrange("(t p) c -> p t c", p=P)).then_inc(expert_loaded[u], 16)
                    sp.dma_start(w1_e[:, u], w1[bass.ds(e, 1)].rearrange("a p f -> p (a f)")).then_inc(expert_loaded[u], 16)
                    sp.dma_start(w2_e[:, u], w2[bass.ds(e, 1)].rearrange("a (t p) c -> p (a t) c", p=P)).then_inc(expert_loaded[u], 16)
                run(sp, load)

            @block.gpsimd
            def _(pool):
                for h in range(H):
                    src = bass.AP(bias_dram.tensor, h * 2 * T, [[1, P], [1, STRIP]])
                    pool.dma_start(strips[:, h, :], src).then_inc(strips_loaded, 16)
                pool.wait_ge(strips_loaded, 16 * H)

            @block.scalar
            def _(act):
                def emit(i, u):
                    act.wait_ge(ex_xT_ready, i * 2 + (u + 1))
                    nc.scalar.copy(xT_e[:, u], ps[:, u, :]).then_inc(ex_xT_evac, 1)
                    for f in range(FT):
                        act.wait_ge(hidden_ready, i * (2 * FT) + (u * FT + f + 1))
                        nc.scalar.activation(hid[:, u, f, :], ps[:, 2 + f, :], ACT.Gelu_apprx_tanh).then_inc(hidden_evac, 1)
                    act.wait_ge(ex_y_evac, i * 2 + (u + 2))
                    act.dma_start(slots_out[bass.ds((i * 2 + u) * CAP, CAP), :].rearrange("(t p) c -> p t c", p=P),
                                  y_e[:, u]).then_inc(expert_stored[u], 16)
                for u in range(2):
                    act.sem_inc(expert_stored[u], 16)
                run(act, emit)
                for u in range(2):
                    act.wait_ge(expert_stored[u], 16 * (E // 2) + 16)

            @block.tensor
            def _(pe):
                def emit(i, u):
                    pe.wait_ge(expert_loaded[u], i * 48 + 48)
                    for t in range(CT):
                        last = nc.tensor.transpose(ps[:, u, t * P:(t + 1) * P], x_e[:, u, t, :], ident[:])
                    last.then_inc(ex_xT_ready, 1)
                    pe.wait_ge(ex_xT_evac, i * 2 + (u + 1))
                    for f in range(FT):
                        nc.tensor.matmul(ps[:, 2 + f, :], w1_e[:, u, f * P:(f + 1) * P], xT_e[:, u], start=True,
                                         stop=True).then_inc(hidden_ready, 1)
                    pe.wait_ge(hidden_evac, i * (2 * FT) + (u + 1) * FT)
                    pe.wait_ge(ex_y_evac, i * 2 + 1)
                    for t in range(CT):
                        for f in range(FT):
                            last = nc.tensor.matmul(ps[:, 6 + u, t * C:(t + 1) * C], hid[:, u, f, t * P:(t + 1) * P],
                                                    w2_e[:, u, f, :], start=(f == 0), stop=(f == FT - 1))
                    last.then_inc(ex_y_ready, 1)
                pe.sem_inc(ex_y_ready, 1)
                run(pe, emit)

            @block.vector
            def _(dve):
                def emit(i, u):
                    dve.wait_ge(ex_y_ready, i * 2 + (u + 2))
                    dve.wait_ge(expert_stored[u], i * 16 + 16)
                    nc.vector.tensor_copy(y_e[:, u], ps[:, 6 + u, :].rearrange("p (t c) -> p t c", t=CT)).then_inc(ex_y_evac, 1)
                dve.sem_inc(ex_y_evac, 1)
                run(dve, emit)


L1_LINKS = 62
TILES = H * TT
FT1 = F1 // P


def evac_by_vector(i):
    return i % 3 == 2


def moved_by(vector, n):
    return sum(evac_by_vector(i) == vector for i in range(n))


SLOTS = 5
S_BANKS = (0, 1, 2, 6)
T_BANKS = (3, 4, 7)
BY_ACT, BY_DVE = moved_by(False, TILES), moved_by(True, TILES)


def layer1_phase(nc, sb_, sem, ps, x_sb, ident, half, mod_col, gb0, mod_row1, strips, parts_dram, gate_keep,
                 slot_all, slots_out, w_in, w_gate, b_gate, g1, Wq, Wdkv, Wuk, Wuv, Wo, g2, gate_w, w1, w2, out):
    local = ExitStack()
    with local:
        def sb(name, shape, dt=FP32):
            return sb_(name, shape, dt, local)

        w_in_sb = sb("w_in_sb", [P, 3 * C])
        w_gate_sb = sb("w_gate_sb", [P, 2 * C])
        b_gate_sb = sb("b_gate_sb", [P, 2 * C])
        g1_col = sb("g1_col", [P, 1])
        g2_col = sb("g2_col", [P, 1])
        Wq_sb = sb("Wq_sb", [P, C])
        Wdkv_sb = sb("Wdkv_sb", [P, LAT])
        Wuk_sb = sb("Wuk_sb", [LAT, C])
        Wuv_sb = sb("Wuv_sb", [LAT, C])
        Wo_sb = sb("Wo_sb", [P, C])
        gate_w_sb = sb("gate_w_sb", [P, E])
        w1_e = sb("l1_w1_e", [P, 2, F1])
        w2_e = sb("l1_w2_e", [P, 2, FT1, C])
        mask = sb("mask", [P, T])
        rank_i = sb("l1_rank_i", [P, E], INT32)
        rank = sb("l1_rank", [P, E])
        slot_now = sb("l1_slot_now", [P, TT], INT32)
        y0 = sb("y0", [P, TT, C])
        stats = sb("l1_stats", [P, TT, 6])
        mean_var = sb("l1_mean_var", [P, TT, 2])
        var_eps = sb("l1_var_eps", [P, TT])
        rstd = sb("l1_rstd", [P, TT])
        xn = sb("l1_xn", [P, TT, C])
        hT = sb("l1_hT", [P, T])
        stack = sb("l1_stack", [STACK, 2, H, T], BF16)
        v_aug = sb("v_aug", [P, TT, H, 32])
        probs = sb("probs", [P, 3, T])
        nmax = sb("l1_nmax", [P, 4])
        PT = sb("PT", [P, SLOTS, TT, T])
        flat = PT[:].rearrange("p j k q -> p (j k q)")
        qk = flat[:, 0:2 * T].rearrange("p (s t) -> p s t", s=2)
        rest = flat[:, 2 * T:4 * T].rearrange("p (s t) -> p s t", s=2)
        parts = flat[:, 4 * T:7 * T].bitcast(BF16).rearrange("p (s n t) -> p s n t", s=2, n=3)
        latT = flat[0:LAT, 7 * T:8 * T]
        hid = flat[:, 0:2 * FT1 * T].rearrange("p (u f t) -> p u f t", u=2, f=FT1)
        O_sb = sb("l1_O_sb", [P, T])
        orec = sb("l1_orec", [P, TT, 4])
        o_tok = sb("l1_o_tok", [P, TT, C])
        oT = sb("l1_oT", [P, T])
        gated = flat[:, 0:4 * 2 * C].rearrange("p (t c) -> p t c", t=TT)
        h_tok = sb("h_tok", [P, TT, C])
        squares = sb("squares", [P, C])
        ssum = sb("ssum", [P, TT])
        logit = sb("l1_logit", [P, TT, E])
        small = sb("small", [P, 6, TT, E])
        tops = sb("tops", [P, 6, TT])
        combine = sb("combine", [P, TT, E])

        l1_loaded = sem("l1_loaded")
        l1_pool = sem("l1_pool")
        l1_consts = sem("l1_consts")
        slot_now_ready = sem("slot_now_ready")
        gathered = sem("gathered")
        l1_var_ready = sem("l1_var_ready")
        l1_rstd_ready = sem("l1_rstd_ready")
        tok_ready = sem("l1_tok_ready")
        tok_T = sem("l1_tok_T")
        hT_ready = sem("l1_hT_ready")
        lat_ready = sem("lat_ready")
        lat_evac = sem("lat_evac")
        qkv_ready = sem("l1_qkv_ready")
        qkv_evac = sem("l1_qkv_evac")
        parts_ready = sem("l1_parts_ready")
        parts_stored = [sem("l1_q_parts_stored"), sem("l1_k_parts_stored")]
        stacked = sem("l1_stacked")
        scores_ready = sem("scores_ready")
        biased_ready = sem("biased_ready")
        probs_ready = sem("probs_ready")
        probs_T = sem("probs_T")
        moved_act = sem("moved_act")
        moved_dve = sem("moved_dve")
        o_ready = sem("l1_o_ready")
        o_evac = sem("l1_o_evac")
        otok_T = sem("l1_otok_T")
        otok_ready = sem("l1_otok_ready")
        oT_ready = sem("l1_oT_ready")
        oT_evac = sem("l1_oT_evac")
        proj_ready = sem("proj_ready")
        gated_ready = sem("gated_ready")
        sigmoid_ready = sem("sigmoid_ready")
        l1_logits = sem("l1_logits")
        gap_ready = sem("gap_ready")
        gap_exp = sem("gap_exp")
        experts_loaded = [sem("l1_expert_loaded0"), sem("l1_expert_loaded1")]
        hid_ready = sem("hid_ready")
        hid_evac = sem("hid_evac")
        ye_ready = sem("ye_ready")
        ye_added = sem("ye_added")
        x_done = sem("x_done")
        stored = sem("stored")
        l1_dve = sem("l1_dve")
        passed = sem("l1_passed")

        def keys(a, q):
            return T if a == 0 else (q + 1) * P

        with nc.Block() as block:
            @block.sync
            def _(sp):
                for dst, src in ((w_in_sb, w_in), (w_gate_sb, w_gate), (Wq_sb, Wq), (Wdkv_sb, Wdkv), (Wuk_sb, Wuk),
                                 (Wuv_sb, Wuv), (Wo_sb, Wo), (gate_w_sb, gate_w)):
                    sp.dma_start(dst[:], src).then_inc(l1_loaded, 16)
                sp.dma_start(b_gate_sb[:], b_gate.rearrange("(a c) -> a c", a=1).to_broadcast([P, 2 * C])).then_inc(l1_loaded, 16)
                for dst, src in ((g1_col, g1), (g2_col, g2)):
                    sp.dma_start(dst[:], src.rearrange("(c a) -> c a", a=1)).then_inc(l1_loaded, 16)
                with sp.Fori(0, B) as b:
                    for a in range(2):
                        for s in range(2):
                            sp.wait_ge(parts_ready, b * 4 + (2 * a + s + 1))
                            sp.dma_start(parts_dram[s][:, :, 0:T].rearrange("n p t -> p n t"), parts[:, s]).then_inc(parts_stored[s], 16)
                        for s in range(2):
                            sp.wait_ge(parts_stored[s], b * 32 + (16 * a + 16))
                            rows = parts_dram[s][:, :, 0:T].rearrange("n (d h) t -> (n d) h t", d=HD)
                            for i in range(3):
                                if s == 0:
                                    sp.dma_start(stack[3 * HD * i:3 * HD * (i + 1), s], rows).then_inc(stacked, 16)
                                else:
                                    for j in range(3):
                                        sp.dma_start(stack[HD * (3 * i + j):HD * (3 * i + j + 1), s],
                                                     rows[HD * i:HD * (i + 1)]).then_inc(stacked, 16)
                    for e in range(E):
                        if e >= 2:
                            sp.wait_ge(ye_ready, b * E + (e - 1))
                        sp.dma_start(w1_e[:, e % 2], w1[e]).then_inc(experts_loaded[e % 2], 16)
                        sp.dma_start(w2_e[:, e % 2], w2[e].rearrange("(f p) c -> p f c", p=P)).then_inc(experts_loaded[e % 2], 16)
                    sp.wait_ge(x_done, b + 1)
                    sp.dma_start(out[bass.ds(b, 1)].rearrange("a (t p) c -> p (a t) c", p=P),
                                 x_sb[:, bass.ds(b * TT, TT), :]).then_inc(stored, 16)
                sp.wait_ge(stored, 16 * B)

            @block.gpsimd
            def _(pool):
                link = Chain(pool, l1_pool).link
                link(nc.gpsimd.memset(stack[64:STACK, :, :, :], 0.0))
                link(nc.gpsimd.memset(v_aug[:], 1.0))
                link(nc.gpsimd.memset(y0[:], 0.0))
                link(nc.gpsimd.memset(mask[:], 0.0))
                link(nc.gpsimd.iota(rank_i[:], [[-1, E]], base=E, channel_multiplier=0))
                link(nc.gpsimd.affine_select(out=mask[:], in_=mask[:], compare_op=ALU.is_ge, fill=-BIG, base=T - P,
                                             pattern=[[-1, T]], channel_multiplier=1))
                with pool.Fori(0, B) as b:
                    wait_apart(pool, slot_now_ready, b + 1, passed)
                    for t in range(TT):
                        nc.gpsimd.indirect_dma_start(y0[:, t, :], None, slots_out,
                                                     bass.IndirectOffsetOnAxis(ap=slot_now[:, t:t + 1], axis=0),
                                                     bounds_check=E * CAP - 1, oob_is_err=False).then_inc(gathered, 16)
                    for n in range(4):
                        pool.wait_ge(l1_var_ready, b * 4 + (n + 1))
                        nc.gpsimd.tensor_tensor(rstd[:], var_eps[:], bc(half[:], [P, TT]), ALU.pow).then_inc(l1_rstd_ready, 1)

            @block.scalar
            def _(act):
                act.wait_ge(l1_pool, 6)
                act.wait_ge(l1_loaded, 16 * 11)
                with act.Fori(0, B) as b:
                    def attention(a):
                        act.wait_ge(qkv_ready, b * 6 + (3 * a + 1))
                        nc.scalar.activation(qk[:, 0, :], ps[:, 1, :], ACT.Copy, scale=float(HD) ** -0.5).then_inc(qkv_evac, 1)
                        act.wait_ge(qkv_ready, b * 6 + (3 * a + 2))
                        nc.scalar.copy(qk[:, 1, :], ps[:, 2, :]).then_inc(qkv_evac, 1)
                        act.wait_ge(qkv_ready, b * 6 + (3 * a + 3))
                        nc.scalar.copy(v_aug[:, :, :, 0:HD], ps[:, 3, :].rearrange("p (t h d) -> p t h d", t=TT, h=H)).then_inc(qkv_evac, 1)

                        def exp(i):
                            n = keys(a, i % TT)
                            act.wait_ge(biased_ready, b * (2 * TILES) + (a * TILES + i + 1))
                            if i >= 3:
                                act.wait_ge(probs_T, b * (2 * TILES) + (a * TILES + i - 2))
                            nc.scalar.activation(probs[:, i % 3, 0:n], ps[:, S_BANKS[i % 4], 0:n], ACT.Exp, bias=nmax[:, i % 4:i % 4 + 1],
                                                 scale=-1.0).then_inc(probs_ready, 1)

                        def move(i):
                            if evac_by_vector(i):
                                return
                            h, q = i // TT, i % TT
                            n = keys(a, q) // P
                            act.wait_ge(probs_T, b * (2 * TILES) + (a * TILES + i + 1))
                            if h >= SLOTS:
                                act.wait_ge(o_ready, b * (2 * G) + (a * G + (h - SLOTS) // 4 + 1))
                            nc.scalar.copy(PT[:, h % SLOTS, 0:n, q * P:(q + 1) * P],
                                           ps[:, T_BANKS[i % 3], 0:n * P].rearrange("p (k q) -> p k q", k=n)).then_inc(moved_act, 1)

                        def o_out(g):
                            act.wait_ge(o_ready, b * (2 * G) + (a * G + g + 1))
                            if g:
                                act.wait_ge(otok_T, b * (2 * G) + (a * G + g))
                            nc.scalar.copy(O_sb[:], ps[:, 5, :]).then_inc(o_evac, 1)

                        for i in range(TILES):
                            exp(i)
                            if i >= 2:
                                move(i - 2)
                            if i % 16 == 7 and i > 7:
                                o_out(i // 16 - 1)
                        move(TILES - 2)
                        move(TILES - 1)
                        o_out(G - 1)
                        act.wait_ge(oT_ready, b * 2 + (a + 1))
                        nc.scalar.copy(oT[:], ps[:, 0, :]).then_inc(oT_evac, 1)

                    act.wait_ge(tok_T, b * 3 + 1)
                    nc.scalar.activation(hT[:], ps[:, 0, :], ACT.Identity, bias=mod_col[:, 1, 0, bass.ds(b, 1)],
                                         scale=mod_col[:, 1, 1, bass.ds(b, 1)]).then_inc(hT_ready, 1)
                    attention(0)
                    act.wait_ge(gated_ready, b + 1)
                    nc.scalar.activation(gated[:, :, C:2 * C], gated[:, :, C:2 * C], ACT.Sigmoid).then_inc(sigmoid_ready, 1)
                    act.wait_ge(tok_T, b * 3 + 2)
                    nc.scalar.activation(hT[:], ps[:, 0, :], ACT.Copy, scale=g1_col[:]).then_inc(hT_ready, 1)
                    act.wait_ge(lat_ready, b + 1)
                    nc.scalar.copy(latT, ps[0:LAT, 4, :]).then_inc(lat_evac, 1)
                    attention(1)
                    act.wait_ge(tok_T, b * 3 + 3)
                    nc.scalar.activation(hT[:], ps[:, 0, :], ACT.Copy, scale=g2_col[:]).then_inc(hT_ready, 1)
                    act.wait_ge(gap_ready, b + 1)
                    nc.scalar.activation(tops[:, 2], tops[:, 2], ACT.Exp).then_inc(gap_exp, 1)
                    for e in range(E):
                        for f in range(FT1):
                            m = e * FT1 + f
                            act.wait_ge(hid_ready, b * (E * FT1) + (m + 1))
                            if e >= 2:
                                act.wait_ge(ye_ready, b * E + (e - 1))
                            nc.scalar.activation(hid[:, e % 2, f, :], ps[:, 2 + m % 4, :], ACT.Silu).then_inc(hid_evac, 1)

            @block.tensor
            def _(pe):
                pe.wait_ge(l1_loaded, 16 * 11)
                pe.wait_ge(l1_pool, 6)
                with pe.Fori(0, B) as b:
                    def turned(n, rows):
                        pe.wait_ge(tok_ready, b * 3 + (n + 1))
                        for t in range(TT):
                            last = nc.tensor.transpose(ps[:, 0, t * P:(t + 1) * P], rows[:, t, :], ident[:])
                        last.then_inc(tok_T, 1)
                        pe.wait_ge(hT_ready, b * 3 + (n + 1))

                    def attention(a):
                        def scores(i):
                            h, q = i // TT, i % TT
                            if i >= 4:
                                pe.wait_ge(probs_ready, b * (2 * TILES) + (a * TILES + i - 3))
                            nc.tensor.matmul(ps[:, S_BANKS[i % 4], 0:keys(a, q)], stack[:, 0, h, q * P:(q + 1) * P],
                                             stack[:, 1, h, 0:keys(a, q)], start=True, stop=True).then_inc(scores_ready, 1)

                        def moved(n):
                            if moved_by(False, n):
                                pe.wait_ge(moved_act, b * (2 * BY_ACT) + (a * BY_ACT + moved_by(False, n)))
                            if moved_by(True, n):
                                pe.wait_ge(moved_dve, b * (2 * BY_DVE) + (a * BY_DVE + moved_by(True, n)))

                        def transpose(i):
                            pe.wait_ge(probs_ready, b * (2 * TILES) + (a * TILES + i + 1))
                            if i >= 3:
                                moved(i - 2)
                            for k in range(keys(a, i % TT) // P):
                                last = nc.tensor.transpose(ps[:, T_BANKS[i % 3], k * P:(k + 1) * P],
                                                           probs[:, i % 3, k * P:(k + 1) * P], ident[:])
                            last.then_inc(probs_T, 1)

                        def values(g, k):
                            if k == 0:
                                moved((g + 1) * 4 * TT)
                                if g:
                                    pe.wait_ge(otok_ready, b * (2 * G) + (a * G + g))
                            q0 = 0 if a == 0 else k * P
                            for j in range(4):
                                last = nc.tensor.matmul(ps[32 * j:32 * (j + 1), 5, q0:T], v_aug[:, k, 4 * g + j, :],
                                                        PT[:, (4 * g + j) % SLOTS, k, q0:T], start=(k == 0), stop=(k == TT - 1),
                                                        tile_position=(0, 32 * j))
                            if k == TT - 1:
                                last.then_inc(o_ready, 1)

                        def tail(g):
                            pe.wait_ge(o_evac, b * (2 * G) + (a * G + g + 1))
                            for t in range(TT):
                                last = nc.tensor.transpose(ps[:, 5, t * P:(t + 1) * P], O_sb[:, t * P:(t + 1) * P], ident[:])
                            last.then_inc(otok_T, 1)

                        pe.wait_ge(stacked, b * (24 * 16) + (a + 1) * 12 * 16)
                        scores(0)
                        scores(1)
                        scores(2)
                        for i in range(TILES):
                            if i + 3 < TILES:
                                scores(i + 3)
                            transpose(i)
                            if i % 16 in (2, 3, 4, 5) and i > 16:
                                values(i // 16 - 1, i % 16 - 2)
                            if i % 16 == 9 and i > 16:
                                tail(i // 16 - 1)
                        for k in range(TT):
                            values(G - 1, k)
                        tail(G - 1)
                        pe.wait_ge(otok_ready, b * (2 * G) + (a * G + G))
                        for t in range(TT):
                            last = nc.tensor.transpose(ps[:, 0, t * P:(t + 1) * P], o_tok[:, t, :], ident[:])
                        last.then_inc(oT_ready, 1)
                        pe.wait_ge(oT_evac, b * 2 + (a + 1))

                    turned(0, xn)
                    for bank, first in ((1, 2 * C), (2, 0)):
                        nc.tensor.matmul(ps[:, bank, :], w_in_sb[:, first:first + C], hT[:], start=True,
                                         stop=True).then_inc(qkv_ready, 1)
                    for t in range(TT):
                        last = nc.tensor.matmul(ps[:, 3, t * C:(t + 1) * C], hT[:, t * P:(t + 1) * P], w_in_sb[:, C:2 * C],
                                                start=True, stop=True)
                    last.then_inc(qkv_ready, 1)
                    pe.wait_ge(qkv_evac, b * 6 + 3)
                    attention(0)
                    for t in range(TT):
                        last = nc.tensor.matmul(ps[:, 1 + t // 2, (t % 2) * 2 * C:(t % 2 + 1) * 2 * C], oT[:, t * P:(t + 1) * P],
                                                w_gate_sb[:], start=True, stop=True)
                    last.then_inc(proj_ready, 1)
                    turned(1, xn)
                    nc.tensor.matmul(ps[0:LAT, 4, :], Wdkv_sb[:], hT[:], start=True, stop=True).then_inc(lat_ready, 1)
                    nc.tensor.matmul(ps[:, 1, :], Wq_sb[:], hT[:], start=True, stop=True).then_inc(qkv_ready, 1)
                    wait_apart(pe, lat_evac, b + 1, passed)
                    nc.tensor.matmul(ps[:, 2, :], Wuk_sb[:], latT, start=True, stop=True).then_inc(qkv_ready, 1)
                    for t in range(TT):
                        last = nc.tensor.matmul(ps[:, 3, t * C:(t + 1) * C], latT[:, t * P:(t + 1) * P], Wuv_sb[:],
                                                start=True, stop=True)
                    last.then_inc(qkv_ready, 1)
                    pe.wait_ge(qkv_evac, b * 6 + 6)
                    attention(1)
                    for t in range(TT):
                        last = nc.tensor.matmul(ps[:, 1, t * C:(t + 1) * C], oT[:, t * P:(t + 1) * P], Wo_sb[:],
                                                start=True, stop=True)
                    last.then_inc(proj_ready, 1)
                    turned(2, xn)
                    for t in range(TT):
                        last = nc.tensor.matmul(ps[:, 1, t * E:(t + 1) * E], hT[:, t * P:(t + 1) * P], gate_w_sb[:],
                                                start=True, stop=True)
                    last.then_inc(l1_logits, 1)

                    def hidden(e):
                        pe.wait_ge(experts_loaded[e % 2], b * (E // 2 * 32) + (e // 2 + 1) * 32)
                        for f in range(FT1):
                            m = e * FT1 + f
                            if m >= 4:
                                pe.wait_ge(hid_evac, b * (E * FT1) + (m - 3))
                            nc.tensor.matmul(ps[:, 2 + m % 4, :], w1_e[:, e % 2, f * P:(f + 1) * P], hT[:],
                                             start=True, stop=True).then_inc(hid_ready, 1)

                    hidden(0)
                    for e in range(E):
                        if e + 1 < E:
                            hidden(e + 1)
                        pe.wait_ge(hid_evac, b * (E * FT1) + (e + 1) * FT1)
                        if e >= 2:
                            pe.wait_ge(ye_added, b * E + (e - 1))
                        for t in range(TT):
                            for f in range(FT1):
                                last = nc.tensor.matmul(ps[:, 6 + e % 2, t * C:(t + 1) * C], hid[:, e % 2, f, t * P:(t + 1) * P],
                                                        w2_e[:, e % 2, f, :], start=(f == 0), stop=(f == FT1 - 1))
                        last.then_inc(ye_ready, 1)

            @block.vector
            def _(dve):
                dve.wait_ge(l1_pool, 6)
                dve.wait_ge(l1_loaded, 16 * 11)
                nc.vector.tensor_copy(rank[:], rank_i[:]).then_inc(l1_consts, 1)
                dve.wait_ge(l1_consts, 1)
                with dve.Fori(0, B) as b:
                    chain = Chain(dve, l1_dve, links=L1_LINKS, turn=b)
                    link = chain.link
                    x_b = x_sb[:, bass.ds(b * TT, TT), :]
                    wide = [P, TT, C]

                    def x_tile(t):
                        return x_sb[:, bass.ds(b * TT + t, 1), :].rearrange("p a c -> p (a c)")

                    def row(k):
                        return bc(mod_row1[:, k, bass.ds(b, 1), :], wide)

                    def layernorm(n):
                        for t in range(TT):
                            last = nc.vector.bn_stats(stats[:, t, :], x_tile(t))
                        link(last, passed)
                        for t in range(TT):
                            last = nc.vector.bn_aggr(mean_var[:, t, :], stats[:, t, :])
                        link(last)
                        nc.vector.tensor_scalar_add(var_eps[:], mean_var[:, :, 1], LN_EPS).then_inc(l1_var_ready, 1)
                        dve.wait_ge(l1_rstd_ready, b * 4 + (n + 1))
                        for t in range(TT):
                            last = nc.vector.tensor_scalar(xn[:, t, :], x_tile(t), mean_var[:, t, 0:1], rstd[:, t:t + 1],
                                                           ALU.subtract, ALU.mult)
                        return last

                    def rmsnorm(n):
                        for t in range(TT):
                            link(nc.vector.tensor_tensor_reduce(out=squares[:], in0=h_tok[:, t, :], in1=h_tok[:, t, :], scale=1.0,
                                                                scalar=0.0, op0=ALU.mult, op1=ALU.add, accum_out=ssum[:, t:t + 1]))
                        nc.vector.tensor_scalar(var_eps[:], ssum[:], 1.0 / C, RMS_EPS, ALU.mult, ALU.add).then_inc(l1_var_ready, 1)
                        dve.wait_ge(l1_rstd_ready, b * 4 + (n + 1))
                        return nc.vector.tensor_tensor(xn[:], h_tok[:], bc(rstd[:].unsqueeze(2), wide), ALU.mult)

                    def attention(a):
                        for s in range(2):
                            dve.wait_ge(qkv_evac, b * 6 + (3 * a + s + 1))
                            link(nc.vector.tensor_copy(parts[:, s, 0, :], qk[:, s, :]))
                            link(nc.vector.tensor_tensor(rest[:, s, :], qk[:, s, :], parts[:, s, 0, :], ALU.subtract))
                            link(nc.vector.tensor_copy(parts[:, s, 1, :], rest[:, s, :]))
                            nc.vector.tensor_tensor(parts[:, s, 2, :], rest[:, s, :], parts[:, s, 1, :], ALU.subtract).then_inc(parts_ready, 1)

                        def shift(i):
                            q = i % TT
                            n = keys(a, q)
                            first = T - P - q * P
                            add = strips[:, i // TT, q * P + T - 1:(q * P - 1 if q else None):-1] if a == 0 else mask[:, first:first + n]
                            wait_apart(dve, scores_ready, b * (2 * TILES) + (a * TILES + i + 1), passed)
                            nc.vector.tensor_tensor_reduce(out=ps[:, S_BANKS[i % 4], 0:n], in0=ps[:, S_BANKS[i % 4], 0:n], in1=add, scale=-1.0,
                                                           scalar=3.0e38, op0=ALU.add, op1=ALU.min,
                                                           accum_out=nmax[:, i % 4:i % 4 + 1]).then_inc(biased_ready, 1)

                        def move(i):
                            if not evac_by_vector(i):
                                return
                            h, q = i // TT, i % TT
                            n = keys(a, q) // P
                            dve.wait_ge(probs_T, b * (2 * TILES) + (a * TILES + i + 1))
                            if h >= SLOTS:
                                dve.wait_ge(o_ready, b * (2 * G) + (a * G + (h - SLOTS) // 4 + 1))
                            nc.vector.tensor_copy(PT[:, h % SLOTS, 0:n, q * P:(q + 1) * P],
                                                  ps[:, T_BANKS[i % 3], 0:n * P].rearrange("p (k q) -> p k q", k=n)).then_inc(moved_dve, 1)

                        def divide(g):
                            dve.wait_ge(otok_T, b * (2 * G) + (a * G + g + 1))
                            if g:
                                dve.wait_ge(otok_ready, b * (2 * G) + (a * G + g))
                            o = ps[:, 5, :].rearrange("p (t j r) -> p t j r", t=TT, j=4)
                            link(nc.vector.reciprocal(orec[:], o[:, :, :, HD]))
                            nc.vector.tensor_tensor(o_tok[:, :, g * 32:(g + 1) * 32].rearrange("p t (j d) -> p t j d", j=4),
                                                    o[:, :, :, 0:HD], bc(orec[:].unsqueeze(3), [P, TT, 4, HD]),
                                                    ALU.mult).then_inc(otok_ready, 1)

                        dve.wait_ge(stacked, b * (24 * 16) + (a + 1) * 12 * 16)
                        for i in range(TILES):
                            shift(i)
                            if i >= 3:
                                move(i - 3)
                            if i % 16 == 12 and i > 16:
                                divide(i // 16 - 1)
                        for i in range(TILES - 3, TILES):
                            move(i)
                        divide(G - 1)

                    nc.vector.tensor_copy(slot_now[:], slot_all[:, bass.ds(b * TT, TT)]).then_inc(slot_now_ready, 1)
                    dve.wait_ge(gathered, b * (16 * TT) + 16 * TT)
                    link(nc.vector.tensor_tensor(y0[:], y0[:], bc(gate_keep[:, bass.ds(b * TT, TT)].unsqueeze(2), wide), ALU.mult))
                    link(nc.vector.tensor_tensor(y0[:], y0[:], bc(gb0[:, bass.ds(b, 1), :], wide), ALU.mult))
                    link(nc.vector.tensor_tensor(x_b, x_b, y0[:], ALU.add), passed)
                    layernorm(0).then_inc(tok_ready, 1)
                    attention(0)
                    dve.wait_ge(proj_ready, b * 2 + 1)
                    nc.vector.tensor_tensor(gated[:], ps[:, 1:3, :].rearrange("p a (t c) -> p (a t) c", t=2),
                                            bc(b_gate_sb[:].unsqueeze(1), [P, TT, 2 * C]), ALU.add).then_inc(gated_ready, 1)
                    dve.wait_ge(sigmoid_ready, b + 1)
                    link(nc.vector.tensor_tensor(h_tok[:], gated[:, :, 0:C], gated[:, :, C:2 * C], ALU.mult))
                    link(nc.vector.tensor_tensor(h_tok[:], h_tok[:], row(0), ALU.mult))
                    link(nc.vector.tensor_tensor(x_b, x_b, h_tok[:], ALU.add), passed)
                    link(layernorm(1))
                    link(nc.vector.tensor_tensor(h_tok[:], xn[:], row(2), ALU.mult))
                    link(nc.vector.tensor_tensor(h_tok[:], h_tok[:], row(1), ALU.add))
                    rmsnorm(2).then_inc(tok_ready, 1)
                    attention(1)
                    dve.wait_ge(proj_ready, b * 2 + 2)
                    link(nc.vector.tensor_tensor(h_tok[:], h_tok[:], ps[:, 1, :].rearrange("p (t c) -> p t c", t=TT), ALU.add))
                    rmsnorm(3).then_inc(tok_ready, 1)
                    few = [P, TT, E]
                    dve.wait_ge(l1_logits, b + 1)
                    link(nc.vector.tensor_copy(logit[:], ps[:, 1, 0:TT * E].rearrange("p (t e) -> p t e", t=TT)))
                    for n in range(2):
                        link(nc.vector.tensor_reduce(tops[:, n], logit[:], AX.X, ALU.max))
                        link(nc.vector.tensor_tensor(small[:, n], logit[:], bc(tops[:, n].unsqueeze(2), few), ALU.is_equal))
                        link(nc.vector.tensor_tensor(small[:, n], small[:, n], bc(rank[:].unsqueeze(1), few), ALU.mult))
                        link(nc.vector.tensor_reduce(tops[:, 4 + n], small[:, n], AX.X, ALU.max))
                        link(nc.vector.tensor_tensor(small[:, 2 + n], small[:, n], bc(tops[:, 4 + n].unsqueeze(2), few), ALU.is_equal))
                        if n == 0:
                            link(nc.vector.tensor_scalar_mul(small[:, 4], small[:, 2], -3.0e38))
                            link(nc.vector.tensor_tensor(logit[:], logit[:], small[:, 4], ALU.add))
                    nc.vector.tensor_tensor(tops[:, 2], tops[:, 1], tops[:, 0], ALU.subtract).then_inc(gap_ready, 1)
                    dve.wait_ge(gap_exp, b + 1)
                    link(nc.vector.tensor_scalar_add(tops[:, 3], tops[:, 2], 1.0))
                    link(nc.vector.reciprocal(tops[:, 4], tops[:, 3]))
                    link(nc.vector.tensor_tensor(tops[:, 5], tops[:, 4], tops[:, 2], ALU.mult))
                    for n in range(2):
                        link(nc.vector.tensor_tensor(small[:, n], small[:, 2 + n], bc(tops[:, 4 + n].unsqueeze(2), few), ALU.mult))
                    link(nc.vector.tensor_tensor(combine[:], small[:, 0], small[:, 1], ALU.add))
                    for e in range(E):
                        dve.wait_ge(ye_ready, b * E + (e + 1))
                        if e:
                            dve.wait_ge(ye_added, b * E + e)
                        for t in range(TT):
                            last = nc.vector.scalar_tensor_tensor(out=h_tok[:, t, :], in0=ps[:, 6 + e % 2, t * C:(t + 1) * C],
                                                                  scalar=combine[:, t, e:e + 1], in1=h_tok[:, t, :],
                                                                  op0=ALU.mult, op1=ALU.add)
                        last.then_inc(ye_added, 1)
                    dve.wait_ge(ye_added, b * E + E)
                    link(nc.vector.tensor_tensor(h_tok[:], h_tok[:], row(3), ALU.mult))
                    nc.vector.tensor_tensor(x_b, x_b, h_tok[:], ALU.add).then_inc(x_done, 1)
                    chain.done()


_INS = ['L0_attn_x', 'L0_attn_W_attn', 'L0_attn_W_proj', 'L0_ffn_router_w', 'L0_ffn_w1', 'L0_ffn_w2', 'L0_c',
        'L0_wmod', 'L1_attn_w_in', 'L1_attn_w_gate', 'L1_attn_b_gate', 'L1_attn_amplitudes',
        'L1_attn_sharpness', 'L1_attn_offsets', 'L1_ffn_g1', 'L1_ffn_Wq', 'L1_ffn_Wdkv', 'L1_ffn_Wuk',
        'L1_ffn_Wuv', 'L1_ffn_Wo', 'L1_ffn_g2', 'L1_ffn_gate_w', 'L1_ffn_w1', 'L1_ffn_w2', 'L1_c', 'L1_wmod']
_TURNED = ('L0_c', 'L1_c')
_BY_WIDTH = {'L0_attn_W_attn': (0, C), 'L1_attn_w_in': (0, 2 * C), 'L1_ffn_Wq': (0,), 'L1_ffn_Wuk': (0,)}
_OUTS = [((B, T, C), 'float32')]


def _by_width(w, first):
    import numpy as _np
    n = w.shape[0]
    turned = w[:, first:first + C].reshape(n, H, HD).transpose(0, 2, 1).reshape(n, C)
    return _np.concatenate([w[:, :first], turned, w[:, first + C:]], axis=1)


def kernel(**inputs):
    import numpy as _np
    import concourse.bacc as _bacc
    from concourse import mybir as _mybir
    from concourse.bass_utils import run_bass_kernel_spmd as _run

    nc = _bacc.Bacc("TRN2", target_bir_lowering=False, num_devices=1)
    arrays, args = {}, []
    for name in _INS:
        a = _np.asarray(inputs[name])
        if name in _TURNED:
            a = a.T
        for first in _BY_WIDTH.get(name, ()):
            a = _by_width(a, first)
        a = _np.ascontiguousarray(a)
        arrays[f"in_{name}_dram"] = a
        args.append(nc.dram_tensor(f"in_{name}_dram", a.shape, _mybir.dt.from_np(a.dtype), kind="ExternalInput").ap())
    for i, (shape, dtype) in enumerate(_OUTS):
        dt = _mybir.dt.from_np(_np.dtype(dtype))
        args.append(nc.dram_tensor(f"out_{i}_dram", shape, dt, kind="ExternalOutput").ap())
    adaln_kernel(nc, *args)
    r = _run(nc, [arrays], core_ids=[0])
    return r.results[0]["out_0_dram"]
```

```python
import concourse.bass as bass
from concourse import mybir
from contextlib import ExitStack

FP32 = mybir.dt.float32
BF16 = mybir.dt.bfloat16
INT32 = mybir.dt.int32
ALU = mybir.AluOpType
ACT = mybir.ActivationFunctionType
AX = mybir.AxisListType

P = 128
B = 8
T = 512
TT = T // P
C = 128
H = 16
HD = C // H
G = H // 4
NL = 64
SEG = T // NL
PAIRS = H // 2
N_ITER = 6
E = 8
CAP = B * T // E
F0 = 512
F1 = 256
LAT = 64
KG = 21
STRIP = T + (TT - 1) * P
QL = T + NL
STACK = 96
BIG = 1.0e9
LN_EPS = 1e-05
RMS_EPS = 1e-06


class Chain:

    def __init__(self, eng, sem, base=0, links=0, turn=None):
        self.eng, self.sem, self.base, self.links, self.turn, self.n = eng, sem, base, links, turn, 0

    def link(self, ins, passed=None):
        self.n += 1
        ins.then_inc(self.sem, 1)
        if self.turn is None:
            self.eng.wait_ge(self.sem, self.base + self.n)
        elif passed is None:
            self.eng.wait_ge(self.sem, self.turn * self.links + (self.base + self.n))
        else:
            wait_apart(self.eng, self.sem, self.turn * self.links + (self.base + self.n), passed)

    def done(self):
        assert self.n == self.links, ("links", self.n, self.links)


def bc(ap, shape):
    return ap.to_broadcast(shape)


def wait_apart(eng, sem, value, passed):
    eng.wait_ge(sem, value)
    eng.sem_inc(passed, 1)


def adaln_kernel(nc, L0_attn_x, L0_attn_W_attn, L0_attn_W_proj, L0_ffn_router_w, L0_ffn_w1, L0_ffn_w2,
                 L0_c, L0_wmod, L1_attn_w_in, L1_attn_w_gate, L1_attn_b_gate, L1_attn_amplitudes,
                 L1_attn_sharpness, L1_attn_offsets, L1_ffn_g1, L1_ffn_Wq, L1_ffn_Wdkv, L1_ffn_Wuk,
                 L1_ffn_Wuv, L1_ffn_Wo, L1_ffn_g2, L1_ffn_gate_w, L1_ffn_w1, L1_ffn_w2, L1_c, L1_wmod,
                 out):
    bias_dram = nc.dram_tensor("bias_dram", (H, 2 * T), FP32, kind="Internal").ap()
    slots_in = nc.dram_tensor("slots_in", (E * CAP, C), FP32, kind="Internal").ap()
    slots_out = nc.dram_tensor("slots_out", (E * CAP, C), FP32, kind="Internal").ap()

    parts_dram = nc.dram_tensor("parts_dram", (2, 3, C, QL), BF16, kind="Internal").ap()
    parts1_dram = nc.dram_tensor("parts1_dram", (2, 3, C, T), BF16, kind="Internal").ap()

    mods_dram = nc.dram_tensor("mods_dram", (5, B, C), FP32, kind="Internal").ap()

    ctx = ExitStack()
    with ctx:
        def sb(name, shape, dt=FP32, where=ctx):
            return where.enter_context(nc.sbuf_tensor(name, shape, dt))

        def sem(name):
            return ctx.enter_context(nc.semaphore(name))

        ps = ctx.enter_context(nc.psum_tensor("ps", [P, 8, 512], FP32))

        x_sb = sb("x_sb", [P, B * TT, C])
        ident = sb("ident", [P, P])
        half = sb("half", [P, 1])
        mod_col = sb("mod_col", [P, 2, 2, B])
        gate_keep = sb("gate_keep", [P, B * TT])
        slot_all = sb("slot_all", [P, B * TT], INT32)

        with ExitStack() as early:
            mod_row0 = sb("mod_row0", [P, 3, B, C], FP32, early)
            setup_phase(nc, sb, sem, ps, x_sb, ident, half, mod_col, mod_row0, mods_dram, bias_dram,
                        L0_attn_x, L0_c, L0_wmod, L1_c, L1_wmod, L1_attn_amplitudes, L1_attn_sharpness,
                        L1_attn_offsets, slots_in, slots_out)
            nystrom_phase(nc, sb, sem, ps, x_sb, ident, half, mod_col, mod_row0, gate_keep, slot_all,
                          slots_in, parts_dram, L0_attn_W_attn, L0_attn_W_proj, L0_ffn_router_w)
        strips = sb("strips", [P, H, STRIP])
        expert_phase(nc, sb, sem, ps, ident, strips, bias_dram, slots_in, slots_out, L0_ffn_w1, L0_ffn_w2)
        layer1_phase(nc, sb, sem, ps, x_sb, ident, half, mod_col, mods_dram, strips, parts1_dram, gate_keep, slot_all,
                     slots_out, L1_attn_w_in, L1_attn_w_gate, L1_attn_b_gate, L1_ffn_g1, L1_ffn_Wq,
                     L1_ffn_Wdkv, L1_ffn_Wuk, L1_ffn_Wuv, L1_ffn_Wo, L1_ffn_g2, L1_ffn_gate_w,
                     L1_ffn_w1, L1_ffn_w2, out)


SETUP_LINKS = 28


def setup_phase(nc, sb_, sem, ps, x_sb, ident, half, mod_col, mod_row0, mods_dram, bias_dram, x, c0, wmod0,
                c1, wmod1, amplitudes, sharpness, offsets, slots_in, slots_out):
    local = ExitStack()
    with local:
        def sb(name, shape, dt=FP32):
            return sb_(name, shape, dt, local)

        gb0 = sb("gb0", [P, B, C])
        mod_row1 = sb("mod_row1", [P, 4, B, C])
        cT = sb("cT", [P, 2, B])
        silu_c = sb("silu_c", [P, 2, B])
        silu_rep = sb("silu_rep", [P, 2, B, P])
        wmod = sb("wmod", [P, 2, 6 * C])
        amp = sb("amp", [P, H * KG])
        shp = sb("shp", [P, H * KG])
        off = sb("off", [P, H * KG])
        rel_i = sb("rel_i", [P, 8], INT32)
        rel = sb("rel", [P, 8])
        dist = sb("dist", [P, 8, H * KG])
        gauss = sb("gauss", [P, 8, H * KG])
        bias_rel = sb("bias_rel", [P, 8, H])
        bias_hr = sb("bias_hr", [H, 2 * T])
        guard = sb("guard", [P, 2, B * C])
        zeros = sb("zeros", [P, 2048])

        mods_loaded = sem("mods_loaded")
        gauss_loaded = sem("gauss_loaded")
        x_and_scratch = sem("x_and_scratch")
        setup_pool = sem("setup_pool")
        silu_ready = sem("silu_ready")
        silu_rep_ready = sem("silu_rep_ready")
        cols_ready = sem("cols_ready")
        row_ready = sem("row_ready")
        row_evac = sem("row_evac")
        exponent_ready = sem("exponent_ready")
        gauss_ready = sem("gauss_ready")
        bias_ready = sem("bias_ready")
        bias_T_ready = sem("bias_T_ready")
        bias_hr_ready = sem("bias_hr_ready")
        setup_dve = sem("setup_dve")

        with nc.Block() as block:
            @block.sync
            def _(sp):
                for l, (c, w) in enumerate(((c0, wmod0), (c1, wmod1))):
                    sp.dma_start(cT[:, l, :], c).then_inc(mods_loaded, 16)
                    sp.dma_start(wmod[:, l, :], w).then_inc(mods_loaded, 16)
                for dst, src in ((amp, amplitudes), (shp, sharpness), (off, offsets)):
                    row = src.rearrange("(a h) k -> a (h k)", a=1)
                    sp.dma_start(dst[:], row.to_broadcast([P, H * KG])).then_inc(gauss_loaded, 16)
                sp.dma_start(x_sb[:], x.rearrange("b (t p) c -> p (b t) c", p=P)).then_inc(x_and_scratch, 16)
                sp.wait_ge(setup_pool, 1)
                for half_, dst in enumerate((slots_in, slots_out)):
                    for r in range(2):
                        sp.dma_start(dst[r * 2048:(r + 1) * 2048, :].rearrange("(p a) c -> p (a c)", p=P),
                                     zeros[:]).then_inc(x_and_scratch, 16)
                sp.wait_ge(bias_hr_ready, 1)
                sp.dma_start(bias_dram, bias_hr[:]).then_inc(x_and_scratch, 16)
                sp.wait_ge(setup_dve, SETUP_LINKS)
                sp.dma_start(mods_dram[0:1].rearrange("k b c -> k (b c)"), gb0[0:1].rearrange("p b c -> p (b c)")).then_inc(x_and_scratch, 16)
                sp.dma_start(mods_dram[1:5].rearrange("(a k) b c -> a (k b c)", a=1),
                             mod_row1[0:1].rearrange("p k b c -> p (k b c)")).then_inc(x_and_scratch, 16)
                sp.wait_ge(x_and_scratch, 16 * 8)

            @block.gpsimd
            def _(pool):
                link = Chain(pool, setup_pool).link
                nc.gpsimd.memset(half[:], -0.5)
                link(nc.gpsimd.memset(zeros[:], 0.0))
                link(nc.gpsimd.memset(ident[:], 0.0))
                link(nc.gpsimd.iota(rel_i[:], [[-P, 8]], base=T - 1, channel_multiplier=-1))
                link(nc.gpsimd.affine_select(out=ident[:], in_=ident[:], compare_op=ALU.not_equal, fill=1.0, base=0,
                                             pattern=[[-1, P]], channel_multiplier=1))

            @block.scalar
            def _(act):
                act.wait_ge(mods_loaded, 64)
                nc.scalar.activation(silu_c[:], cT[:], ACT.Silu).then_inc(silu_ready, 1)
                act.wait_ge(exponent_ready, 1)
                nc.scalar.activation(gauss[:], dist[:], ACT.Exp).then_inc(gauss_ready, 1)
                for i in range(2 * B):
                    act.wait_ge(row_ready, i + 1)
                    row = ps[:, 1 + i % 2, :].rearrange("p (k c) -> p k c", k=4)
                    if i < B:
                        nc.scalar.copy(mod_row0[:, :, i, :], row[:, 0:3, :])
                        nc.scalar.copy(gb0[:, i, :], row[:, 3, :]).then_inc(row_evac, 1)
                    else:
                        nc.scalar.copy(mod_row1[:, :, i - B, :], row).then_inc(row_evac, 1)
                act.wait_ge(bias_T_ready, 1)
                nc.scalar.copy(bias_hr[:], ps[0:H, 3:5, :].rearrange("h a r -> h (a r)")).then_inc(bias_hr_ready, 1)

            @block.tensor
            def _(pe):
                pe.wait_ge(silu_ready, 1)
                for l in range(2):
                    for k in range(2):
                        last = nc.tensor.matmul(ps[:, 0, (2 * l + k) * B:(2 * l + k + 1) * B],
                                                wmod[:, l, k * C:(k + 1) * C], silu_c[:, l, :], start=True, stop=True)
                last.then_inc(cols_ready, 1)
                pe.wait_ge(silu_rep_ready, 1)
                for i in range(2 * B):
                    if i >= 2:
                        pe.wait_ge(row_evac, i - 1)
                    nc.tensor.matmul(ps[:, 1 + i % 2, :], silu_rep[:, i // B, i % B, :],
                                     wmod[:, i // B, 2 * C:6 * C], start=True, stop=True).then_inc(row_ready, 1)
                pe.wait_ge(bias_ready, 1)
                pe.wait_ge(setup_pool, 4)
                for n in range(8):
                    last = nc.tensor.transpose(ps[0:H, 3 + n // 4, (n % 4) * P:(n % 4 + 1) * P],
                                               bias_rel[:, n, :], ident[:])
                last.then_inc(bias_T_ready, 1)

            @block.vector
            def _(dve):
                chain = Chain(dve, setup_dve)
                link = chain.link
                dve.wait_ge(silu_ready, 1)
                nc.vector.tensor_copy(silu_rep[:], bc(silu_c[:].unsqueeze(3), [P, 2, B, P])).then_inc(silu_rep_ready, 1)
                dve.wait_ge(cols_ready, 1)
                cols = ps[:, 0, 0:4 * B].rearrange("p (l k b) -> p l k b", l=2, k=2)
                nc.vector.tensor_copy(mod_col[:, :, 0, :], cols[:, :, 0, :])
                nc.vector.tensor_scalar_add(mod_col[:, :, 1, :], cols[:, :, 1, :], 1.0)
                dve.wait_ge(gauss_loaded, 48)
                dve.wait_ge(setup_pool, 3)
                link(nc.vector.tensor_copy(rel[:], rel_i[:]))
                link(nc.vector.scalar_tensor_tensor(out=shp[:], in0=shp[:], scalar=-1.0, in1=shp[:], op0=ALU.mult, op1=ALU.min))
                wide = [P, 8, H * KG]
                link(nc.vector.tensor_tensor(dist[:], bc(rel[:].unsqueeze(2), wide), bc(off[:].unsqueeze(1), wide), ALU.subtract))
                link(nc.vector.tensor_tensor(gauss[:], dist[:], bc(shp[:].unsqueeze(1), wide), ALU.mult))
                link(nc.vector.tensor_tensor(dist[:], gauss[:], dist[:], ALU.mult))
                nc.vector.tensor_copy(rel[:], rel_i[:]).then_inc(exponent_ready, 1)
                dve.wait_ge(gauss_ready, 1)
                link(nc.vector.tensor_tensor(dist[:], gauss[:], bc(amp[:].unsqueeze(1), wide), ALU.mult))
                nc.vector.tensor_reduce(bias_rel[:], dist[:].rearrange("p n (h k) -> p n h k", k=KG), AX.X,
                                        ALU.add).then_inc(bias_ready, 1)
                dve.wait_ge(row_evac, 2 * B)
                for cb, gates in ((mod_row0[:, 2], (mod_row0[:, 0], gb0[:])), (mod_row1[:, 2], (mod_row1[:, 0], mod_row1[:, 3]))):
                    link(nc.vector.tensor_scalar_add(cb, cb, 1.0))
                    for g in gates:
                        g = g.rearrange("p b c -> p (b c)")
                        link(nc.vector.tensor_scalar(guard[:, 0], g, 0.0, 2.0, ALU.is_ge, ALU.mult))
                        link(nc.vector.scalar_tensor_tensor(out=guard[:, 1], in0=g, scalar=-1.0, in1=g, op0=ALU.mult, op1=ALU.max))
                        link(nc.vector.tensor_scalar_max(guard[:, 1], guard[:, 1], 0.25))
                        link(nc.vector.tensor_scalar_sub(guard[:, 0], guard[:, 0], 1.0))
                        link(nc.vector.tensor_tensor(g, guard[:, 0], guard[:, 1], ALU.mult))
                assert chain.n == SETUP_LINKS, chain.n


NY_LINKS = 52


def nystrom_phase(nc, sb_, sem, ps, x_sb, ident, half, mod_col, mod_row0, gate_keep, slot_all, slots_in,
                  parts_dram, W_attn, W_proj, router_w):
    local = ExitStack()
    with local:
        def sb(name, shape, dt=FP32):
            return sb_(name, shape, dt, local)

        w_attn = sb("w_attn", [P, 3 * C])
        w_proj = sb("w_proj", [P, C])
        w_router = sb("w_router", [P, E])
        w_gated = sb("w_gated", [P, C])
        ones = sb("ones", [P, P])
        upto = sb("upto", [P, P])
        blocks = sb("blocks", [P, P])
        eye = sb("eye", [P, NL])
        eye7 = sb("eye7", [P, NL])
        eye15 = sb("eye15", [P, NL])
        eye325 = sb("eye325", [P, NL])
        rank_i = sb("rank_i", [P, E], INT32)
        rank = sb("rank", [P, E])
        stats = sb("stats", [P, TT, 6])
        mean_var = sb("mean_var", [P, TT, 2])
        var_eps = sb("var_eps", [P, TT])
        rstd = sb("rstd", [P, TT])
        xn = sb("xn", [P, TT, C])
        hT = sb("hT", [P, T])
        lm = sb("lm", [P, 2, NL])
        qk = sb("qk", [P, 2, QL])
        rest = sb("rest", [P, 2, QL])
        parts = sb("parts", [P, 2, 3, QL], BF16)
        stack = sb("stack", [STACK, 2, H, QL], BF16)
        v_tok = sb("v_tok", [P, TT, C])
        kmax = sb("kmax", [P, PAIRS])
        ksum = sb("ksum", [P, PAIRS])
        krec = sb("krec", [P, PAIRS])
        den = sb("den", [P, PAIRS])
        rden = sb("rden", [P, PAIRS])
        K_sb = sb("K_sb", [P, PAIRS, NL])
        KT = sb("KT", [P, PAIRS, NL])
        AV = sb("AV", [P, 2, PAIRS, 2, NL])
        X = sb("X", [P, PAIRS, NL])
        Q = sb("Q", [P, PAIRS, NL])
        L_tok = sb("L_tok", [P, 2, H * NL])
        lmax = sb("lmax", [P, H])
        LT = sb("LT", [P, PAIRS, T])
        N_lm = sb("N_lm", [P, 2, T])
        NT = sb("NT", [P, 2, TT, P])
        nmax = sb("nmax", [P, PAIRS])
        nsum = sb("nsum", [P, PAIRS])
        nrec = sb("nrec", [P, PAIRS])
        Nv = sb("Nv", [P, PAIRS, HD])
        Z = sb("Z", [P, PAIRS, NL])
        O_sb = sb("O_sb", [P, 2, T])
        orec = sb("orec", [P, TT, 4])
        o_tok = sb("o_tok", [P, TT, C])
        oT = sb("oT", [P, T])
        h2 = sb("h2", [P, TT, C])
        logit = sb("logit", [P, TT, E])
        lgmax = sb("lgmax", [P, TT])
        prob = sb("prob", [P, TT, E])
        psum_ = sb("psum_", [P, TT])
        gate = sb("gate", [P, TT])
        first = sb("first", [P, TT, E])
        top = sb("top", [P, TT])
        onehot = sb("onehot", [P, TT, E])
        before = sb("before", [P, TT + 1, E])
        count = sb("count", [P, TT, E])
        pos1 = sb("pos1", [P, TT])
        keep = sb("keep", [P, TT])
        slot = sb("slot", [P, TT])
        beyond = sb("beyond", [P, TT])
        slot_now = sb("slot_now", [P, TT], INT32)

        ny_loaded = sem("ny_loaded")
        consts_pool = sem("consts_pool")
        pool_order = sem("pool_order")
        eyes_ready = sem("eyes_ready")
        var_ready = sem("var_ready")
        rstd_ready = sem("rstd_ready")
        xn_ready = sem("xn_ready")
        xT_ready = sem("xT_ready")
        hT_ready = sem("hT_ready")
        qkv_ready = sem("qkv_ready")
        qk_evac = sem("qk_evac")
        parts_ready = sem("parts_ready")
        parts_stored = [sem("q_parts_stored"), sem("k_parts_stored")]
        stacked = sem("stacked")
        kscore_ready = sem("kscore_ready")
        kshift_ready = sem("kshift_ready")
        kexp_ready = sem("kexp_ready")
        k_ready = sem("k_ready")
        colsum_ready = sem("colsum_ready")
        kT_ready = sem("kT_ready")
        kT_evac = sem("kT_evac")
        a0_ready = sem("a0_ready")
        a0_evac = sem("a0_evac")
        x_ready = sem("x_ready")
        b_ready = sem("b_ready")
        q_ready = sem("q_ready")
        step_ready = sem("step_ready")
        step_evac = sem("step_evac")
        side_scores = sem("side_scores")
        side_max = sem("side_max")
        side_exp = sem("side_exp")
        side_T = sem("side_T")
        side_evac = sem("side_evac")
        nv_sums = sem("nv_sums")
        nv_ready = sem("nv_ready")
        z_ready = sem("z_ready")
        z_evac = sem("z_evac")
        o_ready = sem("o_ready")
        o_evac = sem("o_evac")
        otok_T = sem("otok_T")
        otok_ready = sem("otok_ready")
        oT_ready = sem("oT_ready")
        oT_evac = sem("oT_evac")
        w_gated_ready = sem("w_gated_ready")
        y_ready = sem("y_ready")
        h2_ready = sem("h2_ready")
        h2T_ready = sem("h2T_ready")
        h2T_evac = sem("h2T_evac")
        logits_ready = sem("logits_ready")
        lshift_ready = sem("lshift_ready")
        prob_ready = sem("prob_ready")
        onehot_ready = sem("onehot_ready")
        count_ready = sem("count_ready")
        slot_ready = sem("slot_ready")
        scattered = sem("scattered")
        h2_free = sem("h2_free")
        ny_dve = sem("ny_dve")
        consts_dve = sem("consts_dve")

        SIDES = TT + PAIRS

        def rows(h):
            return slice(NL * (h % 2), NL * (h % 2) + NL)

        passed = sem("passed")

        with nc.Block() as block:
            @block.sync
            def _(sp):
                for dst, src in ((w_attn, W_attn), (w_proj, W_proj), (w_router, router_w)):
                    sp.dma_start(dst[:], src).then_inc(ny_loaded, 16)
                with sp.Fori(0, B) as b:
                    for s in range(2):
                        sp.wait_ge(parts_ready, b * 2 + (s + 1))
                        sp.dma_start(parts_dram[s].rearrange("n p t -> p n t"), parts[:, s]).then_inc(parts_stored[s], 16)
                    for s in range(2):
                        sp.wait_ge(parts_stored[s], b * 16 + 16)
                        flat = parts_dram[s].rearrange("n (d h) t -> (n d) (h t)", d=HD)
                        for i in range(3):
                            rows_i = stack[3 * HD * i:3 * HD * (i + 1), s].rearrange("r h t -> r (h t)")
                            if s == 0:
                                sp.dma_start(rows_i, flat).then_inc(stacked, 16)
                            else:
                                for j in range(3):
                                    sp.dma_start(stack[HD * (3 * i + j):HD * (3 * i + j + 1), s].rearrange("r h t -> r (h t)"),
                                                 flat[HD * i:HD * (i + 1), :]).then_inc(stacked, 16)

            @block.gpsimd
            def _(pool):
                link = Chain(pool, consts_pool).link
                link(nc.gpsimd.memset(stack[64:STACK, :, :, :], 0.0))
                link(nc.gpsimd.memset(before[:], 0.0))
                link(nc.gpsimd.memset(ones[:], 1.0))
                link(nc.gpsimd.memset(blocks[:], 0.0))
                link(nc.gpsimd.memset(Z[:], 0.0))
                link(nc.gpsimd.iota(rank_i[:], [[-1, E]], base=E, channel_multiplier=0))
                link(nc.gpsimd.affine_select(out=upto[:], in_=ones[:], compare_op=ALU.is_ge, fill=0.0, base=0,
                                             pattern=[[1, P]], channel_multiplier=-1))
                for r in range(2):
                    link(nc.gpsimd.memset(blocks[r * NL:(r + 1) * NL, r * NL:(r + 1) * NL], 1.0))
                    link(nc.gpsimd.memset(Z[r * NL:(r + 1) * NL, :, 32 * r + HD:32 * r + 32], 1.0))
                pool.sem_inc(h2_free, 1)
                with pool.Fori(0, B) as b:
                    for n in range(2):
                        pool.wait_ge(var_ready, b * 2 + (n + 1))
                        nc.gpsimd.tensor_tensor(rstd[:], var_eps[:], bc(half[:], [P, TT]), ALU.pow).then_inc(rstd_ready, 1)
                    wait_apart(pool, slot_ready, b + 1, passed)
                    for t in range(TT):
                        nc.gpsimd.indirect_dma_start(slots_in, bass.IndirectOffsetOnAxis(ap=slot_now[:, t:t + 1], axis=0),
                                                     h2[:, t, :], None, bounds_check=E * CAP - 1,
                                                     oob_is_err=False).then_inc(scattered, 16)
                    pool.wait_ge(scattered, b * (16 * TT) + 16 * TT)
                    pool.sem_inc(h2_free, 1)

            @block.scalar
            def _(act):
                with act.Fori(0, B) as b:
                    act.wait_ge(xT_ready, b + 1)
                    nc.scalar.activation(hT[:], ps[:, 0, :], ACT.Identity, bias=mod_col[:, 0, 0, bass.ds(b, 1)],
                                         scale=mod_col[:, 0, 1, bass.ds(b, 1)]).then_inc(hT_ready, 1)
                    for s in range(2):
                        act.wait_ge(qkv_ready, b * 3 + (s + 1))
                        nc.scalar.copy(qk[:, s, 0:T], ps[:, 1 + s, :]).then_inc(qk_evac, 1)
                    act.wait_ge(qkv_ready, b * 3 + 3)
                    nc.scalar.copy(v_tok[:], ps[:, 3, :].rearrange("p (t c) -> p t c", t=TT)).then_inc(qk_evac, 1)
                    act.wait_ge(kshift_ready, b + 1)
                    nc.scalar.activation(K_sb[:], K_sb[:], ACT.Exp).then_inc(kexp_ready, 1)
                    act.wait_ge(kT_ready, b + 1)
                    nc.scalar.copy(KT[:], ps[:, 6, :].rearrange("p (j m) -> p j m", j=PAIRS)).then_inc(kT_evac, 1)

                    def side_exps(k):
                        act.wait_ge(side_max, b * SIDES + (k + 1))
                        if k < TT:
                            nc.scalar.activation(L_tok[:, k % 2, :], L_tok[:, k % 2, :], ACT.Exp).then_inc(side_exp, 1)
                        else:
                            j = k - TT
                            if k >= TT + 2:
                                act.wait_ge(side_T, b * SIDES + (k - 1))
                            nc.scalar.activation(N_lm[:, k % 2, :], ps[:, 2 + k % 2, :], ACT.Exp,
                                                 bias=nmax[:, j:j + 1], accum_out=nsum[:, j:j + 1]).then_inc(side_exp, 1)

                    def side_evacs(k):
                        act.wait_ge(side_T, b * SIDES + (k + 1))
                        if k < TT:
                            nc.scalar.copy(LT[:, :, k * P:(k + 1) * P],
                                           ps[:, 4:6, :].rearrange("p a (j t) -> p (a j) t", t=P)).then_inc(side_evac, 1)
                        else:
                            if k >= TT + 2:
                                act.wait_ge(nv_sums, b * PAIRS + (k - TT - 1))
                            nc.scalar.copy(NT[:, k % 2],
                                           ps[:, 4 + k % 2, :].rearrange("p (t m) -> p t m", t=TT)).then_inc(side_evac, 1)

                    for n in range(N_ITER):
                        for u in range(2):
                            k = 2 * n + u
                            side_exps(k)
                            if k:
                                side_evacs(k - 1)
                        for f in range(2):
                            act.wait_ge(step_ready, b * (2 * N_ITER) + (2 * n + f + 1))
                            pairs = slice(4 * f, 4 * f + 4)
                            if n < N_ITER - 1:
                                nc.scalar.copy(AV[:, (n + 1) % 2, pairs],
                                               ps[:, f, :].rearrange("p (j a m) -> p j a m", j=4, a=2)).then_inc(step_evac, 1)
                            else:
                                nc.scalar.copy(AV[:, (n + 1) % 2, pairs, 1],
                                               ps[:, f, 0:256].rearrange("p (j m) -> p j m", j=4)).then_inc(step_evac, 1)
                    side_evacs(SIDES - 1)
                    for g in range(G):
                        act.wait_ge(o_ready, b * G + (g + 1))
                        if g >= 2:
                            act.wait_ge(otok_T, b * G + (g - 1))
                        nc.scalar.copy(O_sb[:, g % 2, :], ps[:, 2 + g % 2, :]).then_inc(o_evac, 1)
                    act.wait_ge(oT_ready, b + 1)
                    nc.scalar.copy(oT[:], ps[:, 6, :]).then_inc(oT_evac, 1)
                    act.wait_ge(h2T_ready, b + 1)
                    nc.scalar.copy(hT[:], ps[:, 0, :]).then_inc(h2T_evac, 1)
                    act.wait_ge(lshift_ready, b + 1)
                    nc.scalar.activation(prob[:], logit[:], ACT.Exp).then_inc(prob_ready, 1)

            @block.tensor
            def _(pe):
                pe.wait_ge(ny_loaded, 48)
                pe.wait_ge(consts_pool, 11)
                with pe.Fori(0, B) as b:
                    pe.wait_ge(xn_ready, b + 1)
                    for t in range(TT):
                        last = nc.tensor.transpose(ps[:, 0, t * P:(t + 1) * P], xn[:, t, :], ident[:])
                    last.then_inc(xT_ready, 1)
                    pe.wait_ge(hT_ready, b + 1)
                    for s in range(2):
                        nc.tensor.matmul(ps[:, 1 + s, :], w_attn[:, s * C:(s + 1) * C], hT[:],
                                         start=True, stop=True).then_inc(qkv_ready, 1)
                    for t in range(TT):
                        last = nc.tensor.matmul(ps[:, 3, t * C:(t + 1) * C], hT[:, t * P:(t + 1) * P],
                                                w_attn[:, 2 * C:3 * C], start=True, stop=True)
                    last.then_inc(qkv_ready, 1)

                    def side_A(k):
                        if k == 0:
                            pe.wait_ge(qk_evac, b * 3 + 3)
                        if 1 <= k <= TT:
                            pe.wait_ge(side_max, b * SIDES + k)
                        if k > TT + 1:
                            pe.wait_ge(side_exp, b * SIDES + (k - 1))
                        if k < TT:
                            for h in range(H):
                                last = nc.tensor.matmul(ps[:, 2 + h // 8, (h % 8) * NL:(h % 8 + 1) * NL],
                                                        stack[:, 0, h, k * P:(k + 1) * P], stack[:, 1, h, T:QL],
                                                        start=True, stop=True)
                        else:
                            for h in (2 * (k - TT), 2 * (k - TT) + 1):
                                last = nc.tensor.matmul(ps[rows(h), 2 + k % 2, :], stack[:, 0, h, T:QL],
                                                        stack[:, 1, h, 0:T], start=True, stop=True,
                                                        tile_position=(0, NL * (h % 2)))
                        last.then_inc(side_scores, 1)

                    def side_B(k):
                        pe.wait_ge(side_exp, b * SIDES + (k + 1))
                        if k:
                            pe.wait_ge(side_evac, b * SIDES + k)
                        for m in range(PAIRS if k < TT else TT):
                            if k < TT:
                                last = nc.tensor.transpose(ps[:, 4 + m // 4, (m % 4) * P:(m % 4 + 1) * P],
                                                           L_tok[:, k % 2, m * P:(m + 1) * P], ident[:])
                            else:
                                last = nc.tensor.transpose(ps[:, 4 + k % 2, m * P:(m + 1) * P],
                                                           N_lm[:, k % 2, m * P:(m + 1) * P], ident[:])
                        last.then_inc(side_T, 1)

                    def side_C(k):
                        j = k - TT
                        pe.wait_ge(side_evac, b * SIDES + (k + 1))
                        for t in range(TT):
                            last = nc.tensor.matmul(ps[:, 7, j * 2 * HD:(j + 1) * 2 * HD], NT[:, k % 2, t, :],
                                                    v_tok[:, t, j * 2 * HD:(j + 1) * 2 * HD],
                                                    start=(t == 0), stop=(t == TT - 1))
                        last.then_inc(nv_sums, 1)

                    def each(f, out, lhs, rhs):
                        for h in range(8 * f, 8 * f + 8):
                            last = nc.tensor.matmul(out(h), lhs(h), rhs(h), start=True, stop=True)
                        return last

                    pe.wait_ge(stacked, b * (12 * 16) + 12 * 16)
                    for h in range(H):
                        last = nc.tensor.matmul(ps[rows(h), 4, h // 2 * NL:(h // 2 + 1) * NL], stack[:, 0, h, T:QL],
                                                stack[:, 1, h, T:QL], start=True, stop=True,
                                                tile_position=(0, NL * (h % 2)))
                    last.then_inc(kscore_ready, 1)
                    wait_apart(pe, k_ready, b + 1, passed)
                    nc.tensor.matmul(ps[:, 5, :], blocks[:], K_sb[:].rearrange("p j m -> p (j m)"),
                                     start=True, stop=True).then_inc(colsum_ready, 1)
                    for f in range(2):
                        last = each(f, lambda h: ps[rows(h), 6, h // 2 * NL:(h // 2 + 1) * NL],
                                    lambda h: K_sb[rows(h), h // 2, :], lambda h: ident[rows(h), rows(h)])
                    last.then_inc(kT_ready, 1)
                    wait_apart(pe, kT_evac, b + 1, passed)
                    for f in range(2):
                        each(f, lambda h: ps[rows(h), f, h // 2 % 4 * NL:(h // 2 % 4 + 1) * NL],
                             lambda h: KT[rows(h), h // 2, :], lambda h: KT[rows(h), h // 2, :]).then_inc(a0_ready, 1)
                    for n in range(N_ITER):
                        for s in range(2):
                            for f in range(2):
                                if s == 0:
                                    wait_apart(pe, a0_evac, b * 2 + (f + 1), passed)
                                    if n:
                                        wait_apart(pe, step_evac, b * (2 * N_ITER) + (2 * n + f - 1), passed)
                                wait_apart(pe, x_ready, b * (4 * N_ITER) + (4 * n + 2 * s + f + 1), passed)
                                each(f, lambda h: ps[rows(h), f, h // 2 % 4 * NL:(h // 2 % 4 + 1) * NL],
                                     lambda h: AV[rows(h), n % 2, h // 2, 0, :],
                                     lambda h: X[rows(h), h // 2, :]).then_inc(b_ready, 1)
                            k = 2 * n + s
                            side_A(k)
                            if k:
                                side_B(k - 1)
                            if k - 2 >= TT:
                                side_C(k - 2)
                        for f in range(2):
                            wait_apart(pe, q_ready, b * (2 * N_ITER) + (2 * n + f + 1), passed)
                            w = 2 * NL if n < N_ITER - 1 else NL
                            each(f, lambda h: ps[rows(h), f, h // 2 % 4 * w:(h // 2 % 4 + 1) * w],
                                 lambda h: Q[rows(h), h // 2, :],
                                 lambda h: AV[rows(h), n % 2, h // 2].rearrange("p a m -> p (a m)")[:, 2 * NL - w:]
                                 ).then_inc(step_ready, 1)
                    side_C(SIDES - 2)
                    side_B(SIDES - 1)
                    side_C(SIDES - 1)
                    wait_apart(pe, nv_ready, b + 1, passed)
                    wait_apart(pe, step_evac, b * (2 * N_ITER) + 2 * N_ITER, passed)
                    for f in range(2):
                        last = each(f, lambda h: ps[rows(h), 7, 256 + h // 2 * HD:256 + (h // 2 + 1) * HD],
                                    lambda h: AV[rows(h), N_ITER % 2, h // 2, 1, :], lambda h: Nv[rows(h), h // 2, :])
                    last.then_inc(z_ready, 1)
                    pe.wait_ge(z_evac, b + 1)

                    def tail(g):
                        pe.wait_ge(o_evac, b * G + (g + 1))
                        if g >= 2:
                            pe.wait_ge(otok_ready, b * G + (g - 1))
                        for t in range(TT):
                            last = nc.tensor.transpose(ps[:, 4 + g % 2, t * P:(t + 1) * P],
                                                       O_sb[:, g % 2, t * P:(t + 1) * P], ident[:])
                        last.then_inc(otok_T, 1)

                    for g in range(G):
                        if g >= 2:
                            pe.wait_ge(o_evac, b * G + (g - 1))
                        for m in range(2):
                            last = nc.tensor.matmul(ps[m * NL:(m + 1) * NL, 2 + g % 2, :], Z[:, 2 * g + m, :],
                                                    LT[:, 2 * g + m, :], start=True, stop=True,
                                                    tile_position=(0, NL * m))
                        last.then_inc(o_ready, 1)
                        if g:
                            tail(g - 1)
                    tail(G - 1)
                    pe.wait_ge(otok_ready, b * G + G)
                    for t in range(TT):
                        last = nc.tensor.transpose(ps[:, 6, t * P:(t + 1) * P], o_tok[:, t, :], ident[:])
                    last.then_inc(oT_ready, 1)
                    pe.wait_ge(oT_evac, b + 1)
                    pe.wait_ge(w_gated_ready, b + 1)
                    for t in range(TT):
                        last = nc.tensor.matmul(ps[:, 7, t * C:(t + 1) * C], oT[:, t * P:(t + 1) * P], w_gated[:],
                                                start=True, stop=True)
                    last.then_inc(y_ready, 1)
                    pe.wait_ge(h2_ready, b + 1)
                    for t in range(TT):
                        last = nc.tensor.transpose(ps[:, 0, t * P:(t + 1) * P], h2[:, t, :], ident[:])
                    last.then_inc(h2T_ready, 1)
                    pe.wait_ge(h2T_evac, b + 1)
                    for t in range(TT):
                        last = nc.tensor.matmul(ps[:, 1, t * E:(t + 1) * E], hT[:, t * P:(t + 1) * P], w_router[:],
                                                start=True, stop=True)
                    last.then_inc(logits_ready, 1)
                    pe.wait_ge(onehot_ready, b + 1)
                    for t in range(TT):
                        nc.tensor.matmul(ps[:, 1, (TT + t) * E:(TT + t + 1) * E], upto[:], onehot[:, t, :],
                                         start=True, stop=False)
                        last = nc.tensor.matmul(ps[:, 1, (TT + t) * E:(TT + t + 1) * E], ones[:], before[:, t, :],
                                                start=False, stop=True)
                    last.then_inc(count_ready, 1)

            @block.vector
            def _(dve):
                setup = Chain(dve, consts_dve).link
                dve.wait_ge(consts_pool, 11)
                setup(nc.vector.tensor_copy(rank[:], rank_i[:]))
                setup(nc.vector.tensor_tensor(eye[:], ident[:, 0:NL], ident[:, NL:P], ALU.add))
                for dst, by in ((eye7, 7.0), (eye15, 15.0), (eye325, 3.25)):
                    setup(nc.vector.tensor_scalar_mul(dst[:], eye[:], by))
                dve.wait_ge(ny_loaded, 48)

                with dve.Fori(0, B) as b:
                    chain = Chain(dve, ny_dve, links=NY_LINKS, turn=b)
                    link = chain.link
                    x_b = x_sb[:, bass.ds(b * TT, TT), :]

                    def norm(n):
                        for t in range(TT):
                            last = nc.vector.bn_stats(stats[:, t, :], x_sb[:, bass.ds(b * TT + t, 1), :].rearrange("p a c -> p (a c)"))
                        link(last, passed)
                        for t in range(TT):
                            last = nc.vector.bn_aggr(mean_var[:, t, :], stats[:, t, :])
                        link(last)
                        nc.vector.tensor_scalar_add(var_eps[:], mean_var[:, :, 1], LN_EPS).then_inc(var_ready, 1)
                        dve.wait_ge(rstd_ready, b * 2 + (n + 1))
                        for t in range(TT):
                            last = nc.vector.tensor_scalar(xn[:, t, :], x_sb[:, bass.ds(b * TT + t, 1), :].rearrange("p a c -> p (a c)"),
                                                           mean_var[:, t, 0:1], rstd[:, t:t + 1], ALU.subtract, ALU.mult)
                        return last

                    norm(0).then_inc(xn_ready, 1)
                    nc.vector.tensor_tensor(w_gated[:], w_proj[:], mod_row0[:, 0, bass.ds(b, 1), :].rearrange("p a c -> p (a c)"), ALU.mult).then_inc(w_gated_ready, 1)
                    for s in range(2):
                        dve.wait_ge(qk_evac, b * 3 + (s + 1))
                        link(nc.vector.tensor_reduce(lm[:, s, :], qk[:, s, 0:T].rearrange("p (l n) -> p l n", n=SEG), AX.X, ALU.add))
                        link(nc.vector.tensor_scalar_mul(qk[:, s, T:QL], lm[:, s, :], 1.0 / SEG))
                        link(nc.vector.tensor_copy(parts[:, s, 0, :], qk[:, s, :]))
                        link(nc.vector.tensor_tensor(rest[:, s, :], qk[:, s, :], parts[:, s, 0, :], ALU.subtract))
                        link(nc.vector.tensor_copy(parts[:, s, 1, :], rest[:, s, :]))
                        nc.vector.tensor_tensor(parts[:, s, 2, :], rest[:, s, :], parts[:, s, 1, :], ALU.subtract).then_inc(parts_ready, 1)
                    wide = [P, PAIRS, NL]
                    dve.wait_ge(kscore_ready, b + 1)
                    scores = ps[:, 4, :].rearrange("p (j m) -> p j m", j=PAIRS)
                    link(nc.vector.tensor_reduce(kmax[:], scores, AX.X, ALU.max))
                    nc.vector.tensor_tensor(K_sb[:], scores, bc(kmax[:].unsqueeze(2), wide), ALU.subtract).then_inc(kshift_ready, 1)
                    dve.wait_ge(kexp_ready, b + 1)
                    link(nc.vector.tensor_reduce(ksum[:], K_sb[:], AX.X, ALU.add))
                    link(nc.vector.reciprocal(krec[:], ksum[:]))
                    nc.vector.tensor_tensor(K_sb[:], K_sb[:], bc(krec[:].unsqueeze(2), wide), ALU.mult).then_inc(k_ready, 1)
                    dve.wait_ge(colsum_ready, b + 1)
                    dve.wait_ge(k_ready, b + 1)
                    link(nc.vector.tensor_reduce(den[:], ps[:, 5, :].rearrange("p (j m) -> p j m", j=PAIRS), AX.X, ALU.max))
                    link(nc.vector.reciprocal(rden[:], den[:]))
                    link(nc.vector.tensor_tensor(AV[:, 0, :, 1, :], K_sb[:], bc(rden[:].unsqueeze(2), wide), ALU.mult))
                    for f in range(2):
                        pairs = slice(4 * f, 4 * f + 4)
                        dve.wait_ge(a0_ready, b * 2 + (f + 1))
                        nc.vector.tensor_tensor(AV[:, 0, pairs, 0, :], ps[:, f, 0:256].rearrange("p (j m) -> p j m", j=4),
                                                bc(rden[:, pairs].unsqueeze(2), [P, 4, NL]), ALU.mult).then_inc(a0_evac, 1)

                    def side(k):
                        dve.wait_ge(side_scores, b * SIDES + (k + 1))
                        if k < TT:
                            s = ps[:, 2:4, :].rearrange("p a (h m) -> p (a h) m", m=NL)
                            link(nc.vector.tensor_reduce(lmax[:], s, AX.X, ALU.max))
                            if k >= 2:
                                dve.wait_ge(side_T, b * SIDES + (k - 1))
                            nc.vector.tensor_tensor(L_tok[:, k % 2, :].rearrange("p (h m) -> p h m", m=NL), s,
                                                    bc(lmax[:].unsqueeze(2), [P, H, NL]), ALU.subtract).then_inc(side_max, 1)
                        else:
                            nc.vector.tensor_reduce(nmax[:, k - TT:k - TT + 1], ps[:, 2 + k % 2, :], AX.X, ALU.max,
                                                    negate=True).then_inc(side_max, 1)

                    for n in range(N_ITER):
                        for s in range(2):
                            for f in range(2):
                                pairs = slice(4 * f, 4 * f + 4)
                                if s == 0:
                                    if n == 0:
                                        dve.wait_ge(a0_evac, b * 2 + (f + 1))
                                    else:
                                        dve.wait_ge(step_evac, b * (2 * N_ITER) + (2 * n + f - 1))
                                    a = AV[:, n % 2, pairs, 0, :]
                                    scale, shift = -1.0, eye7
                                else:
                                    dve.wait_ge(b_ready, b * (4 * N_ITER) + (4 * n + f + 1))
                                    a, scale, shift = ps[:, f, 0:256].rearrange("p (j m) -> p j m", j=4), -1.0, eye15
                                nc.vector.scalar_tensor_tensor(out=X[:, pairs, :], in0=a, scalar=scale,
                                                               in1=bc(shift[:].unsqueeze(1), [P, 4, NL]),
                                                               op0=ALU.mult, op1=ALU.add).then_inc(x_ready, 1)
                            side(2 * n + s)
                        for f in range(2):
                            pairs = slice(4 * f, 4 * f + 4)
                            dve.wait_ge(b_ready, b * (4 * N_ITER) + (4 * n + 2 + f + 1))
                            nc.vector.scalar_tensor_tensor(out=Q[:, pairs, :], in0=ps[:, f, 0:256].rearrange("p (j m) -> p j m", j=4),
                                                           scalar=-0.25, in1=bc(eye325[:].unsqueeze(1), [P, 4, NL]),
                                                           op0=ALU.mult, op1=ALU.add).then_inc(q_ready, 1)
                    dve.wait_ge(nv_sums, b * PAIRS + PAIRS)
                    link(nc.vector.reciprocal(nrec[:], nsum[:]))
                    for r in range(2):
                        part = ps[r * NL:(r + 1) * NL, 7, 0:P].rearrange("p (j a d) -> p j a d", a=2, d=HD)[:, :, r, :]
                        last = nc.vector.tensor_tensor(Nv[r * NL:(r + 1) * NL], part,
                                                       bc(nrec[r * NL:(r + 1) * NL].unsqueeze(2), [NL, PAIRS, HD]), ALU.mult)
                    last.then_inc(nv_ready, 1)
                    dve.wait_ge(z_ready, b + 1)
                    for r in range(2):
                        last = nc.vector.tensor_copy(Z[r * NL:(r + 1) * NL, :, 32 * r:32 * r + HD],
                                                     ps[r * NL:(r + 1) * NL, 7, 256:256 + 64].rearrange("p (j d) -> p j d", d=HD))
                    last.then_inc(z_evac, 1)
                    for g in range(G):
                        dve.wait_ge(otok_T, b * G + (g + 1))
                        if g:
                            dve.wait_ge(otok_ready, b * G + g)
                        o = ps[:, 4 + g % 2, :].rearrange("p (t j r) -> p t j r", t=TT, j=4)
                        link(nc.vector.reciprocal(orec[:], o[:, :, :, HD]))
                        nc.vector.tensor_tensor(o_tok[:, :, g * 32:(g + 1) * 32].rearrange("p t (j d) -> p t j d", j=4),
                                                o[:, :, :, 0:HD], bc(orec[:].unsqueeze(3), [P, TT, 4, HD]),
                                                ALU.mult).then_inc(otok_ready, 1)
                    dve.wait_ge(y_ready, b + 1)
                    link(nc.vector.tensor_tensor(x_b, x_b, ps[:, 7, :].rearrange("p (t c) -> p t c", t=TT), ALU.add), passed)
                    link(norm(1))
                    wide = [P, TT, C]
                    dve.wait_ge(h2_free, b + 1)
                    link(nc.vector.tensor_tensor(h2[:], xn[:], bc(mod_row0[:, 2, bass.ds(b, 1), :], wide), ALU.mult))
                    nc.vector.tensor_tensor(h2[:], h2[:], bc(mod_row0[:, 1, bass.ds(b, 1), :], wide), ALU.add).then_inc(h2_ready, 1)
                    wide = [P, TT, E]
                    dve.wait_ge(logits_ready, b + 1)
                    lg = ps[:, 1, 0:TT * E].rearrange("p (t e) -> p t e", t=TT)
                    link(nc.vector.tensor_reduce(lgmax[:], lg, AX.X, ALU.max))
                    nc.vector.tensor_tensor(logit[:], lg, bc(lgmax[:].unsqueeze(2), wide), ALU.subtract).then_inc(lshift_ready, 1)
                    dve.wait_ge(lshift_ready, b + 1)
                    link(nc.vector.tensor_single_scalar(first[:], logit[:], 0.0, ALU.is_equal))
                    link(nc.vector.tensor_tensor(first[:], first[:], bc(rank[:].unsqueeze(1), wide), ALU.mult))
                    link(nc.vector.tensor_reduce(top[:], first[:], AX.X, ALU.max))
                    link(nc.vector.tensor_tensor(onehot[:], first[:], bc(top[:].unsqueeze(2), wide), ALU.is_equal))
                    for t in range(TT):
                        last = nc.vector.tensor_tensor(before[:, t + 1, :], before[:, t, :], onehot[:, t, :], ALU.add)
                        if t < TT - 1:
                            link(last)
                    last.then_inc(onehot_ready, 1)
                    dve.wait_ge(prob_ready, b + 1)
                    link(nc.vector.tensor_reduce(psum_[:], prob[:], AX.X, ALU.add))
                    link(nc.vector.reciprocal(gate[:], psum_[:]))
                    dve.wait_ge(count_ready, b + 1)
                    link(nc.vector.tensor_copy(before[:, 0, :], before[:, TT, :]))
                    link(nc.vector.tensor_tensor(count[:], onehot[:], ps[:, 1, TT * E:2 * TT * E].rearrange("p (t e) -> p t e", t=TT), ALU.mult))
                    link(nc.vector.tensor_reduce(pos1[:], count[:], AX.X, ALU.add))
                    link(nc.vector.tensor_single_scalar(keep[:], pos1[:], float(CAP), ALU.is_le))
                    link(nc.vector.tensor_tensor(gate_keep[:, bass.ds(b * TT, TT)], gate[:], keep[:], ALU.mult))
                    link(nc.vector.tensor_scalar(slot[:], top[:], -float(CAP), float(E * CAP - 1), ALU.mult, ALU.add))
                    link(nc.vector.tensor_tensor(slot[:], slot[:], pos1[:], ALU.add))
                    link(nc.vector.tensor_scalar(beyond[:], keep[:], -2.0 * E * CAP, 2.0 * E * CAP, ALU.mult, ALU.add))
                    link(nc.vector.tensor_tensor(slot[:], slot[:], beyond[:], ALU.add))
                    link(nc.vector.tensor_copy(slot_all[:, bass.ds(b * TT, TT)], slot[:]))
                    nc.vector.tensor_copy(slot_now[:], slot[:]).then_inc(slot_ready, 1)
                    chain.done()


def expert_phase(nc, sb_, sem, ps, ident, strips, bias_dram, slots_in, slots_out, w1, w2):
    local = ExitStack()
    with local:
        def sb(name, shape, dt=FP32):
            return sb_(name, shape, dt, local)

        FT = F0 // P
        CT = CAP // P
        x_e = sb("x_e", [P, 2, CT, C])
        w1_e = sb("w1_e", [P, 2, F0])
        w2_e = sb("w2_e", [P, 2, FT, C])
        xT_e = sb("xT_e", [P, 2, CAP])
        hid = sb("hid", [P, 2, FT, CAP])
        y_e = sb("y_e", [P, 2, CT, C])

        strips_loaded = sem("strips_loaded")
        expert_loaded = [sem("expert_loaded0"), sem("expert_loaded1")]
        expert_stored = [sem("expert_stored0"), sem("expert_stored1")]
        ex_xT_ready = sem("ex_xT_ready")
        ex_xT_evac = sem("ex_xT_evac")
        hidden_ready = sem("hidden_ready")
        hidden_evac = sem("hidden_evac")
        ex_y_ready = sem("ex_y_ready")
        ex_y_evac = sem("ex_y_evac")

        def run(eng, emit):
            with eng.Fori(0, E // 2) as i:
                for u in range(2):
                    emit(i, u)

        with nc.Block() as block:
            @block.sync
            def _(sp):
                def load(i, u):
                    sp.wait_ge(ex_y_ready, i * 2 + 1)
                    e = i * 2 + u
                    sp.dma_start(x_e[:, u], slots_in[bass.ds(e * CAP, CAP), :].rearrange("(t p) c -> p t c", p=P)).then_inc(expert_loaded[u], 16)
                    sp.dma_start(w1_e[:, u], w1[bass.ds(e, 1)].rearrange("a p f -> p (a f)")).then_inc(expert_loaded[u], 16)
                    sp.dma_start(w2_e[:, u], w2[bass.ds(e, 1)].rearrange("a (t p) c -> p (a t) c", p=P)).then_inc(expert_loaded[u], 16)
                run(sp, load)

            @block.gpsimd
            def _(pool):
                for h in range(H):
                    src = bass.AP(bias_dram.tensor, h * 2 * T, [[1, P], [1, STRIP]])
                    pool.dma_start(strips[:, h, :], src).then_inc(strips_loaded, 16)
                pool.wait_ge(strips_loaded, 16 * H)

            @block.scalar
            def _(act):
                def emit(i, u):
                    act.wait_ge(ex_xT_ready, i * 2 + (u + 1))
                    nc.scalar.copy(xT_e[:, u], ps[:, u, :]).then_inc(ex_xT_evac, 1)
                    for f in range(FT):
                        act.wait_ge(hidden_ready, i * (2 * FT) + (u * FT + f + 1))
                        nc.scalar.activation(hid[:, u, f, :], ps[:, 2 + f, :], ACT.Gelu_apprx_tanh).then_inc(hidden_evac, 1)
                    act.wait_ge(ex_y_evac, i * 2 + (u + 2))
                    act.dma_start(slots_out[bass.ds((i * 2 + u) * CAP, CAP), :].rearrange("(t p) c -> p t c", p=P),
                                  y_e[:, u]).then_inc(expert_stored[u], 16)
                for u in range(2):
                    act.sem_inc(expert_stored[u], 16)
                run(act, emit)
                for u in range(2):
                    act.wait_ge(expert_stored[u], 16 * (E // 2) + 16)

            @block.tensor
            def _(pe):
                def emit(i, u):
                    pe.wait_ge(expert_loaded[u], i * 48 + 48)
                    for t in range(CT):
                        last = nc.tensor.transpose(ps[:, u, t * P:(t + 1) * P], x_e[:, u, t, :], ident[:])
                    last.then_inc(ex_xT_ready, 1)
                    pe.wait_ge(ex_xT_evac, i * 2 + (u + 1))
                    for f in range(FT):
                        nc.tensor.matmul(ps[:, 2 + f, :], w1_e[:, u, f * P:(f + 1) * P], xT_e[:, u], start=True,
                                         stop=True).then_inc(hidden_ready, 1)
                    pe.wait_ge(hidden_evac, i * (2 * FT) + (u + 1) * FT)
                    pe.wait_ge(ex_y_evac, i * 2 + 1)
                    for t in range(CT):
                        for f in range(FT):
                            last = nc.tensor.matmul(ps[:, 6 + u, t * C:(t + 1) * C], hid[:, u, f, t * P:(t + 1) * P],
                                                    w2_e[:, u, f, :], start=(f == 0), stop=(f == FT - 1))
                    last.then_inc(ex_y_ready, 1)
                pe.sem_inc(ex_y_ready, 1)
                run(pe, emit)

            @block.vector
            def _(dve):
                def emit(i, u):
                    dve.wait_ge(ex_y_ready, i * 2 + (u + 2))
                    dve.wait_ge(expert_stored[u], i * 16 + 16)
                    nc.vector.tensor_copy(y_e[:, u], ps[:, 6 + u, :].rearrange("p (t c) -> p t c", t=CT)).then_inc(ex_y_evac, 1)
                dve.sem_inc(ex_y_evac, 1)
                run(dve, emit)


PRE_LINKS = 11
ATT_LINKS = G
MID_LINKS = 18
MOE_LINKS = 25
TILES = H * TT
FT1 = F1 // P


def evac_by_vector(i):
    return i % 3 == 2


def at(b, each, n):
    register, past = b
    return past * each + n if register is None else register * each + (past * each + n)


def moved_by(vector, n):
    return sum(evac_by_vector(i) == vector for i in range(n))


SLOTS = 5
SIDE, SIDE2 = 6, 7
DVE_LAG = 2
MOE_FIRST, MOE_EACH, MOE_F, MOE_YE = 14, 6, 1, 5
TANH_LAG, MUL_LAG, ADD_LAG = 1, 3, 2
BY_ACT, BY_DVE = moved_by(False, TILES), moved_by(True, TILES)


def layer1_phase(nc, sb_, sem, ps, x_sb, ident, half, mod_col, mods_dram, strips, parts_dram, gate_keep,
                 slot_all, slots_out, w_in, w_gate, b_gate, g1, Wq, Wdkv, Wuk, Wuv, Wo, g2, gate_w, w1, w2, out):
    local = ExitStack()
    with local:
        def sb(name, shape, dt=FP32):
            return sb_(name, shape, dt, local)

        w_in_sb = sb("w_in_sb", [P, 3 * C])
        w_gate_sb = sb("w_gate_sb", [P, 2 * C])
        b_gate_sb = sb("b_gate_sb", [P, 2 * C])
        g1_col = sb("g1_col", [P, 1])
        g2_col = sb("g2_col", [P, 1])
        Wq_sb = sb("Wq_sb", [P, C])
        Wdkv_sb = sb("Wdkv_sb", [P, LAT])
        Wuk_sb = sb("Wuk_sb", [LAT, C])
        Wuv_sb = sb("Wuv_sb", [LAT, C])
        Wo_sb = sb("Wo_sb", [P, C])
        gate_w_sb = sb("gate_w_sb", [P, E])
        w1_e = sb("l1_w1_e", [P, 2, F1])
        w2_e = sb("l1_w2_e", [P, 2, FT1, C])
        mask = sb("mask", [P, T])
        rank_i = sb("l1_rank_i", [P, E], INT32)
        rank = sb("l1_rank", [P, E])
        slot_now = sb("l1_slot_now", [P, TT], INT32)
        y0 = sb("y0", [P, TT, C])
        stats = sb("l1_stats", [P, TT, 6])
        mean_var = sb("l1_mean_var", [P, TT, 2])
        var_eps = sb("l1_var_eps", [P, TT])
        rstd = sb("l1_rstd", [P, TT])
        gb0_now = sb("gb0_now", [P, C])
        mid_rows = sb("mid_rows", [P, 3, C])
        gb_now = sb("gb_now", [P, C])
        xn = sb("l1_xn", [P, TT, C])
        hT = sb("l1_hT", [P, T])
        stack = sb("l1_stack", [STACK, 2, H, T], BF16)
        v_aug = sb("v_aug", [P, TT, H, 32])
        probs = sb("probs", [P, 3, T])
        nmax = sb("l1_nmax", [P, 4])
        qk = sb("l1_qk", [P, 2, T])
        rest = sb("l1_rest", [P, T])
        parts = sb("l1_parts", [P, 2, 3, T], BF16)
        hid = sb("l1_hid", [P, FT1, T])
        PT = sb("PT", [P, SLOTS, TT, T])
        flat = PT[:].rearrange("p j k q -> p (j k q)")
        gated = flat[:, 0:2 * T].rearrange("p (t c) -> p t c", t=TT)
        mid_hT = flat[:, 2 * T:3 * T]
        latT = flat[0:LAT, 3 * T:4 * T]
        O_sb = sb("l1_O_sb", [P, T])
        orec = sb("l1_orec", [P, TT, 4])
        o_tok = sb("l1_o_tok", [P, TT, C])
        oT = sb("l1_oT", [P, T])
        h_tok = sb("h_tok", [P, TT, C])
        squares = sb("squares", [P, C])
        ssum = sb("ssum", [P, TT])
        logit = sb("l1_logit", [P, TT, E])
        small = sb("small", [P, 6, TT, E])
        tops = sb("tops", [P, 6, TT])
        combine = sb("combine", [P, TT, E])

        l1_loaded = sem("l1_loaded")
        l1_pool = sem("l1_pool")
        l1_consts = sem("l1_consts")
        slot_now_ready = sem("slot_now_ready")
        gathered = sem("gathered")
        l1_var_ready = [sem(f"l1_var_ready{n}") for n in range(4)]
        l1_rstd_ready = [sem(f"l1_rstd_ready{n}") for n in range(4)]
        tok_ready = [sem(f"l1_tok_ready{n}") for n in range(3)]
        tok_T = [sem(f"l1_tok_T{n}") for n in range(3)]
        hT_ready = [sem(f"l1_hT_ready{n}") for n in range(3)]
        rows_loaded = [sem(f"rows_loaded{n}") for n in range(3)]
        lat_ready = sem("lat_ready")
        lat_evac = sem("lat_evac")
        qkv_ready = sem("l1_qkv_ready")
        qkv_evac = sem("l1_qkv_evac")
        parts_ready = sem("l1_parts_ready")
        parts_stored = [sem("l1_q_parts_stored"), sem("l1_k_parts_stored")]
        stacked = [sem(f"l1_stacked{g}") for g in range(G)]
        scores_ready = sem("scores_ready")
        biased_ready = sem("biased_ready")
        probs_ready = sem("probs_ready")
        probs_T = sem("probs_T")
        moved_act = sem("moved_act")
        moved_dve = sem("moved_dve")
        o_ready = sem("l1_o_ready")
        o_evac = sem("l1_o_evac")
        otok_T = sem("l1_otok_T")
        otok_ready = sem("l1_otok_ready")
        oT_ready = sem("l1_oT_ready")
        oT_evac = sem("l1_oT_evac")
        proj_ready = sem("proj_ready")
        gated_ready = sem("gated_ready")
        sigmoid_ready = sem("sigmoid_ready")
        l1_logits = sem("l1_logits")
        logits_read = sem("logits_read")
        gap_ready = sem("gap_ready")
        gap_exp = sem("gap_exp")
        experts_loaded = [sem("l1_expert_loaded0"), sem("l1_expert_loaded1")]
        hid_ready = sem("hid_ready")
        hid_tanh = sem("hid_tanh")
        hid_evac = sem("hid_evac")
        ye_ready = sem("ye_ready")
        ye_added = sem("ye_added")
        x_done = sem("x_done")
        stored = sem("stored")
        pre_dve, att_dve, mid_dve, moe_dve = sem("pre_dve"), sem("att_dve"), sem("mid_dve"), sem("moe_dve")
        passed = sem("l1_passed")

        def keys(a, q):
            return T if a == 0 else (q + 1) * P

        FIRST = (None, 0)

        def passes(emit_pre, emit_attention, emit_mid, emit_moe, eng):
            def nothing(b, i):
                pass
            for i in range(TILES):
                emit_pre(FIRST, i)
            emit_attention(0, FIRST, nothing, None)
            emit_mid(FIRST)
            with eng.Fori(0, B - 1) as r:
                now, then = (r, 0), (r, 1)
                emit_attention(1, now, emit_pre, then)
                emit_attention(0, then, emit_moe, now)
                emit_mid(then)
            final = (None, B - 1)
            emit_attention(1, final, nothing, None)
            for i in range(TILES):
                emit_moe(final, i)

        def before(a, b):
            return a == 1 or b[0] is not None or b[1] > 0

        def hidden_step(e, f):
            return MOE_FIRST + MOE_EACH * e + f * MOE_F

        def ye_step(e):
            return MOE_FIRST + MOE_EACH * e + MOE_YE

        with nc.Block() as block:
            @block.sync
            def _(sp):
                for dst, src in ((w_in_sb, w_in), (w_gate_sb, w_gate), (Wq_sb, Wq), (Wdkv_sb, Wdkv), (Wuk_sb, Wuk),
                                 (Wuv_sb, Wuv), (Wo_sb, Wo), (gate_w_sb, gate_w)):
                    sp.dma_start(dst[:], src).then_inc(l1_loaded, 16)
                sp.dma_start(b_gate_sb[:], b_gate.rearrange("(a c) -> a c", a=1).to_broadcast([P, 2 * C])).then_inc(l1_loaded, 16)
                for dst, src in ((g1_col, g1), (g2_col, g2)):
                    sp.dma_start(dst[:], src.rearrange("(c a) -> c a", a=1)).then_inc(l1_loaded, 16)

                def load_row(n, b, first, dst, used):
                    if used is not None:
                        wait_apart(sp, used, at(b, 1, 0), passed)
                    src = mods_dram[first, bass.ds(at(b, 1, 0), 1), :]
                    sp.dma_start(dst, src.to_broadcast([P, C])).then_inc(rows_loaded[n], 16)

                def stack_up(a, b):
                    for s in range(2):
                        wait_apart(sp, parts_ready, at(b, 4, 2 * a + s + 1), passed)
                        if before(a, b):
                            for g in range(G):
                                wait_apart(sp, stacked[g], at(b, 128, 64 * a), passed)
                        sp.dma_start(parts_dram[s].rearrange("n p t -> p n t"), parts[:, s]).then_inc(parts_stored[s], 16)
                    wait_apart(sp, parts_stored[0], at(b, 32, 16 * a + 16), passed)
                    wait_apart(sp, parts_stored[1], at(b, 32, 16 * a + 16), passed)
                    for g in range(G):
                        if before(a, b):
                            wait_apart(sp, scores_ready, at(b, 2 * TILES, (a - 1) * TILES + (g + 1) * 4 * TT), passed)
                        rows = [[0, 3], [H * T, 3 * HD], [1, 4 * T]]
                        sp.dma_start(stack[0:9 * HD, 0, 4 * g:4 * (g + 1), :].rearrange("r h t -> r (h t)"),
                                     bass.AP(parts_dram.tensor, g * 4 * T, rows)).then_inc(stacked[g], 16)
                        for i in range(3):
                            rows = [[0, 3], [H * T, HD], [1, 4 * T]]
                            sp.dma_start(stack[3 * HD * i:3 * HD * (i + 1), 1, 4 * g:4 * (g + 1), :].rearrange("r h t -> r (h t)"),
                                         bass.AP(parts_dram.tensor, (3 + i) * C * T + g * 4 * T, rows)).then_inc(stacked[g], 16)

                def experts(b):
                    for e in range(E):
                        if e >= 2:
                            wait_apart(sp, ye_ready, at(b, E, e - 1), passed)
                        sp.dma_start(w1_e[:, e % 2], w1[e]).then_inc(experts_loaded[e % 2], 16)
                        sp.dma_start(w2_e[:, e % 2], w2[e].rearrange("(f p) c -> p f c", p=P)).then_inc(experts_loaded[e % 2], 16)
                    wait_apart(sp, x_done, at(b, 1, 1), passed)
                    sp.dma_start(out[bass.ds(at(b, 1, 0), 1)].rearrange("a (t p) c -> p (a t) c", p=P),
                                 x_sb[:, bass.ds(at(b, TT, 0), TT), :]).then_inc(stored, 16)

                def load_rows(b, again):
                    load_row(0, b, 0, gb0_now[:], tok_ready[0] if again else None)
                    for k in range(3):
                        load_row(1, b, 1 + k, mid_rows[:, k], tok_ready[1] if again else None)

                load_rows(FIRST, False)
                load_row(2, FIRST, 4, gb_now[:], None)
                stack_up(0, FIRST)
                stack_up(1, FIRST)
                with sp.Fori(0, B - 1) as r:
                    now, then = (r, 0), (r, 1)
                    load_rows(then, True)
                    stack_up(0, then)
                    experts(now)
                    load_row(2, then, 4, gb_now[:], x_done)
                    stack_up(1, then)
                experts((None, B - 1))
                sp.wait_ge(stored, 16 * B)

            @block.gpsimd
            def _(pool):
                link = Chain(pool, l1_pool).link
                link(nc.gpsimd.memset(stack[64:STACK, :, :, :], 0.0))
                link(nc.gpsimd.memset(v_aug[:], 1.0))
                link(nc.gpsimd.memset(y0[:], 0.0))
                link(nc.gpsimd.memset(mask[:], 0.0))
                link(nc.gpsimd.iota(rank_i[:], [[-1, E]], base=E, channel_multiplier=0))
                link(nc.gpsimd.affine_select(out=mask[:], in_=mask[:], compare_op=ALU.is_ge, fill=-BIG, base=T - P,
                                             pattern=[[-1, T]], channel_multiplier=1))

                def power(n, b):
                    pool.wait_ge(l1_var_ready[n], at(b, 1, 1))
                    nc.gpsimd.tensor_tensor(rstd[:], var_eps[:], bc(half[:], [P, TT]), ALU.pow).then_inc(l1_rstd_ready[n], 1)

                def pre(b):
                    wait_apart(pool, slot_now_ready, at(b, 1, 1), passed)
                    for t in range(TT):
                        nc.gpsimd.indirect_dma_start(y0[:, t, :], None, slots_out,
                                                     bass.IndirectOffsetOnAxis(ap=slot_now[:, t:t + 1], axis=0),
                                                     bounds_check=E * CAP - 1, oob_is_err=False).then_inc(gathered, 16)
                    power(0, b)

                def mid(b):
                    power(1, b)
                    power(2, b)

                pre(FIRST)
                mid(FIRST)
                with pool.Fori(0, B - 1) as r:
                    pre((r, 1))
                    power(3, (r, 0))
                    mid((r, 1))
                power(3, (None, B - 1))

            @block.scalar
            def _(act):
                act.wait_ge(l1_pool, 6)
                act.wait_ge(l1_loaded, 16 * 11)

                def attention(a, b, side, side_b):
                    def exp(i):
                        n = keys(a, i % TT)
                        act.wait_ge(biased_ready, at(b, 2 * TILES, a * TILES + i + 1))
                        if i >= 3 or before(a, b):
                            act.wait_ge(probs_T, at(b, 2 * TILES, a * TILES + max(i - 2, 0)))
                        nc.scalar.activation(probs[:, i % 3, 0:n], ps[:, i % 3, 0:n], ACT.Exp, bias=nmax[:, i % 4:i % 4 + 1],
                                             scale=-1.0).then_inc(probs_ready, 1)

                    def move(i):
                        if evac_by_vector(i):
                            return
                        h, q = i // TT, i % TT
                        n = keys(a, q) // P
                        act.wait_ge(probs_T, at(b, 2 * TILES, a * TILES + i + 1))
                        if h >= SLOTS or before(a, b):
                            act.wait_ge(o_ready, at(b, 2 * G, a * G + max((h - SLOTS) // 4 + 1, 0)))
                        nc.scalar.copy(PT[:, h % SLOTS, 0:n, q * P:(q + 1) * P],
                                       ps[:, 3 + i % 2, 0:n * P].rearrange("p (k q) -> p k q", k=n)).then_inc(moved_act, 1)

                    def o_out(g):
                        act.wait_ge(o_ready, at(b, 2 * G, a * G + g + 1))
                        if g or before(a, b):
                            act.wait_ge(otok_T, at(b, 2 * G, a * G + g))
                        nc.scalar.copy(O_sb[:], ps[:, 5, :]).then_inc(o_evac, 1)

                    for i in range(TILES):
                        exp(i)
                        if i >= 2:
                            move(i - 2)
                        if i % 16 == 7 and i > 7:
                            o_out(i // 16 - 1)
                        side(side_b, i)
                        if a == 0 and i == 2:
                            act.wait_ge(qkv_ready, at(b, 6, 3))
                            nc.scalar.copy(v_aug[:, :, :, 0:HD], ps[:, SIDE, :].rearrange("p (t h d) -> p t h d", t=TT, h=H)).then_inc(qkv_evac, 1)
                    move(TILES - 2)
                    move(TILES - 1)
                    o_out(G - 1)

                def o_turned(a, b):
                    act.wait_ge(oT_ready, at(b, 2, a + 1))
                    if before(a, b):
                        act.wait_ge(proj_ready, at(b, 2, a))
                    nc.scalar.copy(oT[:], ps[:, SIDE, :]).then_inc(oT_evac, 1)

                def out_of(n, bank, a, b, emit):
                    act.wait_ge(qkv_ready, at(b, 6, 3 * a + n))
                    emit(ps[:, bank, :]).then_inc(qkv_evac, 1)

                def scaled_q(src):
                    return nc.scalar.activation(qk[:, 0, :], src, ACT.Copy, scale=float(HD) ** -0.5)

                def plain_k(src):
                    return nc.scalar.copy(qk[:, 1, :], src)

                def pre(b, i):
                    if i == 22:
                        act.wait_ge(tok_T[0], at(b, 1, 1))
                        nc.scalar.activation(hT[:], ps[:, SIDE, :], ACT.Identity, bias=mod_col[:, 1, 0, bass.ds(at(b, 1, 0), 1)],
                                             scale=mod_col[:, 1, 1, bass.ds(at(b, 1, 0), 1)]).then_inc(hT_ready[0], 1)
                    if i == 26:
                        if before(0, b):
                            act.wait_ge(parts_ready, at(b, 4, 0))
                        out_of(1, SIDE, 0, b, scaled_q)
                    if i == 30:
                        out_of(2, SIDE, 0, b, plain_k)

                def mid(b):
                    o_turned(0, b)
                    act.wait_ge(gated_ready, at(b, 1, 1))
                    nc.scalar.activation(gated[:, :, C:2 * C], gated[:, :, C:2 * C], ACT.Tanh, scale=0.5).then_inc(sigmoid_ready, 1)
                    act.wait_ge(tok_T[1], at(b, 1, 1))
                    nc.scalar.activation(mid_hT, ps[:, 0, :], ACT.Copy, scale=g1_col[:]).then_inc(hT_ready[1], 1)
                    act.wait_ge(parts_ready, at(b, 4, 2))
                    out_of(1, 1, 1, b, scaled_q)
                    act.wait_ge(lat_ready, at(b, 1, 1))
                    nc.scalar.copy(latT, ps[0:LAT, 4, :]).then_inc(lat_evac, 1)
                    out_of(2, 2, 1, b, plain_k)
                    out_of(3, 3, 1, b, lambda src: nc.scalar.copy(v_aug[:, :, :, 0:HD], src.rearrange("p (t h d) -> p t h d", t=TT, h=H)))

                def moe(b, i):
                    if i == 4:
                        o_turned(1, b)
                    if i == 12:
                        act.wait_ge(tok_T[2], at(b, 1, 1))
                        nc.scalar.activation(hT[:], ps[:, SIDE, :], ACT.Copy, scale=g2_col[:]).then_inc(hT_ready[2], 1)
                    if i == 18:
                        act.wait_ge(gap_ready, at(b, 1, 1))
                        nc.scalar.activation(tops[:, 2], tops[:, 2], ACT.Exp).then_inc(gap_exp, 1)
                    for e in range(E):
                        for f in range(FT1):
                            if i == hidden_step(e, f) + TANH_LAG:
                                act.wait_ge(hid_ready, at(b, E * FT1, e * FT1 + f + 1))
                                if e or before(0, b):
                                    act.wait_ge(ye_ready, at(b, E, e))
                                nc.scalar.activation(hid[:, f, :], ps[:, SIDE + f, :], ACT.Tanh, scale=0.5).then_inc(hid_tanh, 1)

                passes(pre, attention, mid, moe, act)

            @block.tensor
            def _(pe):
                pe.wait_ge(l1_loaded, 16 * 11)
                pe.wait_ge(l1_pool, 6)

                def turn(n, bank, b):
                    pe.wait_ge(tok_ready[n], at(b, 1, 1))
                    for t in range(TT):
                        last = nc.tensor.transpose(ps[:, bank, t * P:(t + 1) * P], xn[:, t, :], ident[:])
                    last.then_inc(tok_T[n], 1)

                def project_v(src, w):
                    def emit(bank):
                        for t in range(TT):
                            last = nc.tensor.matmul(ps[:, bank, t * C:(t + 1) * C], src[:, t * P:(t + 1) * P], w, start=True, stop=True)
                        last.then_inc(qkv_ready, 1)
                    return emit

                def attention(a, b, side, side_b):
                    def scores(i):
                        h, q = i // TT, i % TT
                        if i >= 3 or before(a, b):
                            pe.wait_ge(probs_ready, at(b, 2 * TILES, a * TILES + max(i - 2, 0)))
                        nc.tensor.matmul(ps[:, i % 3, 0:keys(a, q)], stack[:, 0, h, q * P:(q + 1) * P],
                                         stack[:, 1, h, 0:keys(a, q)], start=True, stop=True).then_inc(scores_ready, 1)

                    def moved(n):
                        if moved_by(False, n) or before(a, b):
                            pe.wait_ge(moved_act, at(b, 2 * BY_ACT, a * BY_ACT + moved_by(False, n)))
                        if moved_by(True, n) or before(a, b):
                            pe.wait_ge(moved_dve, at(b, 2 * BY_DVE, a * BY_DVE + moved_by(True, n)))

                    def transpose(i):
                        pe.wait_ge(probs_ready, at(b, 2 * TILES, a * TILES + i + 1))
                        moved(max(i - 1, 0))
                        for k in range(keys(a, i % TT) // P):
                            last = nc.tensor.transpose(ps[:, 3 + i % 2, k * P:(k + 1) * P],
                                                       probs[:, i % 3, k * P:(k + 1) * P], ident[:])
                        last.then_inc(probs_T, 1)

                    def values(g, k):
                        if k == 0:
                            moved((g + 1) * 4 * TT)
                            if g or before(a, b):
                                pe.wait_ge(otok_ready, at(b, 2 * G, a * G + g))
                            if a == 0:
                                pe.wait_ge(qkv_evac, at(b, 6, 3))
                        q0 = 0 if a == 0 else k * P
                        for j in range(4):
                            last = nc.tensor.matmul(ps[32 * j:32 * (j + 1), 5, q0:T], v_aug[:, k, 4 * g + j, :],
                                                    PT[:, (4 * g + j) % SLOTS, k, q0:T], start=(k == 0), stop=(k == TT - 1),
                                                    tile_position=(0, 32 * j))
                        if k == TT - 1:
                            last.then_inc(o_ready, 1)

                    def tail(g):
                        pe.wait_ge(o_evac, at(b, 2 * G, a * G + g + 1))
                        for t in range(TT):
                            last = nc.tensor.transpose(ps[:, 5, t * P:(t + 1) * P], O_sb[:, t * P:(t + 1) * P], ident[:])
                        last.then_inc(otok_T, 1)

                    for i in range(-2, TILES):
                        if i + 2 < TILES:
                            if (i + 2) % 16 == 0:
                                pe.wait_ge(stacked[(i + 2) // 16], at(b, 128, 64 * (a + 1)))
                            scores(i + 2)
                        if i < 0:
                            continue
                        transpose(i)
                        if i % 16 in (2, 3, 4, 5) and i > 16:
                            values(i // 16 - 1, i % 16 - 2)
                        if i % 16 == 9 and i > 16:
                            tail(i // 16 - 1)
                        if a == 0 and i == 0:
                            project_v(hT, w_in_sb[:, C:2 * C])(SIDE)
                        side(side_b, i)
                    for k in range(TT):
                        values(G - 1, k)
                    tail(G - 1)

                def turn_o(a, b):
                    pe.wait_ge(otok_ready, at(b, 2 * G, a * G + G))
                    for t in range(TT):
                        last = nc.tensor.transpose(ps[:, SIDE, t * P:(t + 1) * P], o_tok[:, t, :], ident[:])
                    last.then_inc(oT_ready, 1)

                def pre(b, i):
                    if i == 20:
                        turn(0, SIDE, b)
                    if i == 24:
                        pe.wait_ge(hT_ready[0], at(b, 1, 1))
                        nc.tensor.matmul(ps[:, SIDE, :], w_in_sb[:, 2 * C:3 * C], hT[:], start=True, stop=True).then_inc(qkv_ready, 1)
                    if i == 28:
                        pe.wait_ge(qkv_evac, at(b, 6, 1))
                        nc.tensor.matmul(ps[:, SIDE, :], w_in_sb[:, 0:C], hT[:], start=True, stop=True).then_inc(qkv_ready, 1)
                    if i == 32:
                        pe.wait_ge(qkv_evac, at(b, 6, 2))

                def mid(b):
                    turn_o(0, b)
                    pe.wait_ge(oT_evac, at(b, 2, 1))
                    for t in range(TT):
                        last = nc.tensor.matmul(ps[:, 1 + t // 2, (t % 2) * 2 * C:(t % 2 + 1) * 2 * C], oT[:, t * P:(t + 1) * P],
                                                w_gate_sb[:], start=True, stop=True)
                    last.then_inc(proj_ready, 1)
                    turn(1, 0, b)
                    pe.wait_ge(hT_ready[1], at(b, 1, 1))
                    nc.tensor.matmul(ps[:, 1, :], Wq_sb[:], mid_hT, start=True, stop=True).then_inc(qkv_ready, 1)
                    nc.tensor.matmul(ps[0:LAT, 4, :], Wdkv_sb[:], mid_hT, start=True, stop=True).then_inc(lat_ready, 1)
                    wait_apart(pe, lat_evac, at(b, 1, 1), passed)
                    nc.tensor.matmul(ps[:, 2, :], Wuk_sb[:], latT, start=True, stop=True).then_inc(qkv_ready, 1)
                    project_v(latT, Wuv_sb[:])(3)
                    pe.wait_ge(qkv_evac, at(b, 6, 6))

                def moe(b, i):
                    if i == 3:
                        if b[0] is not None:
                            pe.wait_ge(qkv_evac, at(b, 6, 9))
                        turn_o(1, b)
                    if i == 5:
                        pe.wait_ge(oT_evac, at(b, 2, 2))
                        for t in range(TT):
                            last = nc.tensor.matmul(ps[:, SIDE, t * C:(t + 1) * C], oT[:, t * P:(t + 1) * P], Wo_sb[:],
                                                    start=True, stop=True)
                        last.then_inc(proj_ready, 1)
                    if i == 11:
                        turn(2, SIDE, b)
                    if i == 14:
                        pe.wait_ge(hT_ready[2], at(b, 1, 1))
                        for t in range(TT):
                            last = nc.tensor.matmul(ps[:, SIDE, t * E:(t + 1) * E], hT[:, t * P:(t + 1) * P], gate_w_sb[:],
                                                    start=True, stop=True)
                        last.then_inc(l1_logits, 1)
                    for e in range(E):
                        for f in range(FT1):
                            if i == hidden_step(e, f):
                                if e == 0 and f == 0:
                                    pe.wait_ge(logits_read, at(b, 1, 1))
                                elif f == 0:
                                    pe.wait_ge(hid_evac, at(b, E * FT1, (e - 1) * FT1 + 1))
                                else:
                                    pe.wait_ge(ye_added, at(b, E, e))
                                if f == 0:
                                    pe.wait_ge(experts_loaded[e % 2], at(b, E // 2 * 32, (e // 2 + 1) * 32))
                                nc.tensor.matmul(ps[:, SIDE + f, :], w1_e[:, e % 2, f * P:(f + 1) * P], hT[:],
                                                 start=True, stop=True).then_inc(hid_ready, 1)
                        if i == ye_step(e):
                            pe.wait_ge(hid_evac, at(b, E * FT1, (e + 1) * FT1))
                            for t in range(TT):
                                for f in range(FT1):
                                    last = nc.tensor.matmul(ps[:, SIDE2, t * C:(t + 1) * C], hid[:, f, t * P:(t + 1) * P],
                                                            w2_e[:, e % 2, f, :], start=(f == 0), stop=(f == FT1 - 1))
                            last.then_inc(ye_ready, 1)

                passes(pre, attention, mid, moe, pe)

            @block.vector
            def _(dve):
                dve.wait_ge(l1_pool, 6)
                dve.wait_ge(l1_loaded, 16 * 11)
                nc.vector.tensor_copy(rank[:], rank_i[:]).then_inc(l1_consts, 1)
                dve.wait_ge(l1_consts, 1)
                wide = [P, TT, C]
                few = [P, TT, E]

                class Links(Chain):
                    def start(self, b):
                        self.turn, self.past, self.n = b, 0, 0

                    def link(self, ins, passed=None):
                        self.n += 1
                        ins.then_inc(self.sem, 1)
                        if passed is None:
                            self.eng.wait_ge(self.sem, at(self.turn, self.links, self.n))
                        else:
                            wait_apart(self.eng, self.sem, at(self.turn, self.links, self.n), passed)

                pre_chain = Links(dve, pre_dve, links=PRE_LINKS)
                mid_chain = Links(dve, mid_dve, links=MID_LINKS)
                moe_chain = Links(dve, moe_dve, links=MOE_LINKS)

                def x_rows(b):
                    return x_sb[:, bass.ds(at(b, TT, 0), TT), :]

                def x_tile(b, t):
                    return x_sb[:, bass.ds(at(b, TT, t), 1), :].rearrange("p a c -> p (a c)")

                def row(src):
                    return bc(src.unsqueeze(1), wide)

                def variance(n, b, link):
                    for t in range(TT):
                        last = nc.vector.bn_stats(stats[:, t, :], x_tile(b, t))
                    link(last, passed)
                    for t in range(TT):
                        last = nc.vector.bn_aggr(mean_var[:, t, :], stats[:, t, :])
                    link(last)
                    nc.vector.tensor_scalar_add(var_eps[:], mean_var[:, :, 1], LN_EPS).then_inc(l1_var_ready[n], 1)

                def normalised(n, b):
                    dve.wait_ge(l1_rstd_ready[n], at(b, 1, 1))
                    for t in range(TT):
                        last = nc.vector.tensor_scalar(xn[:, t, :], x_tile(b, t), mean_var[:, t, 0:1], rstd[:, t:t + 1],
                                                       ALU.subtract, ALU.mult)
                    return last

                def mean_square(n, b, link):
                    for t in range(TT):
                        link(nc.vector.tensor_tensor_reduce(out=squares[:], in0=h_tok[:, t, :], in1=h_tok[:, t, :], scale=1.0,
                                                            scalar=0.0, op0=ALU.mult, op1=ALU.add, accum_out=ssum[:, t:t + 1]), passed)
                    nc.vector.tensor_scalar(var_eps[:], ssum[:], 1.0 / C, RMS_EPS, ALU.mult, ALU.add).then_inc(l1_var_ready[n], 1)

                def over_root(n, b):
                    dve.wait_ge(l1_rstd_ready[n], at(b, 1, 1))
                    return nc.vector.tensor_tensor(xn[:], h_tok[:], bc(rstd[:].unsqueeze(2), wide), ALU.mult)

                def split(s, a, b, link):
                    dve.wait_ge(qkv_evac, at(b, 6, 3 * a + s + 1))
                    if before(a, b):
                        dve.wait_ge(parts_stored[s], at(b, 32, 16 * a))
                    link(nc.vector.tensor_copy(parts[:, s, 0, :], qk[:, s, :]))
                    link(nc.vector.tensor_tensor(rest[:], qk[:, s, :], parts[:, s, 0, :], ALU.subtract))
                    link(nc.vector.tensor_copy(parts[:, s, 1, :], rest[:]))
                    nc.vector.tensor_tensor(parts[:, s, 2, :], rest[:], parts[:, s, 1, :], ALU.subtract).then_inc(parts_ready, 1)

                def attention(a, b, side, side_b):
                    def shift(i):
                        q = i % TT
                        n = keys(a, q)
                        first = T - P - q * P
                        add = strips[:, i // TT, q * P + T - 1:(q * P - 1 if q else None):-1] if a == 0 else mask[:, first:first + n]
                        wait_apart(dve, scores_ready, at(b, 2 * TILES, a * TILES + i + 1), passed)
                        nc.vector.tensor_tensor_reduce(out=ps[:, i % 3, 0:n], in0=ps[:, i % 3, 0:n], in1=add, scale=-1.0,
                                                       scalar=3.0e38, op0=ALU.add, op1=ALU.min,
                                                       accum_out=nmax[:, i % 4:i % 4 + 1]).then_inc(biased_ready, 1)

                    def move(i):
                        if not evac_by_vector(i):
                            return
                        h, q = i // TT, i % TT
                        n = keys(a, q) // P
                        dve.wait_ge(probs_T, at(b, 2 * TILES, a * TILES + i + 1))
                        if h >= SLOTS or before(a, b):
                            dve.wait_ge(o_ready, at(b, 2 * G, a * G + max((h - SLOTS) // 4 + 1, 0)))
                        nc.vector.tensor_copy(PT[:, h % SLOTS, 0:n, q * P:(q + 1) * P],
                                              ps[:, 3 + i % 2, 0:n * P].rearrange("p (k q) -> p k q", k=n)).then_inc(moved_dve, 1)

                    def divide(g):
                        dve.wait_ge(otok_T, at(b, 2 * G, a * G + g + 1))
                        if g or before(a, b):
                            dve.wait_ge(otok_ready, at(b, 2 * G, a * G + g))
                        if before(a, b):
                            dve.wait_ge(oT_ready, at(b, 2, a))
                        o = ps[:, 5, :].rearrange("p (t j r) -> p t j r", t=TT, j=4)
                        nc.vector.reciprocal(orec[:], o[:, :, :, HD]).then_inc(att_dve, 1)
                        dve.wait_ge(att_dve, at(b, 2 * G, a * G + g + 1))
                        nc.vector.tensor_tensor(o_tok[:, :, g * 32:(g + 1) * 32].rearrange("p t (j d) -> p t j d", j=4),
                                                o[:, :, :, 0:HD], bc(orec[:].unsqueeze(3), [P, TT, 4, HD]),
                                                ALU.mult).then_inc(otok_ready, 1)

                    for i in range(TILES):
                        shift(i)
                        if i >= DVE_LAG:
                            move(i - DVE_LAG)
                        if i % 16 == 12 and i > 16:
                            divide(i // 16 - 1)
                        side(side_b, i)
                    for i in range(TILES - DVE_LAG, TILES):
                        move(i)
                    divide(G - 1)

                def pre(b, i):
                    link = pre_chain.link
                    if i == 0:
                        nc.vector.tensor_copy(slot_now[:], slot_all[:, bass.ds(at(b, TT, 0), TT)]).then_inc(slot_now_ready, 1)
                    if i == 12:
                        pre_chain.start(b)
                        dve.wait_ge(gathered, at(b, 16 * TT, 16 * TT))
                        link(nc.vector.tensor_tensor(y0[:], y0[:], bc(gate_keep[:, bass.ds(at(b, TT, 0), TT)].unsqueeze(2), wide), ALU.mult))
                        dve.wait_ge(rows_loaded[0], at(b, 16, 16))
                        link(nc.vector.tensor_tensor(y0[:], y0[:], row(gb0_now[:]), ALU.mult))
                        link(nc.vector.tensor_tensor(x_rows(b), x_rows(b), y0[:], ALU.add), passed)
                    if i == 14:
                        variance(0, b, link)
                    if i == 17:
                        normalised(0, b).then_inc(tok_ready[0], 1)
                    if i == 29:
                        split(0, 0, b, link)
                    if i == 33:
                        split(1, 0, b, link)
                        assert pre_chain.n == PRE_LINKS, pre_chain.n

                def mid(b):
                    link = mid_chain.link
                    mid_chain.start(b)
                    dve.wait_ge(proj_ready, at(b, 2, 1))
                    nc.vector.tensor_tensor(gated[:], ps[:, 1:3, :].rearrange("p a (t c) -> p (a t) c", t=2),
                                            bc(b_gate_sb[:].unsqueeze(1), [P, TT, 2 * C]), ALU.add).then_inc(gated_ready, 1)
                    dve.wait_ge(sigmoid_ready, at(b, 1, 1))
                    link(nc.vector.scalar_tensor_tensor(out=h_tok[:], in0=gated[:, :, C:2 * C], scalar=1.0, in1=gated[:, :, 0:C],
                                                        op0=ALU.add, op1=ALU.mult))
                    dve.wait_ge(rows_loaded[1], at(b, 48, 48))
                    link(nc.vector.scalar_tensor_tensor(out=h_tok[:], in0=h_tok[:], scalar=0.5, in1=row(mid_rows[:, 0]),
                                                        op0=ALU.mult, op1=ALU.mult))
                    link(nc.vector.tensor_tensor(x_rows(b), x_rows(b), h_tok[:], ALU.add), passed)
                    variance(1, b, link)
                    link(normalised(1, b))
                    link(nc.vector.tensor_tensor(h_tok[:], xn[:], row(mid_rows[:, 2]), ALU.mult))
                    link(nc.vector.tensor_tensor(h_tok[:], h_tok[:], row(mid_rows[:, 1]), ALU.add), passed)
                    mean_square(2, b, link)
                    over_root(2, b).then_inc(tok_ready[1], 1)
                    for s in range(2):
                        split(s, 1, b, link)
                    assert mid_chain.n == MID_LINKS, mid_chain.n

                def moe(b, i):
                    link = moe_chain.link
                    if i == 7:
                        moe_chain.start(b)
                        dve.wait_ge(proj_ready, at(b, 2, 2))
                        link(nc.vector.tensor_tensor(h_tok[:], h_tok[:], ps[:, SIDE, :].rearrange("p (t c) -> p t c", t=TT), ALU.add), passed)
                        mean_square(3, b, link)
                    if i == 9:
                        over_root(3, b).then_inc(tok_ready[2], 1)
                    if i == 15:
                        dve.wait_ge(l1_logits, at(b, 1, 1))
                        nc.vector.tensor_copy(logit[:], ps[:, SIDE, 0:TT * E].rearrange("p (t e) -> p t e", t=TT)).then_inc(logits_read, 1)
                        dve.wait_ge(logits_read, at(b, 1, 1))
                    if i in (15, 16):
                        n = i - 15
                        link(nc.vector.tensor_reduce(tops[:, n], logit[:], AX.X, ALU.max))
                        link(nc.vector.tensor_tensor(small[:, n], logit[:], bc(tops[:, n].unsqueeze(2), few), ALU.is_equal))
                        link(nc.vector.tensor_tensor(small[:, n], small[:, n], bc(rank[:].unsqueeze(1), few), ALU.mult))
                        link(nc.vector.tensor_reduce(tops[:, 4 + n], small[:, n], AX.X, ALU.max))
                        link(nc.vector.tensor_tensor(small[:, 2 + n], small[:, n], bc(tops[:, 4 + n].unsqueeze(2), few), ALU.is_equal))
                        if n == 0:
                            link(nc.vector.tensor_scalar_mul(small[:, 4], small[:, 2], -3.0e38))
                            link(nc.vector.tensor_tensor(logit[:], logit[:], small[:, 4], ALU.add))
                        else:
                            nc.vector.tensor_tensor(tops[:, 2], tops[:, 1], tops[:, 0], ALU.subtract).then_inc(gap_ready, 1)
                    if i == 20:
                        dve.wait_ge(gap_exp, at(b, 1, 1))
                        link(nc.vector.tensor_scalar_add(tops[:, 3], tops[:, 2], 1.0))
                        link(nc.vector.reciprocal(tops[:, 4], tops[:, 3]))
                        link(nc.vector.tensor_tensor(tops[:, 5], tops[:, 4], tops[:, 2], ALU.mult))
                        for n in range(2):
                            link(nc.vector.tensor_tensor(small[:, n], small[:, 2 + n], bc(tops[:, 4 + n].unsqueeze(2), few), ALU.mult))
                        link(nc.vector.tensor_tensor(small[:, 5], small[:, 0], small[:, 1], ALU.add))
                        link(nc.vector.tensor_scalar_mul(combine[:], small[:, 5], 0.5))
                    for e in range(E):
                        for f in range(FT1):
                            if i == hidden_step(e, f) + MUL_LAG:
                                dve.wait_ge(hid_tanh, at(b, E * FT1, e * FT1 + f + 1))
                                nc.vector.scalar_tensor_tensor(out=hid[:, f, :], in0=hid[:, f, :], scalar=1.0, in1=ps[:, SIDE + f, :],
                                                               op0=ALU.add, op1=ALU.mult).then_inc(hid_evac, 1)
                        if i == min(ye_step(e) + ADD_LAG, TILES - 1):
                            dve.wait_ge(ye_ready, at(b, E, e + 1))
                            if e:
                                dve.wait_ge(ye_added, at(b, E, e))
                            for t in range(TT):
                                last = nc.vector.scalar_tensor_tensor(out=h_tok[:, t, :], in0=ps[:, SIDE2, t * C:(t + 1) * C],
                                                                      scalar=combine[:, t, e:e + 1], in1=h_tok[:, t, :],
                                                                      op0=ALU.mult, op1=ALU.add)
                            last.then_inc(ye_added, 1)
                    if i == TILES - 1:
                        dve.wait_ge(ye_added, at(b, E, E))
                        dve.wait_ge(rows_loaded[2], at(b, 16, 16))
                        link(nc.vector.tensor_tensor(h_tok[:], h_tok[:], row(gb_now[:]), ALU.mult))
                        nc.vector.tensor_tensor(x_rows(b), x_rows(b), h_tok[:], ALU.add).then_inc(x_done, 1)
                        assert moe_chain.n == MOE_LINKS, moe_chain.n

                passes(pre, attention, mid, moe, dve)


_INS = ['L0_attn_x', 'L0_attn_W_attn', 'L0_attn_W_proj', 'L0_ffn_router_w', 'L0_ffn_w1', 'L0_ffn_w2', 'L0_c',
        'L0_wmod', 'L1_attn_w_in', 'L1_attn_w_gate', 'L1_attn_b_gate', 'L1_attn_amplitudes',
        'L1_attn_sharpness', 'L1_attn_offsets', 'L1_ffn_g1', 'L1_ffn_Wq', 'L1_ffn_Wdkv', 'L1_ffn_Wuk',
        'L1_ffn_Wuv', 'L1_ffn_Wo', 'L1_ffn_g2', 'L1_ffn_gate_w', 'L1_ffn_w1', 'L1_ffn_w2', 'L1_c', 'L1_wmod']
_TURNED = ('L0_c', 'L1_c')
_BY_WIDTH = {'L0_attn_W_attn': (0, C), 'L1_attn_w_in': (0, 2 * C), 'L1_ffn_Wq': (0,), 'L1_ffn_Wuk': (0,)}
_OUTS = [((B, T, C), 'float32')]


def _by_width(w, first):
    import numpy as _np
    n = w.shape[0]
    turned = w[:, first:first + C].reshape(n, H, HD).transpose(0, 2, 1).reshape(n, C)
    return _np.concatenate([w[:, :first], turned, w[:, first + C:]], axis=1)


def kernel(**inputs):
    import numpy as _np
    import concourse.bacc as _bacc
    from concourse import mybir as _mybir
    from concourse.bass_utils import run_bass_kernel_spmd as _run

    nc = _bacc.Bacc("TRN2", target_bir_lowering=False, num_devices=1)
    arrays, args = {}, []
    for name in _INS:
        a = _np.asarray(inputs[name])
        if name in _TURNED:
            a = a.T
        for first in _BY_WIDTH.get(name, ()):
            a = _by_width(a, first)
        a = _np.ascontiguousarray(a)
        arrays[f"in_{name}_dram"] = a
        args.append(nc.dram_tensor(f"in_{name}_dram", a.shape, _mybir.dt.from_np(a.dtype), kind="ExternalInput").ap())
    for i, (shape, dtype) in enumerate(_OUTS):
        dt = _mybir.dt.from_np(_np.dtype(dtype))
        args.append(nc.dram_tensor(f"out_{i}_dram", shape, dt, kind="ExternalOutput").ap())
    adaln_kernel(nc, *args)
    r = _run(nc, [arrays], core_ids=[0])
    return r.results[0]["out_0_dram"]
```
